# Optimizing a Trainium2 kernel written in Bass

```python
import numpy as np
import jax
import jax.numpy as jnp

def _softmax(x, axis=-1):
    return jax.nn.softmax(x, axis=axis)

def _gelu(x):
    return jax.nn.gelu(x, approximate=True)

def _silu(x):
    return jax.nn.silu(x)

def _sigmoid(x):
    return jax.nn.sigmoid(x)

def _layernorm(x, axis=-1, eps=1e-05):
    m = jnp.mean(x, axis=axis, keepdims=True)
    v = jnp.var(x, axis=axis, keepdims=True)
    return (x - m) / jnp.sqrt(v + eps)

def _scatter_add(tgt, idx, src, axis=0):
    return tgt.at[idx].add(src)

def _segment_sum(src, seg, n):
    return jax.ops.segment_sum(src, seg, n)
kernel_name = 'mk_gnn_ffn_d1_gnn_r64_172ed7'

def setup_inputs(seed: int=0):
    np.random.seed(seed)
    _w = jnp.asarray

    def _rec_inputs():
        import jax
        import jax.numpy as jnp
        _gk = jax.random.key(seed)
        x = -0.0001538 + 1 * jax.random.normal(jax.random.fold_in(_gk, 1), (128, 768), jnp.float32)
        src = jax.random.randint(jax.random.fold_in(_gk, 2), (4096,), 0, 128, jnp.int32)
        dst = jax.random.randint(jax.random.fold_in(_gk, 3), (4096,), 0, 128, jnp.int32)
        _o = jnp.argsort(dst, stable=True)
        src = src[_o]
        dst = dst[_o]
        return (x, src, dst)
    x, src, dst = _rec_inputs()

    def _L0_gnn_setup():
        import jax, jax.numpy as jnp
        import numpy as np
        N_NODES = 128
        N_EDGES = 512
        D = 768
        H1 = 8
        NEG_SLOPE = 0.2

        def gat_conv(x, src, dst, W, a_src, a_dst, b, heads, out_ch):
            n = x.shape[0]
            h = (x @ W).reshape(n, heads, out_ch)
            alpha_src = jnp.einsum('nhc,hc->nh', h, a_src)
            alpha_dst = jnp.einsum('nhc,hc->nh', h, a_dst)
            e = jax.nn.leaky_relu(alpha_src[src] + alpha_dst[dst], NEG_SLOPE)
            m = jax.ops.segment_max(e, dst, num_segments=n)
            m = jnp.where(jnp.isfinite(m), m, 0.0)
            p = jnp.exp(e - m[dst])
            denom = jax.ops.segment_sum(p, dst, num_segments=n)
            alpha = p / denom[dst]
            msg = h[src] * alpha[:, :, None]
            out = jax.ops.segment_sum(msg, dst, num_segments=n)
            return out.reshape(n, heads * out_ch) + b
        key = jax.random.key(seed)
        ks = jax.random.split(key, 10)
        s = 0.02
        x = jax.random.normal(ks[0], (N_NODES, D), dtype=jnp.float32)
        edge_index = jax.random.randint(ks[1], (2, N_EDGES), 0, N_NODES, dtype=jnp.int64)
        W1 = jax.random.normal(ks[2], (D, H1 * D), dtype=jnp.float32) * s
        a_src1 = jax.random.normal(ks[3], (H1, D), dtype=jnp.float32) * s
        a_dst1 = jax.random.normal(ks[4], (H1, D), dtype=jnp.float32) * s
        b1 = jnp.zeros((H1 * D,), dtype=jnp.float32)
        W2 = jax.random.normal(ks[5], (H1 * D, D), dtype=jnp.float32) * s
        a_src2 = jax.random.normal(ks[6], (1, D), dtype=jnp.float32) * s
        a_dst2 = jax.random.normal(ks[7], (1, D), dtype=jnp.float32) * s
        b2 = jnp.zeros((D,), dtype=jnp.float32)
        return {'x': x, 'edge_index': edge_index, 'W1': W1, 'a_src1': a_src1, 'a_dst1': a_dst1, 'b1': b1, 'W2': W2, 'a_src2': a_src2, 'a_dst2': a_dst2, 'b2': b2}
    _L0_gnn_all = _L0_gnn_setup()
    _L0_gnn_in = {k: v for k, v in _L0_gnn_all.items() if k in ('W1', 'a_src1', 'a_dst1', 'b1', 'W2', 'a_src2', 'a_dst2', 'b2')}
    del _L0_gnn_all

    def _L0_ffn_setup():
        import jax, jax.numpy as jnp
        import numpy as np
        B, N, D, E = (2, 32, 768, 8)
        H = 4 * D
        TARGET_SPARSITY = 0.6
        K_KEEP = int(N * (1.0 - TARGET_SPARSITY))
        V_MAX, FEAT_CLAMP, ETA = (3.0, 10.0, 1.0)

        def _bk_gii(v):
            dr, di = (v, jnp.full_like(v, -ETA))

            def cf(reverse):
                init = (jnp.full((v.shape[0],), 1e+18, v.dtype), jnp.zeros((v.shape[0],), v.dtype))

                def step(c, d):
                    ar, ai = c
                    drr, dii = d
                    den = ar * ar + ai * ai
                    out = (drr - ar / den, dii + ai / den)
                    return (out, out)
                _, (r, i) = jax.lax.scan(step, init, (dr.T, di.T), reverse=reverse)
                return (r.T, i.T)
            ar, ai = cf(False)
            br, bi = cf(True)
            cr, ci = (ar + br - dr, ai + bi - di)
            den = cr * cr + ci * ci
            return (cr / den, -ci / den)
        key = jax.random.key(seed)
        ks = jax.random.split(key, 8)
        s = 0.02
        return {'x': jax.random.normal(ks[0], (B, N, D), jnp.float32), 'Wg': jax.random.normal(ks[1], (D, E), jnp.float32) * s, 'bg': jnp.zeros((E,), jnp.float32), 'W1': jax.random.normal(ks[2], (E, D, H), jnp.float32) * s, 'b1': jnp.zeros((E, H), jnp.float32), 'W2': jax.random.normal(ks[3], (E, H, D), jnp.float32) * s, 'b2': jnp.zeros((E, D), jnp.float32), 'Wv': jax.random.normal(ks[4], (D,), jnp.float32) * s, 'bv': jnp.zeros((), jnp.float32), 'Wm': jax.random.normal(ks[5], (D,), jnp.float32) * s, 'bm': jnp.zeros((), jnp.float32), 'Wo': jax.random.normal(ks[6], (2, D), jnp.float32) * s, 'bo': jnp.zeros((D,), jnp.float32), 'bk_scale': jnp.ones((), jnp.float32)}
    _L0_ffn_all = _L0_ffn_setup()
    _L0_ffn_in = {k: v for k, v in _L0_ffn_all.items() if k in ('Wg', 'bg', 'W1', 'b1', 'W2', 'b2', 'Wv', 'bv', 'Wm', 'bm', 'Wo', 'bo', 'bk_scale')}
    del _L0_ffn_all
    return {'x': x, 'src': src, 'dst': dst, 'L0_gnn_W1': _L0_gnn_in['W1'], 'L0_gnn_a_src1': _L0_gnn_in['a_src1'], 'L0_gnn_a_dst1': _L0_gnn_in['a_dst1'], 'L0_gnn_b1': _L0_gnn_in['b1'], 'L0_gnn_W2': _L0_gnn_in['W2'], 'L0_gnn_a_src2': _L0_gnn_in['a_src2'], 'L0_gnn_a_dst2': _L0_gnn_in['a_dst2'], 'L0_gnn_b2': _L0_gnn_in['b2'], 'L0_ffn_Wg': _L0_ffn_in['Wg'], 'L0_ffn_bg': _L0_ffn_in['bg'], 'L0_ffn_W1': _L0_ffn_in['W1'], 'L0_ffn_b1': _L0_ffn_in['b1'], 'L0_ffn_W2': _L0_ffn_in['W2'], 'L0_ffn_b2': _L0_ffn_in['b2'], 'L0_ffn_Wv': _L0_ffn_in['Wv'], 'L0_ffn_bv': _L0_ffn_in['bv'], 'L0_ffn_Wm': _L0_ffn_in['Wm'], 'L0_ffn_bm': _L0_ffn_in['bm'], 'L0_ffn_Wo': _L0_ffn_in['Wo'], 'L0_ffn_bo': _L0_ffn_in['bo'], 'L0_ffn_bk_scale': _L0_ffn_in['bk_scale']}

def reference(x, src, dst, L0_gnn_W1, L0_gnn_a_src1, L0_gnn_a_dst1, L0_gnn_b1, L0_gnn_W2, L0_gnn_a_src2, L0_gnn_a_dst2, L0_gnn_b2, L0_ffn_Wg, L0_ffn_bg, L0_ffn_W1, L0_ffn_b1, L0_ffn_W2, L0_ffn_b2, L0_ffn_Wv, L0_ffn_bv, L0_ffn_Wm, L0_ffn_bm, L0_ffn_Wo, L0_ffn_bo, L0_ffn_bk_scale):
    import jax
    import jax.numpy as jnp

    def _L0_gnn_ref(x, edge_index, W1, a_src1, a_dst1, b1, W2, a_src2, a_dst2, b2):
        import jax, jax.numpy as jnp
        import numpy as np
        N_NODES = 128
        N_EDGES = 512
        D = 768
        H1 = 8
        NEG_SLOPE = 0.2

        def gat_conv(x, src, dst, W, a_src, a_dst, b, heads, out_ch):
            n = x.shape[0]
            h = (x @ W).reshape(n, heads, out_ch)
            alpha_src = jnp.einsum('nhc,hc->nh', h, a_src)
            alpha_dst = jnp.einsum('nhc,hc->nh', h, a_dst)
            e = jax.nn.leaky_relu(alpha_src[src] + alpha_dst[dst], NEG_SLOPE)
            m = jax.ops.segment_max(e, dst, num_segments=n)
            m = jnp.where(jnp.isfinite(m), m, 0.0)
            p = jnp.exp(e - m[dst])
            denom = jax.ops.segment_sum(p, dst, num_segments=n)
            alpha = p / denom[dst]
            msg = h[src] * alpha[:, :, None]
            out = jax.ops.segment_sum(msg, dst, num_segments=n)
            return out.reshape(n, heads * out_ch) + b
        n = x.shape[0]
        loops = jnp.arange(n, dtype=edge_index.dtype)
        src = jnp.concatenate([edge_index[0], loops])
        dst = jnp.concatenate([edge_index[1], loops])
        h = gat_conv(x, src, dst, W1, a_src1, a_dst1, b1, H1, D)
        h = jax.nn.elu(h)
        out = gat_conv(h, src, dst, W2, a_src2, a_dst2, b2, 1, D)
        return out

    def _L0_ffn_ref(x, Wg, bg, W1, b1, W2, b2, Wv, bv, Wm, bm, Wo, bo, bk_scale):
        import jax, jax.numpy as jnp
        import numpy as np
        B, N, D, E = (2, 32, 768, 8)
        H = 4 * D
        TARGET_SPARSITY = 0.6
        K_KEEP = int(N * (1.0 - TARGET_SPARSITY))
        V_MAX, FEAT_CLAMP, ETA = (3.0, 10.0, 1.0)

        def _bk_gii(v):
            dr, di = (v, jnp.full_like(v, -ETA))

            def cf(reverse):
                init = (jnp.full((v.shape[0],), 1e+18, v.dtype), jnp.zeros((v.shape[0],), v.dtype))

                def step(c, d):
                    ar, ai = c
                    drr, dii = d
                    den = ar * ar + ai * ai
                    out = (drr - ar / den, dii + ai / den)
                    return (out, out)
                _, (r, i) = jax.lax.scan(step, init, (dr.T, di.T), reverse=reverse)
                return (r.T, i.T)
            ar, ai = cf(False)
            br, bi = cf(True)
            cr, ci = (ar + br - dr, ai + bi - di)
            den = cr * cr + ci * ci
            return (cr / den, -ci / den)
        probs = jax.nn.softmax(x @ Wg + bg, axis=-1)
        top_p = jnp.max(probs, axis=-1)
        comb = jax.nn.one_hot(jnp.argmax(probs, -1), E, dtype=x.dtype) * top_p[..., None]
        h = jax.nn.gelu(jnp.einsum('bnd,edh->ebnh', x, W1) + b1[:, None, None, :])
        y = jnp.einsum('ebnh,ehd->ebnd', h, W2) + b2[:, None, None, :]
        ffn_out = jnp.einsum('ebnd,bne->bnd', y, comb)
        v = jnp.clip(ffn_out @ Wv + bv, -V_MAX, V_MAX)
        scores = jax.nn.sigmoid(x @ Wm + bm)
        thr = jax.lax.top_k(scores, K_KEEP)[0][:, -1]
        mask = (scores >= thr[:, None]).astype(x.dtype)
        gr, gi = _bk_gii(v)
        feats = jnp.clip(jnp.stack([gr, gi], -1) * mask[..., None], -FEAT_CLAMP, FEAT_CLAMP)
        return ffn_out + bk_scale * (feats @ Wo + bo)
    edge_index = jnp.stack([src, dst])
    x = x + _L0_gnn_ref(_layernorm(x, axis=-1), edge_index, L0_gnn_W1, L0_gnn_a_src1, L0_gnn_a_dst1, L0_gnn_b1, L0_gnn_W2, L0_gnn_a_src2, L0_gnn_a_dst2, L0_gnn_b2)
    x = x + _L0_ffn_ref(_layernorm(x, axis=-1)[None], L0_ffn_Wg, L0_ffn_bg, L0_ffn_W1, L0_ffn_b1, L0_ffn_W2, L0_ffn_b2, L0_ffn_Wv, L0_ffn_bv, L0_ffn_Wm, L0_ffn_bm, L0_ffn_Wo, L0_ffn_bo, L0_ffn_bk_scale)[0]
    return x

_drawn_inputs = setup_inputs


def setup_inputs(seed=0):
    import zlib

    import numpy as np

    out = dict(_drawn_inputs(seed))
    spreads = {'L0_gnn_b1': (0.0, 0.1),
     'L0_gnn_b2': (0.0, 0.1),
     'L0_ffn_bg': (0.0, 0.1),
     'L0_ffn_b1': (0.0, 0.493),
     'L0_ffn_b2': (0.0, 0.329),
     'L0_ffn_bo': (0.0, 0.1)}
    factors = {'L0_gnn_a_src1': 2.726,
     'L0_gnn_a_dst1': 8.0,
     'L0_gnn_a_src2': 8.0,
     'L0_gnn_a_dst2': 177.81,
     'L0_ffn_Wv': 200.0,
     'L0_ffn_Wm': 23.796,
     'L0_ffn_Wo': 23.543}
    for name, (base, spread) in spreads.items():
        noise = np.random.default_rng([zlib.crc32(name.encode()), seed]).standard_normal(out[name].shape)
        drawn = base * np.exp(spread * noise) if base else spread * noise
        out[name] = jnp.asarray(drawn.astype(out[name].dtype))
    for name, factor in factors.items():
        out[name] = (out[name] * factor).astype(out[name].dtype)
    return out
```

```python
import concourse.bass as bass
from concourse import mybir
from contextlib import ExitStack

P = 128
N = 128
D = 768
HEADS = 8
EDGES = 4096
EXPERTS = 8
HID = 3072
KT = D // P
HB = D // 2
QU = HID // D
CAP = 64
ROUNDS = EXPERTS
SLOTS = 8
GRAINS = 4
KEEP = 12
EPS = 1e-5
VMAX = 3.0
FCLAMP = 10.0
NEG = -1e30
FAR = 1e18
GROUP = 4
GNN_HALVES = 2 * 2 * HEADS
ROUND_HALVES = 2 * 2 * QU
UNITS = [("up", 0), ("up", 1), ("down", 0), ("up", 2), ("down", 1), ("up", 3), ("down", 2), ("down", 3)]


def gnn_moe_kernel(nc, x, src, dst, gw1, gas1, gad1, gb1, gw2, gas2, gad2, gb2,
                   wg, bg, w1, b1, w2, b2, wv, bv, wm, bm, wo, bo, bks, out):
    f32, f32r, bf16, i32 = mybir.dt.float32, mybir.dt.float32r, mybir.dt.bfloat16, mybir.dt.int32
    ALU, ACT = mybir.AluOpType, mybir.ActivationFunctionType
    AX = mybir.AxisListType.X
    V, S, G, T = nc.vector, nc.scalar, nc.gpsimd, nc.tensor

    ctx = ExitStack()
    with ctx:
        ctx.enter_context(nc.allow_non_contiguous_dma(reason="the gate's columns, 768 words each"))

        def sem(name):
            return ctx.enter_context(nc.semaphore(name))

        base = (nc.sbuf_base + 31) // 32 * 32
        ctx.enter_context(nc.sbuf_tensor("slab", [P, (nc.sbuf_usable_end - base - 64) // 4], f32))
        top = [base]

        def size(shape, dt):
            n = 2 if dt == bf16 else 4
            for s in shape[1:]:
                n *= s
            return (n + 31) // 32 * 32

        def place(name, shape, dt=f32):
            t = nc.alloc_sbuf_tensor_at(name, shape, dt, offset=top[0])
            top[0] += size(shape, dt)
            return t

        def region(tenants):
            first, end, got = top[0], top[0], []
            for tensors in tenants:
                top[0] = first
                got += [place(*t) for t in tensors]
                end = max(end, top[0])
            top[0] = end
            return got

        raw = place("raw", [P, SLOTS, 3, D])
        h_sb, whi, wlo = region([
            [("h_sb", [P, HEADS, D])],
            [("whi", [P, GRAINS, 3, HB], f32r), ("wlo", [P, GRAINS, 3, HB], f32r)]])
        (src_hot, dst_hot, eluT, gathered, upper, biased, active, hidden,
         y_sb, ffn, place_now, place_T) = region([
             [("src_hot", [P, 8, P], bf16), ("dst_hot", [P, 8, P], bf16)],
             [("eluT", [P, HEADS * KT, P])],
             [("gathered", [P, KT, P], f32r), ("upper", [P, 2, D]), ("biased", [P, KT, CAP]),
              ("active", [P, KT, CAP]), ("hidden", [P, 2, KT, P], f32r), ("y_sb", [P, D]),
              ("ffn", [P, D]), ("place_now", [P, P]), ("place_T", [P, P])]])
        rows, cf_d, cf_u, cf_t, v_row, alt, alt_i, g_rows = region([
            [("rows", [1, 2, D])],
            [("cf_d", [1, N, 4]), ("cf_u", [1, N + 1, 4]), ("cf_t", [1, 16]), ("v_row", [1, P]),
             ("alt", [1, 2, P]), ("alt_i", [1, P], i32), ("g_rows", [1, 6, P])]])
        att_rows, wo_rows, wv_rows = region([
            [("att_rows", [P, 2, 2, D])],
            [("wo_rows", [P, 2, D]), ("wv_rows", [P, D])]])
        att2_rows = place("att2_rows", [P, 2, D])
        bias_rows = place("bias_rows", [P, 2, D])
        x_sb = place("x_sb", [P, D])
        x1 = place("x1", [P, D])
        xc = place("xc", [P, D])
        xn = place("xn", [P, D])
        xT = place("xT", [P, KT, P])
        att_e = place("att_e", [P, GROUP, P])
        att_p = place("att_p", [P, GROUP, P])
        att_T = place("att_T", [P, GROUP, P])
        elu_y, elu_e, h2_sb = region([
            [("elu_y", [P, 2, 3, P]), ("elu_e", [P, 2, 3, P])],
            [("h2_sb", [P, D])]])
        counts = place("counts", [P, P])
        mask_bias = place("mask_bias", [P, P])
        free_i = place("free_i", [P, P], i32)
        part_i = place("part_i", [P, 1], i32)
        free_f = place("free_f", [P, P])
        part_f = place("part_f", [P, 1])
        ident = place("ident", [P, P])
        ident_b = place("ident_b", [P, P], bf16)
        later = place("later", [P, P])
        slot_no = place("slot_no", [P, 2, CAP])
        fold = place("fold", [P, CAP])
        ones = place("ones", [P, P])
        edges_i = place("edges_i", [P, 2, EDGES // P], i32)
        edges_f = place("edges_f", [P, 2, EDGES // P])
        gb1_rows = place("gb1_rows", [HEADS * KT, P])
        gb1_T = place("gb1_T", [P, HEADS * KT])
        b1_rows = place("b1_rows", [96, 2, P])
        b1_T = place("b1_T", [P, EXPERTS + 1, QU * KT])
        b1_over = place("b1_over", [P, EXPERTS, QU * KT])
        b2_sb = place("b2_sb", [EXPERTS, D])
        gate_w = place("gate_w", [P, KT, EXPERTS + 1])
        gate_b = place("gate_b", [P, EXPERTS + 1])
        bv_c = place("bv_c", [P, 1])
        bk_c = place("bk_c", [P, 1])
        half_pow = place("half_pow", [P, 1])
        alpha = place("alpha", [P, 2, HEADS])
        alpha2 = place("alpha2", [P, 2, 1])
        small = place("small", [P, 64])
        e8 = place("e8", [P, EXPERTS])
        logit = place("logit", [P, EXPERTS + 1])
        prob = place("prob", [P, EXPERTS])
        hot = place("hot", [P, EXPERTS])
        hot_T = place("hot_T", [EXPERTS, P])
        best8 = place("best8", [P, EXPERTS])
        rank = place("rank", [P, EXPERTS + 2])
        over = place("over", [P, EXPERTS])
        route_f = place("route_f", [P, 2])
        route = place("route", [P, 2], i32)
        score_row = place("score_row", [1, 2, P])
        top16 = place("top16", [1, 16])
        keep = place("keep", [P, 1])
        feats = place("feats", [P, 2])
        assert top[0] <= nc.sbuf_usable_end, (top[0], nc.sbuf_usable_end)

        ps = ctx.enter_context(nc.psum_tensor("ps", [P, 8, 512], f32))

        def col(i, n=1):
            return small[:, i:i + n]

        SUM, MEAN, VAR, RSTD, MX, SS, RS = 0, 1, 2, 3, 4, 12, 20
        TOPP, NEGZ, SCORE, THR, VCOL, SMAX, IDX = 28, 29, 30, 31, 32, 33, 34

        raw_in = [sem(f"raw_in{i}") for i in range(SLOTS)]
        used = sem("used")
        x_in, edges_in, small_in = sem("x_in"), sem("edges_in"), sem("small_in")
        row_in = sem("row_in")
        spread = sem("spread")
        iota_done, pool_ones = sem("iota_done"), sem("pool_ones")
        dve_step = sem("dve_step")
        consts = sem("consts")
        var_ready, rstd_ready = sem("var_ready"), sem("rstd_ready")
        xn_ready, xT_done, xT_ready = sem("xn_ready"), sem("xT_done"), sem("xT_ready")
        hot_ready, hot_used = sem("hot_ready"), sem("hot_used")
        bias_done, bias_ready = sem("bias_done"), sem("bias_ready")
        h_ready = sem("h_ready")
        alpha_used = sem("alpha_used")
        att_scores, att_shift, att_exp = sem("att_scores"), sem("att_shift"), sem("att_exp")
        att_prob, att_turned, att_ready = sem("att_prob"), sem("att_turned"), sem("att_ready")
        agg_done, elu_in, elu_exp, elu_ready = sem("agg_done"), sem("elu_in"), sem("elu_exp"), sem("elu_ready")
        h2_ready, out2_done = sem("h2_ready"), sem("out2_done")
        logit_done, gate_in, gate_exp = sem("logit_done"), sem("gate_in"), sem("gate_exp")
        onehot_ready, rank_done, hot_T_ready = sem("onehot_ready"), sem("rank_done"), sem("hot_T_ready")
        route_ready, score_exp = sem("route_ready"), sem("score_exp")
        score_ready, score_turned, thr_ready, thr_done = (sem("score_ready"), sem("score_turned"),
                                                          sem("thr_ready"), sem("thr_done"))
        hi_ready, lo_ready, lo_pool = sem("hi_ready"), sem("lo_ready"), sem("lo_pool")
        upper_ready = sem("upper_ready")
        turned, biased_ready, gelu_done, hidden_ready = (sem("turned"), sem("biased_ready"),
                                                         sem("gelu_done"), sem("hidden_ready"))
        y_ready, scattered, ffn_added = sem("y_ready"), sem("scattered"), sem("ffn_added")
        place_ready, place_turned, place_T_ready = (sem("place_ready"), sem("place_turned"),
                                                    sem("place_T_ready"))
        gather_done, gathered_ready = sem("gather_done"), sem("gathered_ready")
        v_ready, v_turned, g_ready, g_turned = sem("v_ready"), sem("v_turned"), sem("g_ready"), sem("g_turned")
        cf_step = sem("cf_step")
        final_ready, out_done = sem("final_ready"), sem("out_done")

        def used_in(r, pos):
            return GRAINS * (2 * HEADS + 2 * QU * r + pos)

        def blocks(t):
            return t.rearrange("p (b c) -> p b c", b=2)

        block = ctx.enter_context(nc.Block())

        @block.sync
        def _(sp):
            def gnn_half(n):
                unit, half = n // 2, n % 2
                if unit < HEADS:
                    rows_ = gw1[half * 3 * P:(half + 1) * 3 * P, unit * D:(unit + 1) * D]
                else:
                    at = (unit - HEADS) * D + half * 3 * P
                    rows_ = gw2[at:at + 3 * P, :]
                return rows_.rearrange("(k p) c -> p k c", p=P)

            for n in range(GNN_HALVES):
                if n >= SLOTS:
                    sp.wait_ge(used, 2 * (n - SLOTS + 1))
                sp.dma_start(raw[:, n % SLOTS, :, :], gnn_half(n)).then_inc(raw_in[n % SLOTS], 16)

            def load_round(r, e):
                for i in range(ROUND_HALVES):
                    kind, q = UNITS[i // 2]
                    half = i % 2
                    if kind == "up":
                        view = w1[e, half * 3 * P:(half + 1) * 3 * P, q * D:(q + 1) * D]
                    else:
                        view = w2[e, q * D + half * 3 * P:q * D + (half + 1) * 3 * P, :]
                    sp.wait_ge(used, 2 * (GNN_HALVES + ROUND_HALVES * r + i - SLOTS + 1))
                    sp.dma_start(raw[:, i % SLOTS, :, :],
                                 view.rearrange("(k p) c -> p k c", p=P)).then_inc(raw_in[i % SLOTS], 16)

            with sp.Fori(0, ROUNDS) as r:
                load_round(r, r)
            sp.wait_ge(route_ready, 1)
            rounds = sp.value_load(route[0:1, 0:1], min_val=ROUNDS, max_val=ROUNDS + 1)
            expert = sp.value_load(route[0:1, 1:2], min_val=0, max_val=EXPERTS - 1)
            with sp.If(rounds > ROUNDS):
                load_round(ROUNDS, expert)
            sp.end_ifs()
            sp.wait_ge(final_ready, 1)
            sp.dma_start(out, xc[:, :]).then_inc(out_done, 16)
            sp.wait_ge(out_done, 16)

        @block.gpsimd
        def _(pool):
            pairs = [(gas1[h:h + 1, :], gad1[h:h + 1, :]) for h in range(HEADS)]
            pairs += [(gas2, gad2), (gb2, bo), (wo[0:1, :], wo[1:2, :]), (wv, wv)]
            targets = [att2_rows, bias_rows, wo_rows, wv_rows]

            def fetch(i):
                for j in range(2):
                    pool.dma_start(rows[0:1, j, :], pairs[i][j]).then_inc(row_in, 16)

            G.iota(free_i[:, :], pattern=[[1, P]], base=0, channel_multiplier=0).then_inc(iota_done, 1)
            G.iota(part_i[:, :], pattern=[[0, 1]], base=0, channel_multiplier=1).then_inc(iota_done, 1)
            G.memset(half_pow[:, :], -0.5).then_inc(pool_ones, 1)
            fetch(0)
            pool.wait_ge(var_ready, 1)
            pool.wait_ge(pool_ones, 1)
            G.tensor_tensor(col(RSTD), col(VAR), half_pow[:, :], ALU.pow).then_inc(rstd_ready, 1)
            for i in range(len(pairs)):
                pool.wait_ge(row_in, 32 * (i + 1))
                if 2 <= i < HEADS:
                    pool.wait_ge(alpha_used, i - 1)
                if i < HEADS:
                    target = att_rows[:, i % 2, :, :]
                    n = 2
                else:
                    target = targets[i - HEADS]
                    if target is wo_rows:
                        pool.wait_ge(alpha_used, HEADS)
                    n = 1 if i == len(pairs) - 1 else 2
                    target = target[:, :].unsqueeze(1) if n == 1 else target[:, :, :]
                G.partition_broadcast(target.rearrange("p a c -> p (a c)"),
                                      rows[0:1, 0:n, :].rearrange("p a c -> p (a c)")).then_inc(spread, 1)
                if i + 1 < len(pairs):
                    pool.wait_ge(spread, i + 1)
                    fetch(i + 1)
            pool.wait_ge(var_ready, 2)
            G.tensor_tensor(col(RSTD), col(VAR), half_pow[:, :], ALU.pow).then_inc(rstd_ready, 1)

            def round_(r):
                for pos in range(2 * QU):
                    slot = (2 * pos + 1) % SLOTS
                    pool.wait_ge(hi_ready, GRAINS * (2 * QU * r + pos) + 4)
                    G.tensor_tensor(wlo[:, 3, :, :], raw[:, slot, :, HB:D], whi[:, 3, :, :].bitcast(f32),
                                    ALU.subtract).then_inc(lo_pool, 1)

            pool.wait_ge(route_ready, 1)
            rounds = pool.value_load(route[0:1, 0:1], min_val=ROUNDS, max_val=ROUNDS + 1)
            with pool.Fori(0, rounds) as r:
                round_(r)

        @block.scalar
        def _(act):
            act.dma_start(x_sb[:, :], x).then_inc(x_in, 16)
            act.dma_start(edges_i[:, 0, :], src.rearrange("(p j) -> p j", p=P)).then_inc(edges_in, 16)
            act.dma_start(edges_i[:, 1, :], dst.rearrange("(p j) -> p j", p=P)).then_inc(edges_in, 16)
            for target, view in (
                    (gb1_rows[:, :], gb1.rearrange("(j p) -> j p", p=P)),
                    (b1_rows[:, 0, :], b1[0:4, :].rearrange("e (j p) -> (e j) p", p=P)),
                    (b1_rows[:, 1, :], b1[4:8, :].rearrange("e (j p) -> (e j) p", p=P)),
                    (b2_sb[:, :], b2),
                    (gate_w[:, :, 0:EXPERTS], wg.rearrange("(k p) e -> p k e", p=P)),
                    (gate_w[:, :, EXPERTS:EXPERTS + 1], wm.rearrange("(k p) e -> p k e", p=P)),
                    (gate_b[:, 0:EXPERTS], bg.to_broadcast([P, EXPERTS])),
                    (gate_b[:, EXPERTS:EXPERTS + 1], bm.to_broadcast([P, 1])),
                    (bv_c[:, :], bv.to_broadcast([P, 1])),
                    (bk_c[:, :], bks.to_broadcast([P, 1]))):
                act.dma_start(target, view).then_inc(small_in, 16)

            act.wait_ge(bias_done, 1)
            S.copy(gb1_T[:, :], ps[:, 7, 128:128 + HEADS * KT])
            S.copy(b1_T[:, 0:EXPERTS, :].rearrange("p (g e) j -> p g (e j)", g=2),
                   ps[:, 7, 192:384].rearrange("p (g j) -> p g j", g=2)).then_inc(bias_ready, 1)

            def take_head(h):
                act.wait_ge(used, GRAINS * (h + 1))
                b = 2 * (h % 2)
                S.copy(blocks(h_sb[:, h, :]), ps[:, b:b + 2, 0:HB]).then_inc(h_ready, 1)

            def exponents(a, n):
                act.wait_ge(att_shift, a + 1)
                S.activation(att_p[:, 0:n, :], att_e[:, 0:n, :], ACT.Exp).then_inc(att_exp, 1)

            def elu_exponent(k):
                act.wait_ge(elu_in, k + 1)
                S.activation(elu_e[:, k % 2, :, :], elu_e[:, k % 2, :, :], ACT.Exp).then_inc(elu_exp, 1)

            for h in range(5):
                take_head(h)
            exponents(0, GROUP)
            take_head(5)
            take_head(6)
            for k in range(4):
                elu_exponent(k)
            take_head(7)
            for k in range(4, 8):
                elu_exponent(k)
            exponents(1, GROUP)
            for k in range(8, 16):
                elu_exponent(k)

            act.wait_ge(used, GRAINS * 2 * HEADS)
            S.copy(blocks(h2_sb[:, :]), ps[:, 0:2, 0:HB]).then_inc(h2_ready, 1)
            exponents(2, 1)
            act.wait_ge(gate_in, 1)
            S.activation(prob[:, :], prob[:, :], ACT.Exp)
            S.activation(col(SCORE), logit[:, EXPERTS:EXPERTS + 1], ACT.Exp, scale=-1.0).then_inc(gate_exp, 1)
            act.wait_ge(rank_done, 1)
            act.wait_ge(place_ready, 1)
            S.copy(hot_T[:, :], ps[0:EXPERTS, 7, 128:256]).then_inc(hot_T_ready, 1)

            def round_(r):
                def split_high(pos, grains):
                    for j in grains:
                        half, b = j // 2, j % 2
                        slot = (2 * pos + half) % SLOTS
                        if b == 0:
                            act.wait_ge(raw_in[slot], 16 * (GNN_HALVES // SLOTS + 2 * r + (2 * pos + half) // SLOTS + 1))
                        act.wait_ge(used, used_in(r, pos - 1) + j + 1)
                        S.copy(whi[:, j, :, :], raw[:, slot, :, b * HB:(b + 1) * HB]).then_inc(hi_ready, 1)

                def take_upper(q):
                    act.wait_ge(used, used_in(r, UNITS.index(("up", q)) + 1))
                    b = 2 * (q % 2)
                    S.copy(blocks(upper[:, q % 2, :]), ps[:, b:b + 2, 0:HB]).then_inc(upper_ready, 1)

                def gelu(q):
                    act.wait_ge(biased_ready, QU * r + q + 1)
                    S.activation(active[:, :, :], biased[:, :, :], ACT.Gelu_apprx_tanh).then_inc(gelu_done, 1)

                for pos, (kind, q) in enumerate(UNITS):
                    if kind == "up":
                        split_high(pos, range(GRAINS))
                        if q == 0:
                            act.wait_ge(place_turned, r + 1)
                            S.copy(place_T[:, :], ps[:, 5, HB:512]).then_inc(place_T_ready, 1)
                        if 1 <= q:
                            take_upper(q - 1)
                    else:
                        split_high(pos, range(2))
                        gelu(q)
                        split_high(pos, range(2, GRAINS))
                        if q == QU - 2:
                            take_upper(QU - 1)
                act.wait_ge(used, used_in(r, 2 * QU))
                S.copy(blocks(y_sb[:, :]), ps[:, 6:8, 0:HB]).then_inc(y_ready, 1)

            act.wait_ge(route_ready, 1)
            rounds = act.value_load(route[0:1, 0:1], min_val=ROUNDS, max_val=ROUNDS + 1)
            with act.Fori(0, rounds) as r:
                round_(r)

        @block.vector
        def _(dve):
            steps = [0]

            def step(ins):
                steps[0] += 1
                ins.then_inc(dve_step, 1)
                dve.wait_ge(dve_step, steps[0])

            dve.wait_ge(iota_done, 2)
            V.tensor_copy(free_f[:, :], free_i[:, :])
            V.memset(ones[:, :], 1.0)
            V.memset(rank[:, EXPERTS + 1:EXPERTS + 2], -1.0)
            step(V.tensor_copy(part_f[:, :], part_i[:, :]))
            V.tensor_scalar(later[:, :], free_f[:, :], part_f[:, :], None, ALU.is_gt)
            V.tensor_scalar(ident_b[:, :], free_f[:, :], part_f[:, :], None, ALU.is_equal)
            V.tensor_scalar(e8[:, :], free_f[:, 0:EXPERTS], -float(EXPERTS), None, ALU.add)
            V.tensor_copy(slot_no[:, 0, :], free_f[:, 0:CAP])
            V.tensor_copy(slot_no[:, 1, :], free_f[:, 0:CAP])
            step(V.tensor_scalar(ident[:, :], free_f[:, :], part_f[:, :], None, ALU.is_equal))
            V.tensor_tensor(fold[:, :], ident[:, 0:CAP], ident[:, CAP:2 * CAP], ALU.add).then_inc(consts, 1)

            def normalise(source, i):
                step(V.tensor_scalar(col(MEAN), col(SUM), 1.0 / D, None, ALU.mult))
                step(V.tensor_scalar(xc[:, :], source[:, :], col(MEAN), None, ALU.subtract))
                step(V.tensor_tensor_reduce(out=xn[:, :], in0=xc[:, :], in1=xc[:, :], scale=1.0, scalar=0.0,
                                            op0=ALU.mult, op1=ALU.add, accum_out=col(SS)))
                V.tensor_scalar(col(VAR), col(SS), 1.0 / D, EPS, ALU.mult, ALU.add).then_inc(var_ready, 1)
                dve.wait_ge(rstd_ready, i)
                V.tensor_scalar(xn[:, :], xc[:, :], col(RSTD), None, ALU.mult).then_inc(xn_ready, 1)

            def take_xT(i):
                dve.wait_ge(xT_done, i)
                V.tensor_copy(xT[:, :, :].rearrange("p (b k) t -> p b (k t)", b=2),
                              ps[:, 5:7, 0:HB]).then_inc(xT_ready, 1)

            dve.wait_ge(x_in, 16)
            step(V.reduce_sum(col(SUM), x_sb[:, :], AX))
            normalise(x_sb, 1)
            take_xT(1)

            dve.wait_ge(edges_in, 32)
            step(V.tensor_copy(edges_f[:, :, :], edges_i[:, :, :]))
            for c in range(4):
                if c:
                    dve.wait_ge(hot_used, c)
                for j, target in ((0, src_hot), (1, dst_hot)):
                    last = V.tensor_tensor(target[:, :, :], free_f[:, :].unsqueeze(1).to_broadcast([P, 8, P]),
                                           edges_f[:, j, 8 * c:8 * c + 8].unsqueeze(2).to_broadcast([P, 8, P]),
                                           ALU.is_equal)
                last.then_inc(hot_ready, 1)
            dve.wait_ge(hot_used, 4)
            V.tensor_copy(counts[:, :], ps[:, 7, 0:P])
            V.tensor_scalar(mask_bias[:, :], ps[:, 7, 0:P], 0.0, NEG, ALU.is_equal, ALU.mult)

            def head_alpha(h):
                dve.wait_ge(h_ready, h + 1)
                dve.wait_ge(spread, h + 1)
                for j in range(2):
                    dot = V.tensor_tensor_reduce(out=xc[:, :], in0=h_sb[:, h, :], in1=att_rows[:, h % 2, j, :],
                                                 scale=1.0, scalar=0.0, op0=ALU.mult, op1=ALU.add,
                                                 accum_out=alpha[:, j, h:h + 1])
                    if j == 0:
                        step(dot)
                dot.then_inc(alpha_used, 1)
                dve.wait_ge(alpha_used, h + 1)

            def attention(a, n, dst_alpha, turned_at):
                R = ps[:, 4, 0:n * P].rearrange("p (h s) -> p h s", h=n)
                shape = [P, n, P]
                e, p = att_e[:, 0:n, :], att_p[:, 0:n, :]
                dve.wait_ge(att_scores, a + 1)
                step(V.tensor_tensor(p, R, dst_alpha.unsqueeze(2).to_broadcast(shape), ALU.add))
                step(V.scalar_tensor_tensor(out=e, in0=p, scalar=0.2, in1=p, op0=ALU.mult, op1=ALU.max))
                step(V.tensor_tensor(e, e, mask_bias[:, :].unsqueeze(1).to_broadcast(shape), ALU.add))
                step(V.reduce_max(col(MX, n), e, AX))
                V.tensor_tensor(e, e, col(MX, n).unsqueeze(2).to_broadcast(shape), ALU.subtract).then_inc(att_shift, 1)
                dve.wait_ge(att_exp, a + 1)
                step(V.tensor_tensor(p, p, counts[:, :].unsqueeze(1).to_broadcast(shape), ALU.mult))
                step(V.reduce_sum(col(SS, n), p, AX))
                step(V.reciprocal(col(RS, n), col(SS, n)))
                V.tensor_tensor(p, p, col(RS, n).unsqueeze(2).to_broadcast(shape), ALU.mult).then_inc(att_prob, 1)
                dve.wait_ge(att_turned, a + 1)
                V.tensor_copy(att_T[:, 0:n, :].rearrange("p h s -> p (h s)"), turned_at).then_inc(att_ready, 1)

            def elu(k):
                shape = [P, 3, P]
                y, e = elu_y[:, k % 2, :, :], elu_e[:, k % 2, :, :]
                dve.wait_ge(agg_done, k + 1)
                if k >= 2:
                    dve.wait_ge(elu_ready, k - 1)
                step(V.tensor_tensor(y, ps[:, 5 + k % 2, 0:HB].rearrange("p (j t) -> p j t", j=3),
                                     gb1_T[:, 3 * k:3 * k + 3].unsqueeze(2).to_broadcast(shape), ALU.add))
                V.tensor_scalar(e, y, 0.0, None, ALU.min).then_inc(elu_in, 1)
                step(V.tensor_scalar(y, y, 0.0, None, ALU.max))
                if k % 8:
                    elu_out(k - 1)

            def elu_out(k):
                dve.wait_ge(elu_exp, k + 1)
                V.scalar_tensor_tensor(out=eluT[:, 3 * k:3 * k + 3, :], in0=elu_e[:, k % 2, :, :], scalar=-1.0,
                                       in1=elu_y[:, k % 2, :, :], op0=ALU.add, op1=ALU.add).then_inc(elu_ready, 1)

            for h in range(4):
                head_alpha(h)
            head_alpha(4)
            attention(0, GROUP, alpha[:, 1, 0:GROUP], ps[:, 4, 0:512])
            head_alpha(5)
            head_alpha(6)
            dve.wait_ge(bias_ready, 1)
            for k in range(4):
                elu(k)
            head_alpha(7)
            for k in range(4, 8):
                elu(k)
            elu_out(7)
            dve.wait_ge(spread, HEADS + 2)
            V.tensor_tensor(x1[:, :], x_sb[:, :], bias_rows[:, 0, :], ALU.add)
            attention(1, GROUP, alpha[:, 1, GROUP:2 * GROUP], ps[:, 4, 0:512])
            for k in range(8, 16):
                elu(k)
            elu_out(15)

            dve.wait_ge(h2_ready, 1)
            dve.wait_ge(spread, HEADS + 1)
            for j in range(2):
                dot = V.tensor_tensor_reduce(out=xc[:, :], in0=h2_sb[:, :],
                                             in1=att2_rows[:, j, :], scale=1.0, scalar=0.0,
                                             op0=ALU.mult, op1=ALU.add, accum_out=alpha2[:, j, :])
                if j == 0:
                    step(dot)
            dot.then_inc(alpha_used, 1)
            dve.wait_ge(alpha_used, HEADS + 1)
            attention(2, 1, alpha2[:, 1, :], ps[:, 4, P:2 * P])
            dve.wait_ge(out2_done, 1)
            step(V.scalar_tensor_tensor(out=blocks(x1[:, :]), in0=ps[:, 2:4, 0:HB], scalar=1.0,
                                        in1=blocks(x1[:, :]), op0=ALU.mult, op1=ALU.add, accum_out=col(SUM)))
            normalise(x1, 2)
            take_xT(2)

            dve.wait_ge(logit_done, 1)
            step(V.tensor_tensor(logit[:, :], ps[:, 7, 0:EXPERTS + 1], gate_b[:, :], ALU.add))
            step(V.reduce_max(col(SMAX), logit[:, 0:EXPERTS], AX))
            V.tensor_scalar(prob[:, :], logit[:, 0:EXPERTS], col(SMAX), None, ALU.subtract).then_inc(gate_in, 1)
            dve.wait_ge(gate_exp, 1)
            step(V.reduce_sum(col(SS), prob[:, :], AX))
            step(V.reciprocal(col(RS), col(SS)))
            step(V.tensor_scalar(prob[:, :], prob[:, :], col(RS), None, ALU.mult))
            step(V.reduce_max(col(TOPP), prob[:, :], AX))
            step(V.scalar_tensor_tensor(out=best8[:, :], in0=prob[:, :], scalar=col(TOPP), in1=e8[:, :],
                                        op0=ALU.is_equal, op1=ALU.mult))
            step(V.tensor_reduce(col(IDX), best8[:, :], AX, ALU.min))
            V.tensor_scalar(hot[:, :], e8[:, :], col(IDX), None, ALU.is_equal).then_inc(onehot_ready, 1)

            dve.wait_ge(rank_done, 1)
            V.tensor_scalar(over[:, :], ps[:, 7, 24:32], float(CAP), None, ALU.is_gt)
            step(V.scalar_tensor_tensor(out=best8[:, :], in0=ps[:, 7, 16:24], scalar=1.0, in1=hot[:, :],
                                        op0=ALU.add, op1=ALU.mult))
            step(V.tensor_scalar(rank[:, 0:EXPERTS], best8[:, :], -1.0, None, ALU.add))
            V.tensor_scalar(place_now[:, :], slot_no[:, :, :].rearrange("p a j -> p (a j)"), rank[:, 0:1],
                            None, ALU.is_equal).then_inc(place_ready, 1)
            V.reduce_sum(route_f[:, 0:1], over[:, :], AX)
            step(V.tensor_tensor_reduce(out=best8[:, :], in0=over[:, :], in1=free_f[:, 0:EXPERTS], scale=1.0,
                                        scalar=0.0, op0=ALU.mult, op1=ALU.add, accum_out=route_f[:, 1:2]))
            step(V.tensor_scalar(route_f[:, 0:1], route_f[:, 0:1], float(ROUNDS), None, ALU.add))
            V.tensor_copy(route[:, :], route_f[:, :]).then_inc(route_ready, 1)
            step(V.tensor_tensor_reduce(out=best8[:, :], in0=over[:, :], in1=rank[:, 0:EXPERTS], scale=1.0,
                                        scalar=0.0, op0=ALU.mult, op1=ALU.add, accum_out=rank[:, 8:9]))
            step(V.tensor_scalar(rank[:, 8:9], rank[:, 8:9], -float(CAP), None, ALU.add))
            V.memset(ffn[:, :], 0.0).then_inc(ffn_added, 1)

            def take_gathered(r_done, bank):
                dve.wait_ge(gather_done, r_done)
                view = ps[:, bank, 0:HB].rearrange("p (k j) -> p k j", k=KT)
                V.tensor_copy(gathered[:, :, 0:CAP], view).then_inc(gathered_ready, 1)
                dve.wait_ge(gathered_ready, 2 * r_done - 1)
                V.tensor_tensor(gathered[:, :, CAP:P], view, gathered[:, :, 0:CAP].bitcast(f32),
                                ALU.subtract).then_inc(gathered_ready, 1)

            take_gathered(1, 6)

            step(V.tensor_tensor(b1_over[:, :, :], b1_T[:, 0:EXPERTS, :],
                                 over[:, :].unsqueeze(2).to_broadcast([P, EXPERTS, QU * KT]), ALU.mult))
            step(V.reduce_sum(b1_T[:, EXPERTS, :], b1_over[:, :, :].rearrange("p e j -> p j e"), AX))

            step(V.tensor_scalar(col(SCORE), col(SCORE), 1.0, None, ALU.add))
            V.reciprocal(col(SCORE), col(SCORE)).then_inc(score_ready, 1)
            dve.wait_ge(score_turned, 1)
            step(V.tensor_copy(score_row[:, 0, :], ps[0:1, 7, 256:384]))
            step(V.max(top16[:, 0:8], score_row[:, 0, :]))
            step(V.match_replace(out=score_row[:, 1, :], in_to_replace=top16[:, 0:8],
                                 in_values=score_row[:, 0, :], imm_value=-1.0))
            V.max(top16[:, 8:16], score_row[:, 1, :]).then_inc(thr_ready, 1)
            dve.wait_ge(thr_done, 1)
            V.tensor_scalar(keep[:, :], col(SCORE), ps[:, 7, 32:33], None, ALU.is_ge)
            dve.wait_ge(small_in, 16 * 10)
            V.scalar_tensor_tensor(out=x1[:, :], in0=bias_rows[:, 1, :], scalar=bk_c[:, :], in1=x1[:, :],
                                   op0=ALU.mult, op1=ALU.add)

            def add_ffn(n):
                dve.wait_ge(scattered, n)
                dve.wait_ge(ffn_added, n)
                V.tensor_tensor(blocks(ffn[:, :]), ps[:, 4:6, 0:HB], blocks(ffn[:, :]),
                                ALU.add).then_inc(ffn_added, 1)

            def round_(r):
                unit0 = 2 * QU * r

                def split_low(pos, grains):
                    for j in grains:
                        half, b = j // 2, j % 2
                        slot = (2 * pos + half) % SLOTS
                        dve.wait_ge(hi_ready, GRAINS * (unit0 + pos) + j + 1)
                        V.tensor_tensor(wlo[:, j, :, :], raw[:, slot, :, b * HB:(b + 1) * HB],
                                        whi[:, j, :, :].bitcast(f32), ALU.subtract).then_inc(lo_ready, 1)

                def add_bias(q):
                    dve.wait_ge(turned, QU * r + q + 1)
                    V.tensor_tensor(biased[:, :, :], ps[:, 4, 0:HB].rearrange("p (k j) -> p k j", k=KT),
                                    b1_T[:, bass.ds(r, 1), q * KT:(q + 1) * KT].rearrange("p o k -> p (o k)")
                                    .unsqueeze(2).to_broadcast([P, KT, CAP]),
                                    ALU.add).then_inc(biased_ready, 1)

                def split_hidden(q):
                    dve.wait_ge(gelu_done, QU * r + q + 1)
                    V.tensor_copy(hidden[:, q % 2, :, 0:CAP], active[:, :, :]).then_inc(hidden_ready, 1)
                    dve.wait_ge(hidden_ready, 2 * (QU * r + q) + 1)
                    V.tensor_tensor(hidden[:, q % 2, :, CAP:P], active[:, :, :],
                                    hidden[:, q % 2, :, 0:CAP].bitcast(f32), ALU.subtract).then_inc(hidden_ready, 1)

                for pos, (kind, q) in enumerate(UNITS):
                    if kind == "up":
                        split_low(pos, range(3))
                        if q == 0:
                            add_ffn(r + 1)
                            dve.wait_ge(place_turned, r + 1)
                            V.tensor_scalar(place_now[:, :], slot_no[:, :, :].rearrange("p a j -> p (a j)"),
                                            rank[:, bass.ds(r + 1, 1)], None, ALU.is_equal).then_inc(place_ready, 1)
                    else:
                        split_low(pos, range(1))
                        add_bias(q)
                        split_low(pos, range(1, 2))
                        split_hidden(q)
                        split_low(pos, range(2, 3))
                        if q == QU - 2:
                            take_gathered(r + 2, 5)

            dve.wait_ge(route_ready, 1)
            rounds = dve.value_load(route[0:1, 0:1], min_val=ROUNDS, max_val=ROUNDS + 1)
            with dve.Fori(0, rounds) as r:
                round_(r)
            dve.wait_ge(scattered, rounds + 1)
            dve.wait_ge(ffn_added, rounds + 1)
            step(V.tensor_tensor(blocks(ffn[:, :]), ps[:, 4:6, 0:HB], blocks(ffn[:, :]), ALU.add))

            dve.wait_ge(spread, HEADS + 4)
            step(V.tensor_scalar(ffn[:, :], ffn[:, :], col(TOPP), None, ALU.mult))
            step(V.tensor_tensor_reduce(out=xc[:, :], in0=ffn[:, :], in1=wv_rows[:, :], scale=1.0, scalar=0.0,
                                        op0=ALU.mult, op1=ALU.add, accum_out=col(VCOL)))
            step(V.tensor_tensor(col(VCOL), col(VCOL), bv_c[:, :], ALU.add))
            V.tensor_scalar(col(VCOL), col(VCOL), VMAX, -VMAX, ALU.min, ALU.max).then_inc(v_ready, 1)
            V.tensor_tensor(x1[:, :], x1[:, :], ffn[:, :], ALU.add)

            V.tensor_scalar(alt_i[:, :], free_i[0:1, :], 1, None, ALU.bitwise_and)
            V.memset(cf_d[:, :, :], 1.0)
            step(V.memset(cf_u[:, 0, :], 0.0))
            V.memset(cf_u[:, 0, 0:1], FAR)
            step(V.memset(cf_u[:, 0, 2:3], FAR))
            step(V.tensor_copy(alt[:, 0, :], alt_i[:, :]))
            step(V.tensor_scalar(alt[:, 1, :], alt[:, 0, :], -2.0, 1.0, ALU.mult, ALU.add))
            dve.wait_ge(v_turned, 1)
            step(V.tensor_copy(v_row[:, :], ps[0:1, 7, 0:P]))
            V.tensor_tensor(cf_d[:, :, 0], v_row[:, :], alt[:, 1, :], ALU.mult)
            step(V.tensor_tensor(cf_d[:, :, 2], v_row[:, ::-1], alt[:, 1, :], ALU.mult))
            CF_UNROLL, CF_OPS = 4, 5
            with dve.Fori(0, N // CF_UNROLL) as i:
                for k in range(CF_UNROLL):
                    at = i * CF_UNROLL + k
                    u = cf_u[:, bass.ds(at, 1), :].rearrange("p o (d c) -> p (o d) c", d=2)
                    nxt = cf_u[:, bass.ds(at + 1, 1), :].rearrange("p o (d c) -> p (o d) c", d=2)
                    dd = cf_d[:, bass.ds(at, 1), :].rearrange("p o (d c) -> p (o d) c", d=2)
                    sq = cf_t[:, 0:4].rearrange("p (d c) -> p d c", d=2)
                    ops = [
                        lambda: V.tensor_tensor(sq, u, u, ALU.mult),
                        lambda: V.tensor_tensor(cf_t[:, 4:6], sq[:, :, 0], sq[:, :, 1], ALU.add),
                        lambda: V.reciprocal(cf_t[:, 6:8], cf_t[:, 4:6]),
                        lambda: V.tensor_tensor(cf_t[:, 8:12].rearrange("p (d c) -> p d c", d=2), u,
                                                cf_t[:, 6:8].unsqueeze(2).to_broadcast([1, 2, 2]), ALU.mult),
                        lambda: V.tensor_tensor(nxt, cf_t[:, 8:12].rearrange("p (d c) -> p d c", d=2), dd, ALU.add),
                    ]
                    for o, op in enumerate(ops):
                        op().then_inc(cf_step, 1)
                        dve.wait_ge(cf_step, i * (CF_UNROLL * CF_OPS) + k * CF_OPS + o + 1)

            g = [g_rows[:, n, :] for n in range(6)]
            step(V.tensor_tensor(g[0], cf_u[:, 1:N + 1, 0], cf_d[:, :, 0], ALU.subtract))
            step(V.tensor_tensor(g[0], g[0], alt[:, 1, :], ALU.mult))
            step(V.tensor_tensor(g[1], cf_u[:, N:0:-1, 2], alt[:, 1, ::-1], ALU.mult))
            step(V.tensor_tensor(g[0], g[0], g[1], ALU.add))
            step(V.tensor_tensor(g[1], cf_u[:, 1:N + 1, 1], cf_u[:, N:0:-1, 3], ALU.add))
            step(V.tensor_scalar(g[1], g[1], -1.0, None, ALU.add))
            V.tensor_tensor(g[2], g[0], g[0], ALU.mult)
            step(V.tensor_tensor(g[3], g[1], g[1], ALU.mult))
            step(V.tensor_tensor(g[2], g[2], g[3], ALU.add))
            step(V.reciprocal(g[3], g[2]))
            V.tensor_tensor(g[4], g[0], g[3], ALU.mult)
            V.tensor_tensor(g[5], g[1], g[3], ALU.mult).then_inc(g_ready, 1)
            dve.wait_ge(g_turned, 1)
            step(V.tensor_scalar(feats[:, :], ps[:, 7, 40:42], keep[:, :], FCLAMP, ALU.mult, ALU.min))
            step(V.tensor_scalar(feats[:, :], feats[:, :], -FCLAMP, bk_c[:, :], ALU.max, ALU.mult))
            step(V.scalar_tensor_tensor(out=x1[:, :], in0=wo_rows[:, 0, :], scalar=feats[:, 0:1], in1=x1[:, :],
                                        op0=ALU.mult, op1=ALU.add))
            V.scalar_tensor_tensor(out=xc[:, :], in0=wo_rows[:, 1, :], scalar=feats[:, 1:2], in1=x1[:, :],
                                   op0=ALU.mult, op1=ALU.add).then_inc(final_ready, 1)

        @block.tensor
        def _(pe):
            def turn_x(i):
                pe.wait_ge(xn_ready, i)
                for k in range(KT):
                    last = T.transpose(ps[:, 5 + k // 3, (k % 3) * P:(k % 3 + 1) * P], xn[:, k * P:(k + 1) * P],
                                       ident[:, :])
                last.then_inc(xT_done, 1)

            pe.wait_ge(consts, 1)
            turn_x(1)
            pe.wait_ge(small_in, 16 * 10)
            T.transpose(ps[:, 7, 128:128 + HEADS * KT], gb1_rows[:, :], ident[0:HEADS * KT, 0:HEADS * KT])
            for g in range(2):
                last = T.transpose(ps[:, 7, 192 + 96 * g:288 + 96 * g], b1_rows[:, g, :], ident[0:96, 0:96])
            last.then_inc(bias_done, 1)
            pe.wait_ge(bias_ready, 1)
            for c in range(4):
                pe.wait_ge(hot_ready, c + 1)
                for j in range(8):
                    last = T.matmul(ps[:, 7, 0:P], dst_hot[:, j, :], src_hot[:, j, :],
                                    start=(c == 0 and j == 0), stop=False)
                if c == 3:
                    last = T.matmul(ps[:, 7, 0:P], ident_b[:, :], ident_b[:, :], start=False, stop=True)
                last.then_inc(hot_used, 1)

            def raw_ready(n):
                pe.wait_ge(raw_in[n % SLOTS], 16 * (n // SLOTS + 1))

            def head_up(h):
                if h >= 2:
                    pe.wait_ge(h_ready, h - 1)
                for half in range(2):
                    n = 2 * h + half
                    raw_ready(n)
                    for k in range(3):
                        for b in range(2):
                            last = T.matmul(ps[:, 2 * (h % 2) + b, 0:HB], xT[:, 3 * half + k, :],
                                            raw[:, n % SLOTS, k, b * HB:(b + 1) * HB],
                                            start=(n % 2 == 0 and k == 0), stop=(n % 2 == 1 and k == 2))
                    last.then_inc(used, 2)

            def scores(a, n, source):
                if a:
                    pe.wait_ge(att_ready, a)
                for h in range(n):
                    last = T.matmul(ps[:, 4, h * P:(h + 1) * P], source(h).to_broadcast([P, P]), ident[:, :],
                                    start=True, stop=True)
                last.then_inc(att_scores, 1)

            def turn_weights(a, n, first):
                pe.wait_ge(att_prob, a + 1)
                for h in range(n):
                    last = T.transpose(ps[:, 4, first + h * P:first + (h + 1) * P], att_p[:, h, :], ident[:, :])
                last.then_inc(att_turned, 1)

            def aggregate(k):
                h = k // 2
                pe.wait_ge(att_ready, h // GROUP + 1)
                if k >= 2:
                    pe.wait_ge(elu_in, k - 1)
                for j in range(3):
                    c = (3 * (k % 2) + j) * P
                    last = T.matmul(ps[:, 5 + k % 2, j * P:(j + 1) * P], h_sb[:, h, c:c + P],
                                    att_T[:, h % GROUP, :], start=True, stop=True)
                last.then_inc(agg_done, 1)

            def head_down(h):
                pe.wait_ge(elu_ready, 2 * (h + 1))
                for half in range(2):
                    n = 2 * (HEADS + h) + half
                    raw_ready(n)
                    for k in range(3):
                        for b in range(2):
                            last = T.matmul(ps[:, b, 0:HB], eluT[:, KT * h + 3 * half + k, :],
                                            raw[:, n % SLOTS, k, b * HB:(b + 1) * HB],
                                            start=(h == 0 and half == 0 and k == 0),
                                            stop=(h == HEADS - 1 and half == 1 and k == 2))
                    last.then_inc(used, 2)

            pe.wait_ge(xT_ready, 1)
            for h in range(5):
                head_up(h)
            pe.wait_ge(alpha_used, GROUP)
            scores(0, GROUP, lambda h: alpha[:, 0, h:h + 1])
            head_up(5)
            turn_weights(0, GROUP, 0)
            head_up(6)
            for k in range(4):
                aggregate(k)
            head_up(7)
            for k in range(4, 8):
                aggregate(k)
            pe.wait_ge(h_ready, HEADS - 1)
            head_down(0)
            pe.wait_ge(alpha_used, HEADS)
            scores(1, GROUP, lambda h: alpha[:, 0, GROUP + h:GROUP + h + 1])
            head_down(1)
            turn_weights(1, GROUP, 0)
            head_down(2)
            for k in range(8, 12):
                aggregate(k)
            head_down(3)
            for k in range(12, 16):
                aggregate(k)
            for h in range(4, HEADS):
                head_down(h)

            pe.wait_ge(alpha_used, HEADS + 1)
            scores(2, 1, lambda h: alpha2[:, 0, :])
            turn_weights(2, 1, P)
            pe.wait_ge(att_ready, 3)
            pe.wait_ge(h2_ready, 1)
            for b in range(2):
                last = T.matmul(ps[:, 2 + b, 0:HB], att_T[:, 0, :], h2_sb[:, b * HB:(b + 1) * HB],
                                start=True, stop=True)
            last.then_inc(out2_done, 1)
            turn_x(2)
            pe.wait_ge(xT_ready, 2)
            for k in range(KT):
                last = T.matmul(ps[:, 7, 0:EXPERTS + 1], xT[:, k, :], gate_w[:, k, :], start=(k == 0),
                                stop=(k == KT - 1))
            last.then_inc(logit_done, 1)

            pe.wait_ge(onehot_ready, 1)
            T.matmul(ps[:, 7, 16:24], later[:, :], hot[:, :], start=True, stop=True)
            T.matmul(ps[:, 7, 24:32], ones[:, :], hot[:, :], start=True, stop=True)
            T.transpose(ps[0:EXPERTS, 7, 128:256], hot[:, :], ident[:, :]).then_inc(rank_done, 1)

            def gather(bank):
                for k in range(KT):
                    last = T.matmul(ps[:, bank, k * CAP:(k + 1) * CAP], xn[:, k * P:(k + 1) * P],
                                    place_now[:, 0:CAP], start=True, stop=True)
                last.then_inc(gather_done, 1)

            pe.wait_ge(place_ready, 1)
            gather(6)
            pe.wait_ge(hot_T_ready, 1)
            for b in range(2):
                last = T.matmul(ps[:, 4 + b, 0:HB], hot_T[:, :], b2_sb[:, b * HB:(b + 1) * HB],
                                start=True, stop=True)
            last.then_inc(scattered, 1)
            pe.wait_ge(score_ready, 1)
            T.matmul(ps[0:1, 7, 256:384], col(SCORE), ident[:, :], start=True, stop=True).then_inc(score_turned, 1)
            pe.wait_ge(thr_ready, 1)
            T.matmul(ps[:, 7, 32:33], ones[0:1, :], top16[0:1, KEEP - 1:KEEP], start=True,
                     stop=True).then_inc(thr_done, 1)

            def round_(r):
                unit0 = 2 * QU * r

                def stream(pos, stationary, bank, first, last_):
                    for j in range(GRAINS):
                        half, b = j // 2, j % 2
                        if j < 3:
                            pe.wait_ge(lo_ready, 3 * (unit0 + pos) + j + 1)
                        else:
                            pe.wait_ge(lo_pool, unit0 + pos + 1)
                        for k in range(3):
                            for part in (whi, wlo):
                                last = T.matmul(ps[:, bank + b, 0:HB], stationary[:, 3 * half + k, :],
                                                part[:, j, k, :],
                                                start=(first and half == 0 and k == 0 and part is whi),
                                                stop=(last_ and half == 1 and k == 2 and part is wlo))
                        last.then_inc(used, 1)

                for pos, (kind, q) in enumerate(UNITS):
                    if kind == "up":
                        if q == 0:
                            pe.wait_ge(gathered_ready, 2 * r + 2)
                        stream(pos, gathered, 2 * (q % 2), True, True)
                        if q == 0:
                            pe.wait_ge(ffn_added, r + 2)
                            T.transpose(ps[:, 5, HB:512], place_now[:, :], ident[:, :]).then_inc(place_turned, 1)
                        if q == QU - 1:
                            pe.wait_ge(place_ready, r + 2)
                            pe.wait_ge(place_T_ready, r + 1)
                            gather(5)
                    else:
                        pe.wait_ge(upper_ready, QU * r + q + 1)
                        for k in range(KT):
                            last = T.matmul(ps[:, 4, k * CAP:(k + 1) * CAP], upper[:, q % 2, k * P:(k + 1) * P],
                                            fold[:, :], start=True, stop=True)
                        last.then_inc(turned, 1)
                        pe.wait_ge(hidden_ready, 2 * (QU * r + q + 1))
                        stream(pos, hidden[:, q % 2, :, :], 6, q == 0, q == QU - 1)
                pe.wait_ge(y_ready, r + 1)
                pe.wait_ge(gathered_ready, 2 * r + 4)
                for b in range(2):
                    last = T.matmul(ps[:, 4 + b, 0:HB], place_T[:, :], y_sb[:, b * HB:(b + 1) * HB],
                                    start=True, stop=True)
                last.then_inc(scattered, 1)

            pe.wait_ge(route_ready, 1)
            rounds = pe.value_load(route[0:1, 0:1], min_val=ROUNDS, max_val=ROUNDS + 1)
            with pe.Fori(0, rounds) as r:
                round_(r)

            pe.wait_ge(v_ready, 1)
            T.matmul(ps[0:1, 7, 0:P], col(VCOL), ident[:, :], start=True, stop=True).then_inc(v_turned, 1)
            pe.wait_ge(g_ready, 1)
            for n in range(2):
                last = T.matmul(ps[:, 7, 40 + n:41 + n], g_rows[0:1, 4 + n, :], ones[0:1, 0:1],
                                start=True, stop=True)
            last.then_inc(g_turned, 1)


_SHAPES = {
    "x": (N, D), "src": (EDGES,), "dst": (EDGES,), "L0_gnn_W1": (D, HEADS * D), "L0_gnn_a_src1": (HEADS, D),
    "L0_gnn_a_dst1": (HEADS, D), "L0_gnn_b1": (HEADS * D,), "L0_gnn_W2": (HEADS * D, D),
    "L0_gnn_a_src2": (1, D), "L0_gnn_a_dst2": (1, D), "L0_gnn_b2": (1, D), "L0_ffn_Wg": (D, EXPERTS),
    "L0_ffn_bg": (1, EXPERTS), "L0_ffn_W1": (EXPERTS, D, HID), "L0_ffn_b1": (EXPERTS, HID),
    "L0_ffn_W2": (EXPERTS, HID, D), "L0_ffn_b2": (EXPERTS, D), "L0_ffn_Wv": (1, D), "L0_ffn_bv": (1, 1),
    "L0_ffn_Wm": (D, 1), "L0_ffn_bm": (1, 1), "L0_ffn_Wo": (2, D), "L0_ffn_bo": (1, D),
    "L0_ffn_bk_scale": (1, 1),
}


def kernel(**inputs):
    import numpy as _np
    import concourse.bacc as _bacc
    from concourse import mybir as _mybir
    from concourse.bass_utils import run_bass_kernel_spmd as _run

    nc = _bacc.Bacc("TRN2", target_bir_lowering=False, num_devices=1)
    arrays, args = {}, []
    for name, shape in _SHAPES.items():
        a = _np.ascontiguousarray(inputs[name]).reshape(shape)
        arrays[f"in_{name}"] = a
        args.append(nc.dram_tensor(f"in_{name}", shape, _mybir.dt.from_np(a.dtype), kind="ExternalInput").ap())
    out = nc.dram_tensor("out", (N, D), _mybir.dt.float32, kind="ExternalOutput").ap()
    gnn_moe_kernel(nc, *args, out)
    r = _run(nc, [arrays], core_ids=[0])
    return r.results[0]["out"]
```

```python
import concourse.bass as bass
from concourse import mybir
from contextlib import ExitStack

P = 128
N = 128
D = 768
HEADS = 8
EDGES = 4096
EXPERTS = 8
HID = 3072
KT = D // P
HB = D // 2
QU = HID // D
CAP = 64
ROUNDS = EXPERTS
SLOTS = 8
GRAINS = 4
POOL_GRAIN = 2
VECTOR_GRAINS = (0, 1, 3)
KEEP = 12
EPS = 1e-5
VMAX = 3.0
FCLAMP = 10.0
NEG = -1e30
FAR = 1e18
CL = 8
CH = N // CL
BACK = 32
CP = BACK + CH
CHUNK_SCALE = 2.3 ** -CL
GROUP = 4
SMALL = 10
GNN_HALVES = 2 * 2 * HEADS
ROUND_HALVES = 2 * 2 * QU
EARLY = 3
ATONCE = 6
UNITS = [("up", 0), ("up", 1), ("down", 0), ("up", 2), ("down", 1), ("up", 3), ("down", 2), ("down", 3)]


def gnn_moe_kernel(nc, x, src, dst, gw1, gas1, gad1, gb1, gw2, gas2, gad2, gb2,
                   wg, bg, w1, b1, w2, b2, wv, bv, wm, bm, wo, bo, bks, out):
    f32, f32r, bf16, i32 = mybir.dt.float32, mybir.dt.float32r, mybir.dt.bfloat16, mybir.dt.int32
    ALU, ACT = mybir.AluOpType, mybir.ActivationFunctionType
    AX = mybir.AxisListType.X
    V, S, G, T = nc.vector, nc.scalar, nc.gpsimd, nc.tensor

    ctx = ExitStack()
    with ctx:
        ctx.enter_context(nc.allow_non_contiguous_dma(reason="the gate's columns, 768 words each"))

        def sem(name):
            return ctx.enter_context(nc.semaphore(name))

        base = (nc.sbuf_base + 31) // 32 * 32
        ctx.enter_context(nc.sbuf_tensor("slab", [P, (nc.sbuf_usable_end - base - 64) // 4], f32))
        top = [base]

        def size(shape, dt):
            n = 2 if dt == bf16 else 4
            for s in shape[1:]:
                n *= s
            return (n + 31) // 32 * 32

        def place(name, shape, dt=f32):
            t = nc.alloc_sbuf_tensor_at(name, shape, dt, offset=top[0])
            top[0] += size(shape, dt)
            return t

        def region(tenants):
            first, end, got = top[0], top[0], []
            for tensors in tenants:
                top[0] = first
                got += [place(*t) for t in tensors]
                end = max(end, top[0])
            top[0] = end
            return got

        raw = place("raw", [P, SLOTS, 3, D])
        h_sb, whi, wlo = region([
            [("h_sb", [P, HEADS, D])],
            [("whi", [P, GRAINS, 3, HB], f32r), ("wlo", [P, GRAINS, 3, HB], f32r)]])
        (src_hot, dst_hot, early_rows, eluT, gathered, upper, biased, active, hidden,
         y_sb, ffn, place_now, place_T) = region([
             [("src_hot", [P, 8, P], bf16), ("dst_hot", [P, 8, P], bf16), ("early_rows", [1, 3, 2, D])],
             [("eluT", [P, HEADS * KT, P])],
             [("gathered", [P, KT, P], f32r), ("upper", [P, 2, D]), ("biased", [P, KT, CAP]),
              ("active", [P, KT, CAP]), ("hidden", [P, 2, KT, P], f32r), ("y_sb", [P, D]),
              ("ffn", [P, D]), ("place_now", [P, P]), ("place_T", [P, P])]])
        (rows, cf_w, cf_v, cf_t, cf_m, cf_mm, cf_s, cf_x, cf_n, cf_p, cf_b, cf_y, cf_th, cf_q, cf_r, cf_a,
         cf_d, cf_c, cf_g, cf_e, cf_f) = region([
             [("rows", [1, 2, D])],
             [("cf_w", [CP, CL + 2, 4 * (CL + 2)]), ("cf_v", [CP, CL]), ("cf_t", [CP, 4 * (CL + 2)]),
              ("cf_m", [CP, CH, 16]), ("cf_mm", [2, CH, 16]), ("cf_s", [2, CH, 4]), ("cf_x", [2, 4, 4]),
              ("cf_n", [2, CH]), ("cf_p", [CP, CH, 4]), ("cf_b", [CP, 4]), ("cf_y", [CP, CL + 1, 2, 4]),
              ("cf_th", [CP, CL + 1, 2]), ("cf_q", [CP, 3, CL, 2]), ("cf_r", [CP, CL]), ("cf_a", [CP, CL, 2]),
              ("cf_d", [CH, CL, 2]), ("cf_c", [CH, CL, 2]), ("cf_g", [CH, CL, 2]), ("cf_e", [CH, CL]),
              ("cf_f", [P, CL, 2])]])
        att_rows, wo_rows, wv_rows = region([
            [("att_rows", [P, 2, 2, D])],
            [("wo_rows", [P, 2, D]), ("wv_rows", [P, D])]])
        att2_rows = place("att2_rows", [P, 2, D])
        bias_rows = place("bias_rows", [P, 2, D])
        x_sb = place("x_sb", [P, D])
        x1 = place("x1", [P, D])
        xc = place("xc", [P, D])
        xn = place("xn", [P, D])
        xT = place("xT", [P, KT, P])
        att_e = place("att_e", [P, GROUP, P])
        att_p = place("att_p", [P, GROUP, P])
        att_T = place("att_T", [P, GROUP, P])
        elu_y, elu_e, h2_sb = region([
            [("elu_y", [P, 2, 3, P]), ("elu_e", [P, 2, 3, P])],
            [("h2_sb", [P, D])]])
        counts = place("counts", [P, P])
        mask_bias = place("mask_bias", [P, P])
        free_i = place("free_i", [P, P], i32)
        part_i = place("part_i", [P, 1], i32)
        free_f = place("free_f", [P, P])
        part_f = place("part_f", [P, 1])
        ident = place("ident", [P, P])
        ident_b = place("ident_b", [P, P], bf16)
        later = place("later", [P, P])
        slot_no = place("slot_no", [P, 2, CAP])
        fold = place("fold", [P, CAP])
        ones = place("ones", [P, P])
        edges_i = place("edges_i", [P, 2, EDGES // P], i32)
        edges_f = place("edges_f", [P, 2, EDGES // P])
        gb1_rows = place("gb1_rows", [HEADS * KT, P])
        gb1_T = place("gb1_T", [P, HEADS * KT])
        b1_rows = place("b1_rows", [96, 2, P])
        b1_T = place("b1_T", [P, EXPERTS + 1, QU * KT])
        b1_over = place("b1_over", [P, EXPERTS, QU * KT])
        b2_sb = place("b2_sb", [EXPERTS, D])
        gate_w = place("gate_w", [P, KT, EXPERTS + 1])
        gate_b = place("gate_b", [P, EXPERTS + 1])
        bv_c = place("bv_c", [P, 1])
        bk_c = place("bk_c", [P, 1])
        minus_bk = place("minus_bk", [P, 1])
        half_pow = place("half_pow", [P, 1])
        alpha = place("alpha", [P, 2, HEADS])
        alpha2 = place("alpha2", [P, 2, 1])
        small = place("small", [P, 64])
        e8 = place("e8", [P, EXPERTS])
        logit = place("logit", [P, EXPERTS + 1])
        prob = place("prob", [P, EXPERTS])
        hot_wide = place("hot_wide", [P, P])
        hot = hot_wide[:, 0:EXPERTS]
        best8 = place("best8", [P, EXPERTS])
        rank = place("rank", [P, EXPERTS + 2])
        over = place("over", [P, EXPERTS])
        route_f = place("route_f", [P, 2])
        route = place("route", [P, 2], i32)
        score_row = place("score_row", [1, 2, P])
        top16 = place("top16", [1, 16])
        keep = place("keep", [P, 1])
        feats = place("feats", [P, 2])
        shifted_i = place("shifted_i", [P, 4], i32)
        shifted = place("shifted", [P, 4])
        wide_i = place("wide_i", [P, 2, P], i32)
        wide = place("wide", [P, 2, P])
        to_forward = place("to_forward", [P, CP])
        to_back = place("to_back", [P, CP])
        step_mask = place("step_mask", [P, CL])
        own_step = place("own_step", [P, CL])
        v_steps = place("v_steps", [P, CL])
        own_chunk = place("own_chunk", [CP, CH])
        direction = place("direction", [CP, 2])
        to_chunks = place("to_chunks", [2, CP])
        turn_back = place("turn_back", [CP, CH])
        to_nodes = place("to_nodes", [CH, P])
        assert top[0] <= nc.sbuf_usable_end, (top[0], nc.sbuf_usable_end)

        ps = ctx.enter_context(nc.psum_tensor("ps", [P, 8, 512], f32))

        def col(i, n=1):
            return small[:, i:i + n]

        SUM, MEAN, VAR, RSTD, MX, SS, RS = 0, 1, 2, 3, 4, 12, 20
        TOPP, VSUM, SCORE, VCOL, SMAX, IDX = 28, 29, 30, 32, 33, 34

        raw_in = [sem(f"raw_in{i}") for i in range(SLOTS)]
        used = sem("used")
        x_in, edges_in, small_in = sem("x_in"), sem("edges_in"), sem("small_in")
        early_in = sem("early_in")
        row_in = sem("row_in")
        spread = sem("spread")
        iota_done, pool_ones = sem("iota_done"), sem("pool_ones")
        dve_step = sem("dve_step")
        consts = sem("consts")
        var_ready, rstd_ready = sem("var_ready"), sem("rstd_ready")
        xc_ready, xT_done = sem("xc_ready"), sem("xT_done")
        xT_first, xT_second = sem("xT_first"), sem("xT_second")
        xn_ready, pre_split = sem("xn_ready"), sem("pre_split")
        hot_ready, hot_used = sem("hot_ready"), sem("hot_used")
        bias_done, bias_ready = sem("bias_done"), sem("bias_ready")
        h_ready = sem("h_ready")
        alpha_used = sem("alpha_used")
        att_scores, att_shift, att_exp = sem("att_scores"), sem("att_shift"), sem("att_exp")
        att_prob, att_turned, att_ready = sem("att_prob"), sem("att_turned"), sem("att_ready")
        agg_done, elu_in, elu_exp, elu_ready = sem("agg_done"), sem("elu_in"), sem("elu_exp"), sem("elu_ready")
        h2_ready, out2_done = sem("h2_ready"), sem("out2_done")
        logit_done, gate_in, gate_exp = sem("logit_done"), sem("gate_in"), sem("gate_exp")
        onehot_ready, rank_done, hot_T_ready = sem("onehot_ready"), sem("rank_done"), sem("hot_T_ready")
        b2_ready = sem("b2_ready")
        route_ready, score_exp = sem("route_ready"), sem("score_exp")
        score_ready, score_turned, thr_ready, thr_done = (sem("score_ready"), sem("score_turned"),
                                                          sem("thr_ready"), sem("thr_done"))
        hi_ready, lo_ready, lo_pool = sem("hi_ready"), sem("lo_ready"), sem("lo_pool")
        upper_ready = sem("upper_ready")
        turned, biased_ready, gelu_done, hidden_ready = (sem("turned"), sem("biased_ready"),
                                                         sem("gelu_done"), sem("hidden_ready"))
        y_ready, scattered, ffn_added = sem("y_ready"), sem("scattered"), sem("ffn_added")
        place_ready, place_turned, place_T_ready = (sem("place_ready"), sem("place_turned"),
                                                    sem("place_T_ready"))
        gather_done, gathered_ready = sem("gather_done"), sem("gathered_ready")
        keep_ready, minus_ready, wo_scaled = sem("keep_ready"), sem("minus_ready"), sem("wo_scaled")
        last_dot, last_scaled, x1_done = sem("last_dot"), sem("last_scaled"), sem("x1_done")
        v_ready, v_turned = sem("v_ready"), sem("v_turned")
        cf_init, cf_ready, cf_moved = sem("cf_init"), sem("cf_ready"), sem("cf_moved")
        final_ready, out_done = sem("final_ready"), sem("out_done")

        def used_in(r, pos):
            return GRAINS * (2 * HEADS + 2 * QU * r + pos)

        def blocks(t):
            return t.rearrange("p (b c) -> p b c", b=2)

        block = ctx.enter_context(nc.Block())

        @block.sync
        def _(sp):
            def gnn_half(n):
                unit, half = n // 2, n % 2
                if unit < HEADS:
                    rows_ = gw1[half * 3 * P:(half + 1) * 3 * P, unit * D:(unit + 1) * D]
                else:
                    at = (unit - HEADS) * D + half * 3 * P
                    rows_ = gw2[at:at + 3 * P, :]
                return rows_.rearrange("(k p) c -> p k c", p=P)

            sp.dma_start(x_sb[:, :], x).then_inc(x_in, 16)
            for j, vectors in enumerate((gas1, gad1)):
                sp.dma_start(early_rows[0:1, :, j, :], vectors[0:EARLY, :].unsqueeze(0)).then_inc(early_in, 16)
            for n in range(GNN_HALVES):
                if n >= SLOTS:
                    sp.wait_ge(used, 2 * (n - SLOTS + 1))
                sp.dma_start(raw[:, n % SLOTS, :, :], gnn_half(n)).then_inc(raw_in[n % SLOTS], 16)

            def load_round(r, e, first=False):
                for i in range(ROUND_HALVES):
                    kind, q = UNITS[i // 2]
                    half = i % 2
                    if kind == "up":
                        view = w1[e, half * 3 * P:(half + 1) * 3 * P, q * D:(q + 1) * D]
                    else:
                        view = w2[e, q * D + half * 3 * P:q * D + (half + 1) * 3 * P, :]
                    if first and i < SLOTS:
                        sp.wait_ge(used, 2 * (GNN_HALVES + i - SLOTS + 1))
                    elif half == 0:
                        sp.wait_ge(lo_ready, 3 * (2 * QU * r + (i - SLOTS) // 2) + 2)
                    elif first:
                        sp.wait_ge(lo_ready, 3 * ((i - SLOTS) // 2) + 3)
                        sp.wait_ge(lo_pool, (i - SLOTS) // 2 + 1)
                    else:
                        sp.wait_ge(used, used_in(r, (i - SLOTS) // 2 + 1))
                    sp.dma_start(raw[:, i % SLOTS, :, :],
                                 view.rearrange("(k p) c -> p k c", p=P)).then_inc(raw_in[i % SLOTS], 16)

            load_round(0, 0, first=True)
            with sp.Fori(1, ROUNDS) as r:
                load_round(r, r)
            sp.wait_ge(route_ready, 1)
            rounds = sp.value_load(route[0:1, 0:1], min_val=ROUNDS, max_val=ROUNDS + 1)
            expert = sp.value_load(route[0:1, 1:2], min_val=0, max_val=EXPERTS - 1)
            with sp.If(rounds > ROUNDS):
                load_round(ROUNDS, expert)
            sp.end_ifs()
            sp.wait_ge(final_ready, 1)
            sp.dma_start(out, xc[:, :]).then_inc(out_done, 16)
            sp.wait_ge(out_done, 16)

        @block.gpsimd
        def _(pool):
            pairs = [(gas1[h:h + 1, :], gad1[h:h + 1, :]) for h in range(HEADS)]
            pairs += [(gas2, gad2), (gb2, bo), (wo[0:1, :], wo[1:2, :]), (wv, wv)]
            targets = [att2_rows, bias_rows, wo_rows, wv_rows]

            def split_last(r, pos):
                slot = (2 * pos + 1) % SLOTS
                pool.wait_ge(hi_ready, GRAINS * (2 * QU * r + pos) + POOL_GRAIN + 1)
                G.tensor_tensor(wlo[:, POOL_GRAIN, :, :], raw[:, slot, :, 0:HB], whi[:, POOL_GRAIN, :, :].bitcast(f32),
                                ALU.subtract).then_inc(lo_pool, 1)

            G.iota(free_i[:, :], pattern=[[1, P]], base=0, channel_multiplier=0).then_inc(iota_done, 1)
            G.iota(part_i[:, :], pattern=[[0, 1]], base=0, channel_multiplier=1).then_inc(iota_done, 1)
            G.memset(half_pow[:, :], -0.5).then_inc(pool_ones, 1)
            places = [early_rows[0:1, i, :, :] for i in range(EARLY)]
            places += [rows[0:1, :, :], att2_rows[0:1, :, :], bias_rows[0:1, :, :], rows[0:1, :, :],
                       early_rows[0:1, EARLY - 1, :, :]] + [rows[0:1, :, :]] * (len(pairs) - HEADS)

            def fetch(i, landed):
                for j in range(2):
                    pool.dma_start(places[i][:, j, :], pairs[i][j]).then_inc(landed, 16)

            for i in range(EARLY, ATONCE):
                fetch(i, row_in)
            pool.wait_ge(var_ready, 1)
            pool.wait_ge(pool_ones, 1)
            G.tensor_tensor(col(RSTD), col(VAR), half_pow[:, :], ALU.pow).then_inc(rstd_ready, 1)
            pool.wait_ge(early_in, 32)
            for i in range(len(pairs)):
                if i >= EARLY:
                    pool.wait_ge(row_in, 32 * (max(i, HEADS - 1 if i >= ATONCE else ATONCE - 1) - EARLY + 1))
                if 2 <= i < HEADS:
                    pool.wait_ge(alpha_used, i - 1)
                if i < HEADS:
                    target = att_rows[:, i % 2, :, :]
                    n = 2
                else:
                    target = targets[i - HEADS]
                    if target is wo_rows:
                        pool.wait_ge(alpha_used, HEADS)
                    n = 1 if i == len(pairs) - 1 else 2
                    target = target[:, :].unsqueeze(1) if n == 1 else target[:, :, :]
                G.partition_broadcast(target.rearrange("p a c -> p (a c)"),
                                      places[i][:, 0:n, :].rearrange("p a c -> p (a c)")).then_inc(spread, 1)
                following = {EARLY: (ATONCE, ATONCE + 1), ATONCE: (HEADS,)}.get(i, (i + 1,) if i >= HEADS else ())
                for later_pair in following:
                    if later_pair < len(pairs):
                        pool.wait_ge(spread, i + 1)
                        fetch(later_pair, row_in)
            split_last(0, 0)
            pool.wait_ge(var_ready, 2)
            G.tensor_tensor(col(RSTD), col(VAR), half_pow[:, :], ALU.pow).then_inc(rstd_ready, 1)

            pool.wait_ge(spread, len(pairs))
            G.memset(cf_w[:, 0:2, :], 0.0).then_inc(cf_init, 1)
            G.memset(cf_s[:, 0, :], 0.0).then_inc(cf_init, 1)
            G.memset(cf_d[:, :, 1], -1.0)
            pool.wait_ge(cf_init, 2)
            for at in range(2):
                for row, sign in ((0, 1.0), (1, 1.0), (2, -1.0), (3, -1.0)):
                    first = 4 * row + 2 * at + row % 2
                    G.memset(cf_w[:, at, first::16], sign)
            G.memset(cf_s[:, 0, 0:1], 1.0 / FAR)
            G.memset(cf_s[:, 0, 2:3], 1.0).then_inc(cf_init, 1)

            def round_(r, first=0):
                for pos in range(first, 2 * QU):
                    split_last(r, pos)

            round_(0, first=1)
            pool.wait_ge(route_ready, 1)
            rounds = pool.value_load(route[0:1, 0:1], min_val=ROUNDS, max_val=ROUNDS + 1)
            with pool.Fori(1, rounds) as r:
                round_(r)
            pool.wait_ge(last_scaled, 1)
            G.tensor_tensor(x1[:, :], x1[:, :], ffn[:, :], ALU.add).then_inc(x1_done, 1)

        @block.scalar
        def _(act):
            act.dma_start(edges_i[:, 0, :], src.rearrange("(p j) -> p j", p=P)).then_inc(edges_in, 16)
            act.dma_start(edges_i[:, 1, :], dst.rearrange("(p j) -> p j", p=P)).then_inc(edges_in, 16)
            for target, view in (
                    (gb1_rows[:, :], gb1.rearrange("(j p) -> j p", p=P)),
                    (b1_rows[:, 0, :], b1[0:4, :].rearrange("e (j p) -> (e j) p", p=P)),
                    (b1_rows[:, 1, :], b1[4:8, :].rearrange("e (j p) -> (e j) p", p=P)),
                    (b2_sb[:, :], b2),
                    (gate_w[:, :, 0:EXPERTS], wg.rearrange("(k p) e -> p k e", p=P)),
                    (gate_w[:, :, EXPERTS:EXPERTS + 1], wm.rearrange("(k p) e -> p k e", p=P)),
                    (gate_b[:, 0:EXPERTS], bg.to_broadcast([P, EXPERTS])),
                    (gate_b[:, EXPERTS:EXPERTS + 1], bm.to_broadcast([P, 1])),
                    (bv_c[:, :], bv.to_broadcast([P, 1])),
                    (bk_c[:, :], bks.to_broadcast([P, 1]))):
                act.dma_start(target, view).then_inc(small_in, 16)

            def take_xT(i):
                act.wait_ge(xT_done, 2 * i)
                S.copy(xT[:, 3:KT, :].rearrange("p k t -> p (k t)"), ps[:, 6, 0:HB]).then_inc(xT_second, 1)

            def split_high(r, pos, j):
                half, b = j // 2, j % 2
                slot = (2 * pos + half) % SLOTS
                if b == 0:
                    act.wait_ge(raw_in[slot], 16 * (GNN_HALVES // SLOTS + 2 * r + (2 * pos + half) // SLOTS + 1))
                S.copy(whi[:, j, :, :], raw[:, slot, :, b * HB:(b + 1) * HB]).then_inc(hi_ready, 1)

            def take_head(h):
                act.wait_ge(used, GRAINS * (h + 1))
                b = 2 * (h % 2)
                S.activation(blocks(h_sb[:, h, :]), ps[:, b:b + 2, 0:HB], ACT.Identity,
                             scale=col(RSTD)).then_inc(h_ready, 1)

            def exponents(a, n):
                act.wait_ge(att_shift, a + 1)
                S.activation(att_p[:, 0:n, :], att_e[:, 0:n, :], ACT.Exp).then_inc(att_exp, 1)

            def elu_exponent(k):
                act.wait_ge(elu_in, k + 1)
                S.activation(elu_e[:, k % 2, :, :], elu_e[:, k % 2, :, :], ACT.Exp).then_inc(elu_exp, 1)

            take_xT(1)
            act.wait_ge(rstd_ready, 1)
            for h in range(4):
                take_head(h)
            act.wait_ge(bias_done, 1)
            S.copy(gb1_T[:, :], ps[:, 4, 0:HEADS * KT])
            S.copy(b1_T[:, 0:EXPERTS, :].rearrange("p (g e) j -> p g (e j)", g=2),
                   ps[:, 4, 192:384].rearrange("p (g j) -> p g j", g=2)).then_inc(bias_ready, 1)
            take_head(4)
            exponents(0, GROUP)
            take_head(5)
            take_head(6)
            for k in range(4):
                elu_exponent(k)
            take_head(7)
            for k in range(4, 8):
                elu_exponent(k)
            exponents(1, GROUP)
            for k in range(8, 16):
                elu_exponent(k)

            act.wait_ge(alpha_used, HEADS)
            act.wait_ge(agg_done, 2 * HEADS)
            for j in range(GRAINS):
                split_high(0, 0, j)

            act.wait_ge(used, GRAINS * 2 * HEADS)
            S.copy(blocks(h2_sb[:, :]), ps[:, 0:2, 0:HB]).then_inc(h2_ready, 1)
            act.wait_ge(att_shift, 3)
            S.activation(att_p[:, 0, :], att_e[:, 0, :], ACT.Exp, bias=col(MX)).then_inc(att_exp, 1)
            take_xT(2)
            act.wait_ge(gate_in, 1)
            S.activation(prob[:, :], prob[:, :], ACT.Exp)
            S.activation(col(SCORE), logit[:, EXPERTS:EXPERTS + 1], ACT.Exp, scale=-1.0).then_inc(gate_exp, 1)
            S.preload_act_table(ACT.Gelu_apprx_tanh)
            act.wait_ge(rank_done, 1)
            act.wait_ge(place_ready, 1)
            S.copy(place_T[:, :], ps[:, 7, 128:256]).then_inc(hot_T_ready, 1)

            def round_(r, first=False):
                def split_highs(pos, grains):
                    for j in grains:
                        act.wait_ge(used, used_in(r, pos - 1) + j + 1)
                        split_high(r, pos, j)

                def take_upper(q):
                    act.wait_ge(used, used_in(r, UNITS.index(("up", q)) + 1))
                    b = 2 * (q % 2)
                    S.copy(blocks(upper[:, q % 2, :]), ps[:, b:b + 2, 0:HB]).then_inc(upper_ready, 1)

                def gelu(q):
                    act.wait_ge(biased_ready, QU * r + q + 1)
                    S.activation(active[:, :, :], biased[:, :, :], ACT.Gelu_apprx_tanh).then_inc(gelu_done, 1)

                for pos, (kind, q) in enumerate(UNITS):
                    if first and pos == 0:
                        continue
                    split_highs(pos, range(1))
                    if pos >= 2 and UNITS[pos - 2][0] == "up":
                        gelu(UNITS[pos - 2][1])
                    split_highs(pos, range(1, 3))
                    if pos == 0:
                        take_y(r)
                    elif UNITS[pos - 1][0] == "up":
                        take_upper(UNITS[pos - 1][1])
                    split_highs(pos, range(3, GRAINS))
                    if first and pos == 1:
                        act.wait_ge(b2_ready, 1)
                        take_y(0)
                    if pos == 2:
                        act.wait_ge(place_turned, r + 1)
                        S.copy(place_T[:, :], ps[:, 5, HB:512]).then_inc(place_T_ready, 1)

            def take_y(n):
                act.wait_ge(used, used_in(n, 0))
                S.copy(blocks(y_sb[:, :]), ps[:, 6:8, 0:HB]).then_inc(y_ready, 1)

            round_(0, first=True)
            act.wait_ge(route_ready, 1)
            rounds = act.value_load(route[0:1, 0:1], min_val=ROUNDS, max_val=ROUNDS + 1)
            with act.Fori(1, rounds) as r:
                round_(r)
            take_y(rounds)
            act.wait_ge(last_dot, 1)
            S.activation(blocks(ffn[:, :]), ps[:, 4:6, 0:HB], ACT.Identity, scale=col(TOPP)).then_inc(last_scaled, 1)
            act.wait_ge(spread, HEADS + 3)
            act.wait_ge(minus_ready, 1)
            S.activation(wo_rows[:, 0, :], wo_rows[:, 0, :], ACT.Identity, scale=bk_c[:, :])
            S.activation(wo_rows[:, 1, :], wo_rows[:, 1, :], ACT.Identity, scale=minus_bk[:, :]).then_inc(wo_scaled, 1)

        @block.vector
        def _(dve):
            steps = [0]

            def step(ins):
                steps[0] += 1
                ins.then_inc(dve_step, 1)
                dve.wait_ge(dve_step, steps[0])

            dve.wait_ge(iota_done, 2)
            V.tensor_copy(free_f[:, :], free_i[:, :])
            V.memset(ones[:, :], 1.0)
            V.memset(rank[:, EXPERTS + 1:EXPERTS + 2], 0.0)
            V.memset(hot_wide[:, EXPERTS:P], 0.0)
            step(V.tensor_copy(part_f[:, :], part_i[:, :]))
            V.tensor_scalar(later[:, :], free_f[:, :], part_f[:, :], None, ALU.is_gt)
            V.tensor_scalar(ident_b[:, :], free_f[:, :], part_f[:, :], None, ALU.is_equal)
            V.tensor_scalar(e8[:, :], free_f[:, 0:EXPERTS], -float(EXPERTS), None, ALU.add)
            for copy in range(2):
                V.tensor_scalar(slot_no[:, copy, :], free_f[:, 0:CAP], 1.0, None, ALU.add)
            step(V.tensor_scalar(ident[:, :], free_f[:, :], part_f[:, :], None, ALU.is_equal))
            V.tensor_tensor(fold[:, :], ident[:, 0:CAP], ident[:, CAP:2 * CAP], ALU.add).then_inc(consts, 1)

            def normalise(source, i):
                step(V.tensor_scalar(col(MEAN), col(SUM), 1.0 / D, None, ALU.mult))
                V.tensor_scalar(xc[:, :], source[:, :], col(MEAN), None, ALU.subtract).then_inc(xc_ready, 1)
                dve.wait_ge(xc_ready, i)
                step(V.tensor_tensor_reduce(out=xn[:, :], in0=xc[:, :], in1=xc[:, :], scale=1.0, scalar=0.0,
                                            op0=ALU.mult, op1=ALU.add, accum_out=col(SS)))
                V.tensor_scalar(col(VAR), col(SS), 1.0 / D, EPS, ALU.mult, ALU.add).then_inc(var_ready, 1)

            def take_xT(i):
                dve.wait_ge(xT_done, 2 * i - 1)
                V.tensor_copy(xT[:, 0:3, :].rearrange("p k t -> p (k t)"), ps[:, 5, 0:HB]).then_inc(xT_first, 1)

            dve.wait_ge(x_in, 16)
            step(V.reduce_sum(col(SUM), x_sb[:, :], AX))
            normalise(x_sb, 1)
            take_xT(1)

            dve.wait_ge(edges_in, 32)
            step(V.tensor_copy(edges_f[:, :, :], edges_i[:, :, :]))

            def hot_edges(c):
                if c:
                    dve.wait_ge(hot_used, c)
                for j, target in ((0, src_hot), (1, dst_hot)):
                    last = V.tensor_tensor(target[:, :, :], free_f[:, :].unsqueeze(1).to_broadcast([P, 8, P]),
                                           edges_f[:, j, 8 * c:8 * c + 8].unsqueeze(2).to_broadcast([P, 8, P]),
                                           ALU.is_equal)
                last.then_inc(hot_ready, 1)

            def take_counts():
                dve.wait_ge(hot_used, 4)
                V.tensor_copy(counts[:, :], ps[:, 7, 0:P])
                step(V.tensor_scalar(mask_bias[:, :], ps[:, 7, 0:P], 0.0, NEG, ALU.is_equal, ALU.mult))

            def head_alpha(h):
                dve.wait_ge(h_ready, h + 1)
                dve.wait_ge(spread, h + 1)
                for j in range(2):
                    dot = V.tensor_tensor_reduce(out=xc[:, :], in0=h_sb[:, h, :], in1=att_rows[:, h % 2, j, :],
                                                 scale=1.0, scalar=0.0, op0=ALU.mult, op1=ALU.add,
                                                 accum_out=alpha[:, j, h:h + 1])
                    if j == 0:
                        step(dot)
                dot.then_inc(alpha_used, 1)
                dve.wait_ge(alpha_used, h + 1)

            def attention(a, n, dst_alpha, turned_at):
                R = ps[:, 4, 0:n * P].rearrange("p (h s) -> p h s", h=n)
                shape = [P, n, P]
                e, p = att_e[:, 0:n, :], att_p[:, 0:n, :]
                dve.wait_ge(att_scores, a + 1)
                step(V.tensor_tensor(p, R, dst_alpha.unsqueeze(2).to_broadcast(shape), ALU.add))
                step(V.scalar_tensor_tensor(out=e, in0=p, scalar=0.2, in1=p, op0=ALU.mult, op1=ALU.max))
                step(V.tensor_tensor(e, e, mask_bias[:, :].unsqueeze(1).to_broadcast(shape), ALU.add))
                step(V.reduce_max(col(MX, n), e, AX))
                V.tensor_tensor(e, e, col(MX, n).unsqueeze(2).to_broadcast(shape), ALU.subtract).then_inc(att_shift, 1)
                dve.wait_ge(att_exp, a + 1)
                step(V.tensor_tensor(p, p, counts[:, :].unsqueeze(1).to_broadcast(shape), ALU.mult))
                step(V.reduce_sum(col(SS, n), p, AX))
                step(V.reciprocal(col(RS, n), col(SS, n)))
                V.tensor_tensor(p, p, col(RS, n).unsqueeze(2).to_broadcast(shape), ALU.mult).then_inc(att_prob, 1)
                dve.wait_ge(att_turned, a + 1)
                V.tensor_copy(att_T[:, 0:n, :].rearrange("p h s -> p (h s)"), turned_at).then_inc(att_ready, 1)

            def split_low(r, pos, j):
                half, b = j // 2, j % 2
                slot = (2 * pos + half) % SLOTS
                dve.wait_ge(hi_ready, GRAINS * (2 * QU * r + pos) + j + 1)
                V.tensor_tensor(wlo[:, j, :, :], raw[:, slot, :, b * HB:(b + 1) * HB],
                                whi[:, j, :, :].bitcast(f32), ALU.subtract).then_inc(lo_ready, 1)

            def elu(k):
                shape = [P, 3, P]
                y, e = elu_y[:, k % 2, :, :], elu_e[:, k % 2, :, :]
                dve.wait_ge(agg_done, k + 1)
                if k >= 2:
                    dve.wait_ge(elu_ready, k - 1)
                step(V.tensor_tensor(y, ps[:, 5 + k % 2, 0:HB].rearrange("p (j t) -> p j t", j=3),
                                     gb1_T[:, 3 * k:3 * k + 3].unsqueeze(2).to_broadcast(shape), ALU.add))
                V.tensor_scalar(e, y, 0.0, None, ALU.min).then_inc(elu_in, 1)
                step(V.tensor_scalar(y, y, 0.0, None, ALU.max))
                if k % 8:
                    elu_out(k - 1)

            def elu_out(k):
                dve.wait_ge(elu_exp, k + 1)
                V.scalar_tensor_tensor(out=eluT[:, 3 * k:3 * k + 3, :], in0=elu_e[:, k % 2, :, :], scalar=-1.0,
                                       in1=elu_y[:, k % 2, :, :], op0=ALU.add, op1=ALU.add).then_inc(elu_ready, 1)

            hot_edges(0)
            V.tensor_scalar(shifted_i[:, 0:1], part_i[:, :], 3, None, ALU.logical_shift_right)
            V.tensor_scalar(shifted_i[:, 1:2], part_i[:, :], CL - 1, None, ALU.bitwise_and)
            V.tensor_scalar(shifted_i[:, 2:3], part_i[:, :], CH - 1, None, ALU.bitwise_and)
            V.tensor_scalar(wide_i[:, 0, :], free_i[:, :], 3, None, ALU.logical_shift_right)
            V.tensor_scalar(wide_i[:, 1, :], free_i[:, :], 5, None, ALU.logical_shift_right)
            V.memset(to_forward[:, :], 0.0)
            step(V.memset(to_back[:, :], 0.0))
            V.tensor_copy(wide[:, :, :], wide_i[:, :, :])
            step(V.tensor_copy(shifted[:, 0:3], shifted_i[:, 0:3]))
            step(V.tensor_scalar(shifted[:, 3:4], shifted[:, 0:1], -1.0, float(CH - 1), ALU.mult, ALU.add))
            V.tensor_scalar(to_forward[:, 0:CH], free_f[:, 0:CH], shifted[:, 0:1], None, ALU.is_equal)
            V.tensor_scalar(to_back[:, BACK:CP], free_f[:, 0:CH], shifted[:, 3:4], None, ALU.is_equal)
            V.tensor_scalar(step_mask[:, :], free_f[:, 0:CL], shifted[:, 1:2], None, ALU.is_equal)
            V.tensor_scalar(own_chunk[:, :], free_f[0:CP, 0:CH], shifted[0:CP, 2:3], CHUNK_SCALE,
                            ALU.is_equal, ALU.mult)
            V.tensor_scalar(direction[:, 0:1], part_f[0:CP, :], float(CH), None, ALU.is_lt)
            V.tensor_scalar(direction[:, 1:2], part_f[0:CP, :], float(BACK), None, ALU.is_ge)
            V.tensor_scalar(to_chunks[:, :], wide[0:2, 1, 0:CP], part_f[0:2, :], None, ALU.is_equal)
            V.tensor_scalar(turn_back[:, :], free_f[0:CP, 0:CH], part_f[0:CP, :], None, ALU.add)
            step(V.tensor_scalar(to_nodes[:, :], wide[0:CH, 0, :], part_f[0:CH, :], None, ALU.is_equal))
            V.tensor_scalar(turn_back[:, :], turn_back[:, :], float(CP - 1), None, ALU.is_equal)

            hot_edges(1)
            for h in range(2):
                head_alpha(h)
                hot_edges(h + 2)
            head_alpha(2)
            head_alpha(3)
            take_counts()
            attention(0, GROUP, alpha[:, 1, 0:GROUP], ps[:, 4, 0:512])
            head_alpha(4)
            head_alpha(5)
            head_alpha(6)
            dve.wait_ge(bias_ready, 1)
            for k in range(4):
                elu(k)
            head_alpha(7)
            for k in range(4, 8):
                elu(k)
            elu_out(7)
            dve.wait_ge(spread, HEADS + 2)
            V.tensor_tensor(x1[:, :], x_sb[:, :], bias_rows[:, 0, :], ALU.add)
            attention(1, GROUP, alpha[:, 1, GROUP:2 * GROUP], ps[:, 4, 0:512])
            for k in range(8, 16):
                elu(k)
            elu_out(15)

            for j in VECTOR_GRAINS:
                split_low(0, 0, j)

            dve.wait_ge(h2_ready, 1)
            dve.wait_ge(spread, HEADS + 1)
            for j in range(2):
                dot = V.tensor_tensor_reduce(out=xc[:, :], in0=h2_sb[:, :],
                                             in1=att2_rows[:, j, :], scale=1.0, scalar=0.0,
                                             op0=ALU.mult, op1=ALU.add, accum_out=alpha2[:, j, :])
                if j == 0:
                    dot.then_inc(alpha_used, 1)
                    dve.wait_ge(alpha_used, HEADS + 1)
            step(dot)
            e, p = att_e[:, 0, :], att_p[:, 0, :]
            dve.wait_ge(att_scores, 3)
            step(V.tensor_scalar(p, ps[:, 4, 0:P], alpha2[:, 1, :], None, ALU.add))
            step(V.scalar_tensor_tensor(out=e, in0=p, scalar=0.2, in1=p, op0=ALU.mult, op1=ALU.max))
            step(V.tensor_tensor(e, e, mask_bias[:, :], ALU.add))
            step(V.reduce_max(col(MX), e, AX))
            V.tensor_scalar(col(MX), col(MX), -1.0, None, ALU.mult).then_inc(att_shift, 1)
            dve.wait_ge(att_exp, 3)
            V.tensor_tensor_reduce(out=p, in0=p, in1=counts[:, :], scale=1.0, scalar=0.0, op0=ALU.mult,
                                   op1=ALU.add, accum_out=col(SS)).then_inc(att_prob, 1)
            dve.wait_ge(att_prob, 3)
            V.reciprocal(col(RS), col(SS))
            dve.wait_ge(att_turned, 3)
            V.tensor_copy(att_T[:, 0, :], ps[:, 4, P:2 * P]).then_inc(att_ready, 1)
            dve.wait_ge(out2_done, 1)
            dve.wait_ge(att_ready, 3)
            step(V.scalar_tensor_tensor(out=blocks(x1[:, :]), in0=ps[:, 2:4, 0:HB], scalar=col(RS),
                                        in1=blocks(x1[:, :]), op0=ALU.mult, op1=ALU.add, accum_out=col(SUM)))
            normalise(x1, 2)
            take_xT(2)
            dve.wait_ge(rstd_ready, 2)
            V.tensor_scalar(xn[:, :], xc[:, :], col(RSTD), None, ALU.mult).then_inc(xn_ready, 1)

            dve.wait_ge(logit_done, 1)
            step(V.scalar_tensor_tensor(out=logit[:, :], in0=ps[:, 7, 0:EXPERTS + 1], scalar=col(RSTD),
                                        in1=gate_b[:, :], op0=ALU.mult, op1=ALU.add))
            step(V.reduce_max(col(SMAX), logit[:, 0:EXPERTS], AX))
            step(V.scalar_tensor_tensor(out=best8[:, :], in0=logit[:, 0:EXPERTS], scalar=col(SMAX), in1=e8[:, :],
                                        op0=ALU.is_equal, op1=ALU.mult))
            step(V.tensor_reduce(col(IDX), best8[:, :], AX, ALU.min))
            V.tensor_scalar(hot, e8[:, :], col(IDX), None, ALU.is_equal).then_inc(onehot_ready, 1)
            V.tensor_scalar(prob[:, :], logit[:, 0:EXPERTS], col(SMAX), None, ALU.subtract).then_inc(gate_in, 1)

            dve.wait_ge(rank_done, 1)
            step(V.scalar_tensor_tensor(out=rank[:, 0:EXPERTS], in0=ps[:, 7, 16:24], scalar=1.0, in1=hot,
                                        op0=ALU.add, op1=ALU.mult))
            V.tensor_scalar(over[:, :], ps[:, 7, 24:32], float(CAP), None, ALU.is_gt)
            V.tensor_scalar(place_now[:, :], slot_no[:, :, :].rearrange("p a j -> p (a j)"), rank[:, 0:1],
                            None, ALU.is_equal).then_inc(place_ready, 1)
            dve.wait_ge(place_ready, 1)
            V.reduce_sum(route_f[:, 0:1], over[:, :], AX)
            step(V.tensor_tensor_reduce(out=best8[:, :], in0=over[:, :], in1=free_f[:, 0:EXPERTS], scale=1.0,
                                        scalar=0.0, op0=ALU.mult, op1=ALU.add, accum_out=route_f[:, 1:2]))
            step(V.tensor_scalar(route_f[:, 0:1], route_f[:, 0:1], float(ROUNDS), None, ALU.add))
            V.tensor_copy(route[:, :], route_f[:, :]).then_inc(route_ready, 1)
            dve.wait_ge(gate_exp, 1)
            V.reduce_sum(col(SS), prob[:, :], AX)
            step(V.tensor_scalar(col(SCORE), col(SCORE), 1.0, None, ALU.add))
            V.reciprocal(col(SCORE), col(SCORE)).then_inc(score_ready, 1)
            V.reciprocal(col(TOPP), col(SS))

            def take_gathered(r_done, bank):
                dve.wait_ge(gather_done, r_done)
                view = ps[:, bank, 0:HB].rearrange("p (k j) -> p k j", k=KT)
                V.tensor_copy(gathered[:, :, 0:CAP], view).then_inc(gathered_ready, 1)
                dve.wait_ge(gathered_ready, 2 * r_done - 1)
                V.tensor_tensor(gathered[:, :, CAP:P], view, gathered[:, :, 0:CAP].bitcast(f32),
                                ALU.subtract).then_inc(gathered_ready, 1)

            take_gathered(1, 5)

            dve.wait_ge(score_turned, 1)
            step(V.tensor_copy(score_row[:, 0, :], ps[0:1, 4, 0:P]))
            step(V.max(top16[:, 0:8], score_row[:, 0, :]))
            step(V.match_replace(out=score_row[:, 1, :], in_to_replace=top16[:, 0:8],
                                 in_values=score_row[:, 0, :], imm_value=-1.0))
            V.max(top16[:, 8:16], score_row[:, 1, :]).then_inc(thr_ready, 1)

            def take_threshold():
                dve.wait_ge(thr_done, 1)
                V.tensor_scalar(keep[:, :], col(SCORE), ps[:, 4, P:P + 1], None, ALU.is_ge).then_inc(keep_ready, 1)

            def prepare_end():
                dve.wait_ge(small_in, 16 * SMALL)
                dve.wait_ge(keep_ready, 1)
                V.tensor_scalar(minus_bk[:, :], bk_c[:, :], -1.0, None, ALU.mult).then_inc(minus_ready, 1)
                V.tensor_scalar(own_step[:, :], step_mask[:, :], keep[:, :], None, ALU.mult)
                step(V.tensor_tensor_reduce(out=best8[:, :], in0=over[:, :], in1=rank[:, 0:EXPERTS], scale=1.0,
                                            scalar=0.0, op0=ALU.mult, op1=ALU.add, accum_out=rank[:, 8:9]))
                step(V.tensor_scalar(rank[:, 8:9], rank[:, 8:9], -float(CAP), None, ALU.add))
                step(V.tensor_tensor(b1_over[:, :, :], b1_T[:, 0:EXPERTS, :],
                                     over[:, :].unsqueeze(2).to_broadcast([P, EXPERTS, QU * KT]), ALU.mult))
                step(V.reduce_sum(b1_T[:, EXPERTS, :], b1_over[:, :, :].rearrange("p e j -> p j e"), AX))

            def add_ffn(n):
                dve.wait_ge(scattered, n)
                dve.wait_ge(ffn_added, n)
                V.tensor_tensor(blocks(ffn[:, :]), ps[:, 4:6, 0:HB], blocks(ffn[:, :]),
                                ALU.add).then_inc(ffn_added, 1)

            def round_(r, first=False):
                def add_bias(q):
                    dve.wait_ge(turned, QU * r + q + 1)
                    V.tensor_tensor(biased[:, :, :], ps[:, 4, 0:HB].rearrange("p (k j) -> p k j", k=KT),
                                    b1_T[:, bass.ds(r, 1), q * KT:(q + 1) * KT].rearrange("p o k -> p (o k)")
                                    .unsqueeze(2).to_broadcast([P, KT, CAP]),
                                    ALU.add).then_inc(biased_ready, 1)

                def split_hidden(q):
                    dve.wait_ge(gelu_done, QU * r + q + 1)
                    V.tensor_copy(hidden[:, q % 2, :, 0:CAP], active[:, :, :]).then_inc(hidden_ready, 1)
                    dve.wait_ge(hidden_ready, 2 * (QU * r + q) + 1)
                    V.tensor_tensor(hidden[:, q % 2, :, CAP:P], active[:, :, :],
                                    hidden[:, q % 2, :, 0:CAP].bitcast(f32), ALU.subtract).then_inc(hidden_ready, 1)

                g0, g1, g3 = VECTOR_GRAINS
                for pos in range(2 * QU):
                    if first and pos == 0:
                        continue
                    split_low(r, pos, g0)
                    if first and pos == 1:
                        take_threshold()
                    if pos >= 2 and UNITS[pos - 2][0] == "up":
                        split_hidden(UNITS[pos - 2][1])
                    split_low(r, pos, g1)
                    split_low(r, pos, g3)
                    if pos == (1 if first else 0):
                        add_ffn(r + 1)
                    if pos >= 1 and UNITS[pos - 1][0] == "up":
                        add_bias(UNITS[pos - 1][1])
                    if pos == 3:
                        dve.wait_ge(place_turned, r + 1)
                        V.tensor_scalar(place_now[:, :], slot_no[:, :, :].rearrange("p a j -> p (a j)"),
                                        rank[:, bass.ds(r + 1, 1)], None, ALU.is_equal).then_inc(place_ready, 1)
                    if first and pos == 5:
                        prepare_end()
                    if pos == 2 * QU - 1:
                        take_gathered(r + 2, 5)

            V.memset(ffn[:, :], 0.0).then_inc(ffn_added, 1)
            round_(0, first=True)
            dve.wait_ge(route_ready, 1)
            rounds = dve.value_load(route[0:1, 0:1], min_val=ROUNDS, max_val=ROUNDS + 1)
            with dve.Fori(1, rounds) as r:
                round_(r)

            dve.wait_ge(spread, HEADS + 4)
            dve.wait_ge(ffn_added, rounds + 1)
            V.tensor_tensor_reduce(out=xc[:, :], in0=ffn[:, :], in1=wv_rows[:, :], scale=1.0, scalar=0.0,
                                   op0=ALU.mult, op1=ALU.add, accum_out=col(VSUM))
            dve.wait_ge(small_in, 16 * SMALL)
            step(V.scalar_tensor_tensor(out=x1[:, :], in0=bias_rows[:, 1, :], scalar=bk_c[:, :], in1=x1[:, :],
                                        op0=ALU.mult, op1=ALU.add))
            step(V.scalar_tensor_tensor(out=x1[:, :], in0=ffn[:, :], scalar=col(TOPP), in1=x1[:, :], op0=ALU.mult,
                                        op1=ALU.add))
            dve.wait_ge(scattered, rounds + 1)
            V.tensor_tensor_reduce(out=blocks(xc[:, :]), in0=ps[:, 4:6, 0:HB], in1=blocks(wv_rows[:, :]), scale=1.0,
                                   scalar=0.0, op0=ALU.mult, op1=ALU.add, accum_out=col(VCOL)).then_inc(last_dot, 1)
            dve.wait_ge(last_dot, 1)
            step(V.tensor_tensor(col(VCOL), col(VCOL), col(VSUM), ALU.add))
            step(V.scalar_tensor_tensor(out=col(VCOL), in0=col(VCOL), scalar=col(TOPP), in1=bv_c[:, :], op0=ALU.mult,
                                        op1=ALU.add))
            step(V.tensor_scalar(col(VCOL), col(VCOL), VMAX, -VMAX, ALU.min, ALU.max))
            V.tensor_scalar(v_steps[:, :], step_mask[:, :], col(VCOL), None, ALU.mult).then_inc(v_ready, 1)

            dve.wait_ge(cf_init, 3)
            dve.wait_ge(v_turned, 1)
            step(V.tensor_copy(cf_v[:, :], ps[0:CP, 7, 0:CL]))
            V.tensor_copy(cf_d[:, :, 0], cf_v[0:CH, :])
            for i in range(CL):
                n = 4 * (CL + 1 - i)
                step(V.tensor_tensor(cf_t[:, 0:n], cf_w[:, i + 1, 4:4 + n], cf_w[:, i, 0:n], ALU.subtract))
                step(V.scalar_tensor_tensor(out=cf_w[:, i + 2, 0:n], in0=cf_w[:, i + 1, 0:n],
                                            scalar=cf_v[:, i:i + 1], in1=cf_t[:, 0:n], op0=ALU.mult, op1=ALU.add))
            V.tensor_tensor(cf_m[:, :, :].rearrange("p c (a b) -> p c a b", a=2),
                            cf_w[:, CL:CL + 2, 0:8].unsqueeze(1).to_broadcast([CP, CH, 2, 8]),
                            own_chunk[:, :].unsqueeze(2).unsqueeze(3).to_broadcast([CP, CH, 2, 8]),
                            ALU.mult).then_inc(cf_ready, 1)
            dve.wait_ge(cf_moved, 1)
            step(V.tensor_copy(cf_mm[:, :, :], ps[0:2, 7, 0:16 * CH].rearrange("p (c m) -> p c m", c=CH)))
            for c in range(CH - 1):
                step(V.tensor_tensor(cf_x[:, :, :], cf_mm[:, c, :].rearrange("p (a b) -> p a b", a=4),
                                     cf_s[:, c, :].unsqueeze(1).to_broadcast([2, 4, 4]), ALU.mult))
                step(V.reduce_sum(cf_s[:, c + 1, :], cf_x[:, :, :], AX))
            step(V.tensor_reduce(cf_n[:, :], cf_s[:, :, :], AX, ALU.max, apply_absolute_value=True))
            step(V.reciprocal(cf_n[:, :], cf_n[:, :]))
            V.tensor_tensor(cf_s[:, :, :], cf_s[:, :, :], cf_n[:, :].unsqueeze(2).to_broadcast([2, CH, 4]),
                            ALU.mult).then_inc(cf_ready, 1)
            dve.wait_ge(cf_moved, 2)
            step(V.tensor_tensor(cf_p[:, :, :], ps[0:CP, 7, 0:4 * CH].rearrange("p (c m) -> p c m", c=CH),
                                 own_chunk[:, :].unsqueeze(2).to_broadcast([CP, CH, 4]), ALU.mult))
            step(V.reduce_sum(cf_b[:, :], cf_p[:, :, :].rearrange("p c m -> p m c"), AX))
            step(V.tensor_tensor(cf_y[:, :, :, :], cf_w[:, 1:CL + 2, 0:8].rearrange("p s (a b) -> p s a b", a=2),
                                 cf_b[:, :].unsqueeze(1).unsqueeze(1).to_broadcast([CP, CL + 1, 2, 4]), ALU.mult))
            step(V.reduce_sum(cf_th[:, :, :], cf_y[:, :, :, :], AX))
            tx, ty = cf_th[:, 1:CL + 1, :], cf_th[:, 0:CL, :]
            V.tensor_tensor(cf_q[:, 0, :, :], ty, ty, ALU.mult)
            V.tensor_tensor(cf_q[:, 1, :, :], tx, ty, ALU.mult)
            step(V.tensor_tensor(cf_q[:, 2, :, :], tx[:, :, ::-1], ty, ALU.mult))
            V.reduce_sum(cf_r[:, :], cf_q[:, 0, :, :], AX)
            V.reduce_sum(cf_a[:, :, 0], cf_q[:, 1, :, :], AX)
            step(V.tensor_tensor(cf_a[:, :, 1], cf_q[:, 2, :, 0], cf_q[:, 2, :, 1], ALU.subtract))
            step(V.reciprocal(cf_r[:, :], cf_r[:, :]))
            V.tensor_tensor(cf_a[:, :, :], cf_a[:, :, :], cf_r[:, :].unsqueeze(2).to_broadcast([CP, CL, 2]),
                            ALU.mult).then_inc(cf_ready, 1)
            dve.wait_ge(cf_moved, 3)
            step(V.tensor_tensor(cf_c[:, :, :], ps[0:CH, 7, 0:2 * CL].rearrange("p (j c) -> p j c", j=CL),
                                 cf_d[:, :, :], ALU.subtract))
            step(V.tensor_tensor(cf_g[:, :, :], cf_c[:, :, :], cf_c[:, :, :], ALU.mult))
            step(V.reduce_sum(cf_e[:, :], cf_g[:, :, :], AX))
            step(V.reciprocal(cf_e[:, :], cf_e[:, :]))
            V.tensor_tensor(cf_g[:, :, :], cf_c[:, :, :], cf_e[:, :].unsqueeze(2).to_broadcast([CH, CL, 2]),
                            ALU.mult).then_inc(cf_ready, 1)
            dve.wait_ge(cf_moved, 4)
            step(V.tensor_tensor(cf_f[:, :, :], ps[:, 7, 0:2 * CL].rearrange("p (j c) -> p j c", j=CL),
                                 own_step[:, :].unsqueeze(2).to_broadcast([P, CL, 2]), ALU.mult))
            step(V.reduce_sum(feats[:, :], cf_f[:, :, :].rearrange("p j c -> p c j"), AX))
            step(V.tensor_scalar(feats[:, :], feats[:, :], FCLAMP, -FCLAMP, ALU.min, ALU.max))
            dve.wait_ge(x1_done, 1)
            dve.wait_ge(wo_scaled, 1)
            step(V.scalar_tensor_tensor(out=x1[:, :], in0=wo_rows[:, 0, :], scalar=feats[:, 0:1], in1=x1[:, :],
                                        op0=ALU.mult, op1=ALU.add))
            V.scalar_tensor_tensor(out=xc[:, :], in0=wo_rows[:, 1, :], scalar=feats[:, 1:2], in1=x1[:, :],
                                   op0=ALU.mult, op1=ALU.add).then_inc(final_ready, 1)

        @block.tensor
        def _(pe):
            def turn_x(i):
                pe.wait_ge(xc_ready, i)
                for half in range(2):
                    for k in range(3):
                        c = (3 * half + k) * P
                        last = T.transpose(ps[:, 5 + half, k * P:(k + 1) * P], xc[:, c:c + P], ident[:, :])
                    last.then_inc(xT_done, 1)

            pe.wait_ge(consts, 1)
            turn_x(1)
            def raw_ready(n):
                pe.wait_ge(raw_in[n % SLOTS], 16 * (n // SLOTS + 1))

            def head_up(h, halves=(0, 1)):
                if h >= 2 and 0 in halves:
                    pe.wait_ge(h_ready, h - 1)
                for half in halves:
                    n = 2 * h + half
                    raw_ready(n)
                    if n == 1:
                        pe.wait_ge(xT_second, 1)
                    for k in range(3):
                        for b in range(2):
                            last = T.matmul(ps[:, 2 * (h % 2) + b, 0:HB], xT[:, 3 * half + k, :],
                                            raw[:, n % SLOTS, k, b * HB:(b + 1) * HB],
                                            start=(n % 2 == 0 and k == 0), stop=(n % 2 == 1 and k == 2))
                    last.then_inc(used, 2)

            def scores(a, n, source):
                if a:
                    pe.wait_ge(att_ready, a)
                for h in range(n):
                    last = T.matmul(ps[:, 4, h * P:(h + 1) * P], source(h).to_broadcast([P, P]), ident[:, :],
                                    start=True, stop=True)
                last.then_inc(att_scores, 1)

            def turn_weights(a, n, first):
                pe.wait_ge(att_prob, a + 1)
                for h in range(n):
                    last = T.transpose(ps[:, 4, first + h * P:first + (h + 1) * P], att_p[:, h, :], ident[:, :])
                last.then_inc(att_turned, 1)

            def aggregate(k):
                h = k // 2
                pe.wait_ge(att_ready, h // GROUP + 1)
                if k >= 2:
                    pe.wait_ge(elu_in, k - 1)
                for j in range(3):
                    c = (3 * (k % 2) + j) * P
                    last = T.matmul(ps[:, 5 + k % 2, j * P:(j + 1) * P], h_sb[:, h, c:c + P],
                                    att_T[:, h % GROUP, :], start=True, stop=True)
                last.then_inc(agg_done, 1)

            def head_down(h, halves=(0, 1)):
                for half in halves:
                    pe.wait_ge(elu_ready, 2 * h + half + 1)
                    n = 2 * (HEADS + h) + half
                    raw_ready(n)
                    for k in range(3):
                        for b in range(2):
                            last = T.matmul(ps[:, b, 0:HB], eluT[:, KT * h + 3 * half + k, :],
                                            raw[:, n % SLOTS, k, b * HB:(b + 1) * HB],
                                            start=(h == 0 and half == 0 and k == 0),
                                            stop=(h == HEADS - 1 and half == 1 and k == 2))
                    last.then_inc(used, 2)

            def turn_biases():
                pe.wait_ge(small_in, 16 * SMALL)
                T.transpose(ps[:, 4, 0:HEADS * KT], gb1_rows[:, :], ident[0:HEADS * KT, 0:HEADS * KT])
                for g in range(2):
                    last = T.transpose(ps[:, 4, 192 + 96 * g:288 + 96 * g], b1_rows[:, g, :], ident[0:96, 0:96])
                last.then_inc(bias_done, 1)

            def count_edges(c):
                pe.wait_ge(hot_ready, c + 1)
                for j in range(8):
                    last = T.matmul(ps[:, 7, 0:P], dst_hot[:, j, :], src_hot[:, j, :],
                                    start=(c == 0 and j == 0), stop=False)
                if c == 3:
                    last = T.matmul(ps[:, 7, 0:P], ident_b[:, :], ident_b[:, :], start=False, stop=True)
                last.then_inc(hot_used, 1)

            pe.wait_ge(xT_first, 1)
            for h in range(4):
                head_up(h)
                count_edges(h)
            head_up(4, [0])
            turn_biases()
            head_up(4, [1])
            head_up(5, [0])
            pe.wait_ge(bias_ready, 1)
            pe.wait_ge(alpha_used, GROUP)
            scores(0, GROUP, lambda h: alpha[:, 0, h:h + 1])
            head_up(5, [1])
            head_up(6, [0])
            turn_weights(0, GROUP, 0)
            head_up(6, [1])
            aggregate(0)
            aggregate(1)
            head_up(7, [0])
            aggregate(2)
            aggregate(3)
            head_up(7, [1])
            aggregate(4)
            aggregate(5)
            pe.wait_ge(h_ready, HEADS - 1)
            head_down(0, [0])
            aggregate(6)
            aggregate(7)
            head_down(0, [1])
            pe.wait_ge(alpha_used, HEADS)
            scores(1, GROUP, lambda h: alpha[:, 0, GROUP + h:GROUP + h + 1])
            head_down(1)
            head_down(2, [0])
            turn_weights(1, GROUP, 0)
            head_down(2, [1])
            aggregate(8)
            aggregate(9)
            head_down(3, [0])
            aggregate(10)
            aggregate(11)
            head_down(3, [1])
            aggregate(12)
            aggregate(13)
            head_down(4, [0])
            aggregate(14)
            aggregate(15)
            head_down(4, [1])
            for h in range(5, HEADS):
                head_down(h)

            pe.wait_ge(alpha_used, HEADS + 1)
            scores(2, 1, lambda h: alpha2[:, 0, :])
            turn_weights(2, 1, P)
            pe.wait_ge(att_ready, 3)
            pe.wait_ge(h2_ready, 1)
            for b in range(2):
                last = T.matmul(ps[:, 2 + b, 0:HB], att_T[:, 0, :], h2_sb[:, b * HB:(b + 1) * HB],
                                start=True, stop=True)
            last.then_inc(out2_done, 1)
            turn_x(2)
            pe.wait_ge(xT_first, 2)
            for k in range(KT):
                if k == 3:
                    pe.wait_ge(xT_second, 2)
                last = T.matmul(ps[:, 7, 0:EXPERTS + 1], xT[:, k, :], gate_w[:, k, :], start=(k == 0),
                                stop=(k == KT - 1))
            last.then_inc(logit_done, 1)

            pe.wait_ge(onehot_ready, 1)
            T.matmul(ps[:, 7, 16:24], later[:, :], hot, start=True, stop=True)
            T.matmul(ps[:, 7, 24:32], ones[:, :], hot, start=True, stop=True)
            T.transpose(ps[:, 7, 128:256], hot_wide[:, :], ident[:, :]).then_inc(rank_done, 1)

            def gather(bank):
                for k in range(KT):
                    last = T.matmul(ps[:, bank, k * CAP:(k + 1) * CAP], xn[:, k * P:(k + 1) * P],
                                    place_now[:, 0:CAP], start=True, stop=True)
                last.then_inc(gather_done, 1)

            pe.wait_ge(xn_ready, 1)
            pe.wait_ge(place_ready, 1)
            gather(5)
            pe.wait_ge(score_ready, 1)
            T.matmul(ps[0:1, 4, 0:P], col(SCORE), ident[:, :], start=True, stop=True).then_inc(score_turned, 1)

            def threshold():
                pe.wait_ge(thr_ready, 1)
                T.matmul(ps[:, 4, P:P + 1], ones[0:1, :], top16[0:1, KEEP - 1:KEEP], start=True,
                         stop=True).then_inc(thr_done, 1)

            def first_y():
                pe.wait_ge(hot_T_ready, 1)
                for b in range(2):
                    last = T.matmul(ps[:, 6 + b, 0:HB], ident[0:EXPERTS, :], b2_sb[:, b * HB:(b + 1) * HB],
                                    start=True, stop=True)
                last.then_inc(b2_ready, 1)

            def round_(r, first=False):
                unit0 = 2 * QU * r

                def stream(pos, stationary, bank, first, last_, grains=range(GRAINS)):
                    for j in grains:
                        half, b = j // 2, j % 2
                        if j == POOL_GRAIN:
                            pe.wait_ge(lo_pool, unit0 + pos + 1)
                        else:
                            pe.wait_ge(lo_ready, 3 * (unit0 + pos) + VECTOR_GRAINS.index(j) + 1)
                        for k in range(3):
                            for part in (whi, wlo):
                                last = T.matmul(ps[:, bank + b, 0:HB], stationary[:, 3 * half + k, :],
                                                part[:, j, k, :],
                                                start=(first and half == 0 and k == 0 and part is whi),
                                                stop=(last_ and half == 1 and k == 2 and part is wlo))
                        last.then_inc(used, 1)

                def turn_upper(q):
                    pe.wait_ge(upper_ready, QU * r + q + 1)
                    for k in range(KT):
                        last = T.matmul(ps[:, 4, k * CAP:(k + 1) * CAP], upper[:, q % 2, k * P:(k + 1) * P],
                                        fold[:, :], start=True, stop=True)
                    last.then_inc(turned, 1)

                def up(q, grains):
                    stream(UNITS.index(("up", q)), gathered, 2 * (q % 2), True, True, grains)

                def down(q, grains):
                    if 0 in grains:
                        pe.wait_ge(hidden_ready, 2 * (QU * r + q + 1))
                    stream(UNITS.index(("down", q)), hidden[:, q % 2, :, :], 6, q == 0, q == QU - 1, grains)

                pe.wait_ge(gathered_ready, 2 * r + 2)
                if first:
                    up(0, range(GRAINS))
                    threshold()
                    first_y()
                    up(1, range(2))
                    pe.wait_ge(keep_ready, 1)
                    scatter(0)
                    up(1, range(2, 3))
                else:
                    up(0, range(2))
                    scatter(r)
                    up(0, range(2, GRAINS))
                    up(1, range(1))
                pe.wait_ge(ffn_added, r + 2)
                T.transpose(ps[:, 5, HB:512], place_now[:, :], ident[:, :]).then_inc(place_turned, 1)
                turn_upper(0)
                up(1, range(3 if first else 1, GRAINS))
                down(0, range(1))
                turn_upper(1)
                down(0, range(1, GRAINS))
                up(2, range(GRAINS))
                down(1, range(1))
                turn_upper(2)
                down(1, range(1, GRAINS))
                up(3, range(GRAINS))
                pe.wait_ge(place_ready, r + 2)
                pe.wait_ge(place_T_ready, r + 1)
                gather(5)
                down(2, range(1))
                turn_upper(3)
                down(2, range(1, GRAINS))
                down(3, range(GRAINS))

            def scatter(n):
                pe.wait_ge(y_ready, n + 1)
                for b in range(2):
                    last = T.matmul(ps[:, 4 + b, 0:HB], place_T[:, :], y_sb[:, b * HB:(b + 1) * HB],
                                    start=True, stop=True)
                last.then_inc(scattered, 1)

            round_(0, first=True)
            pe.wait_ge(route_ready, 1)
            rounds = pe.value_load(route[0:1, 0:1], min_val=ROUNDS, max_val=ROUNDS + 1)
            with pe.Fori(1, rounds) as r:
                round_(r)
            pe.wait_ge(gathered_ready, 2 * rounds + 2)
            scatter(rounds)

            pe.wait_ge(v_ready, 1)
            T.matmul(ps[0:CP, 7, 0:CL], to_forward[:, :], v_steps[:, :], start=True, stop=False)
            T.matmul(ps[0:CP, 7, 0:CL], to_back[:, :], v_steps[:, ::-1], start=False, stop=True).then_inc(v_turned, 1)
            pe.wait_ge(cf_ready, 1)
            T.matmul(ps[0:2, 7, 0:16 * CH], direction[:, :], cf_m[:, :, :].rearrange("p c m -> p (c m)"),
                     start=True, stop=True).then_inc(cf_moved, 1)
            pe.wait_ge(cf_ready, 2)
            T.matmul(ps[0:CP, 7, 0:4 * CH], to_chunks[:, :], cf_s[:, :, :].rearrange("p c m -> p (c m)"),
                     start=True, stop=True).then_inc(cf_moved, 1)
            pe.wait_ge(cf_ready, 3)
            T.matmul(ps[0:CH, 7, 0:2 * CL], ident[0:CP, 0:CH], cf_a[:, :, :].rearrange("p j c -> p (j c)"),
                     start=True, stop=False)
            T.matmul(ps[0:CH, 7, 0:2 * CL].rearrange("p (j c) -> p j c", j=CL), turn_back[:, :],
                     cf_a[:, ::-1, :], start=False, stop=True).then_inc(cf_moved, 1)
            pe.wait_ge(cf_ready, 4)
            T.matmul(ps[:, 7, 0:2 * CL], to_nodes[:, :], cf_g[:, :, :].rearrange("p j c -> p (j c)"),
                     start=True, stop=True).then_inc(cf_moved, 1)


_SHAPES = {
    "x": (N, D), "src": (EDGES,), "dst": (EDGES,), "L0_gnn_W1": (D, HEADS * D), "L0_gnn_a_src1": (HEADS, D),
    "L0_gnn_a_dst1": (HEADS, D), "L0_gnn_b1": (HEADS * D,), "L0_gnn_W2": (HEADS * D, D),
    "L0_gnn_a_src2": (1, D), "L0_gnn_a_dst2": (1, D), "L0_gnn_b2": (1, D), "L0_ffn_Wg": (D, EXPERTS),
    "L0_ffn_bg": (1, EXPERTS), "L0_ffn_W1": (EXPERTS, D, HID), "L0_ffn_b1": (EXPERTS, HID),
    "L0_ffn_W2": (EXPERTS, HID, D), "L0_ffn_b2": (EXPERTS, D), "L0_ffn_Wv": (1, D), "L0_ffn_bv": (1, 1),
    "L0_ffn_Wm": (D, 1), "L0_ffn_bm": (1, 1), "L0_ffn_Wo": (2, D), "L0_ffn_bo": (1, D),
    "L0_ffn_bk_scale": (1, 1),
}


def kernel(**inputs):
    import numpy as _np
    import concourse.bacc as _bacc
    from concourse import mybir as _mybir
    from concourse.bass_utils import run_bass_kernel_spmd as _run

    nc = _bacc.Bacc("TRN2", target_bir_lowering=False, num_devices=1)
    arrays, args = {}, []
    for name, shape in _SHAPES.items():
        a = _np.ascontiguousarray(inputs[name]).reshape(shape)
        arrays[f"in_{name}"] = a
        args.append(nc.dram_tensor(f"in_{name}", shape, _mybir.dt.from_np(a.dtype), kind="ExternalInput").ap())
    out = nc.dram_tensor("out", (N, D), _mybir.dt.float32, kind="ExternalOutput").ap()
    gnn_moe_kernel(nc, *args, out)
    r = _run(nc, [arrays], core_ids=[0])
    return r.results[0]["out"]
```

```python
import concourse.bass as bass
from concourse import mybir
from contextlib import ExitStack

P = 128
N = 128
D = 768
HEADS = 8
EDGES = 4096
EXPERTS = 8
HID = 3072
KT = D // P
HB = D // 2
QU = HID // D
CAP = 64
ROUNDS = EXPERTS
SLOTS = 8
GRAINS = 4
POOL_GRAIN = 2
VECTOR_GRAINS = (0, 1, 3)
KEEP = 12
EPS = 1e-5
VMAX = 3.0
FCLAMP = 10.0
NEG = -1e30
FAR = 1e18
CL = 8
CH = N // CL
BACK = 32
CP = BACK + CH
CHUNK_SCALE = 2.3 ** -CL
GROUP = 4
SMALL = 10
GNN_HALVES = 2 * 2 * HEADS
ROUND_HALVES = 2 * 2 * QU
EARLY = 3
ATONCE = 6
WARM = (6, 4, 9, 13, 2, 9, 4, 6, 4, 4)
UNITS = [("up", 0), ("up", 1), ("down", 0), ("up", 2), ("down", 1), ("up", 3), ("down", 2), ("down", 3)]


def gnn_moe_kernel(nc, x, src, dst, gw1, gas1, gad1, gb1, gw2, gas2, gad2, gb2,
                   wg, bg, w1, b1, w2, b2, wv, bv, wm, bm, wo, bo, bks, out):
    f32, f32r, bf16, i32 = mybir.dt.float32, mybir.dt.float32r, mybir.dt.bfloat16, mybir.dt.int32
    ALU, ACT = mybir.AluOpType, mybir.ActivationFunctionType
    AX = mybir.AxisListType.X
    V, S, G, T = nc.vector, nc.scalar, nc.gpsimd, nc.tensor

    ctx = ExitStack()
    with ctx:
        ctx.enter_context(nc.allow_non_contiguous_dma(reason="the gate's columns, 768 words each"))

        def sem(name):
            return ctx.enter_context(nc.semaphore(name))

        base = (nc.sbuf_base + 31) // 32 * 32
        ctx.enter_context(nc.sbuf_tensor("slab", [P, (nc.sbuf_usable_end - base - 64) // 4], f32))
        top = [base]

        def size(shape, dt):
            n = 2 if dt == bf16 else 4
            for s in shape[1:]:
                n *= s
            return (n + 31) // 32 * 32

        def place(name, shape, dt=f32):
            t = nc.alloc_sbuf_tensor_at(name, shape, dt, offset=top[0])
            top[0] += size(shape, dt)
            return t

        def region(tenants):
            first, end, got = top[0], top[0], []
            for tensors in tenants:
                top[0] = first
                got += [place(*t) for t in tensors]
                end = max(end, top[0])
            top[0] = end
            return got

        raw = place("raw", [P, SLOTS, 3, D])
        h_sb, whi, wlo = region([
            [("h_sb", [P, HEADS, D])],
            [("whi", [P, GRAINS, 3, HB], f32r), ("wlo", [P, GRAINS, 3, HB], f32r)]])
        (src_hot, dst_hot, early_rows, eluT, gathered, upper, biased, active, hidden,
         y_sb, ffn, place_now, place_T) = region([
             [("src_hot", [P, 8, P], bf16), ("dst_hot", [P, 8, P], bf16), ("early_rows", [1, 3, 2, D])],
             [("eluT", [P, HEADS * KT, P])],
             [("gathered", [P, KT, P], f32r), ("upper", [P, 2, D]), ("biased", [P, KT, CAP]),
              ("active", [P, KT, CAP]), ("hidden", [P, 2, KT, P], f32r), ("y_sb", [P, D]),
              ("ffn", [P, D]), ("place_now", [P, P]), ("place_T", [P, P])]])
        (rows, cf_w, cf_v, cf_t, cf_m, cf_mm, cf_s, cf_x, cf_n, cf_p, cf_b, cf_y, cf_th, cf_q, cf_r, cf_a,
         cf_d, cf_c, cf_g, cf_e, cf_f) = region([
             [("rows", [1, 2, D])],
             [("cf_w", [CP, CL + 2, 4 * (CL + 2)]), ("cf_v", [CP, CL]), ("cf_t", [CP, 4 * (CL + 2)]),
              ("cf_m", [CP, CH, 16]), ("cf_mm", [2, CH, 16]), ("cf_s", [2, CH, 4]), ("cf_x", [2, 4, 4]),
              ("cf_n", [2, CH]), ("cf_p", [CP, CH, 4]), ("cf_b", [CP, 4]), ("cf_y", [CP, CL + 1, 2, 4]),
              ("cf_th", [CP, CL + 1, 2]), ("cf_q", [CP, 3, CL, 2]), ("cf_r", [CP, CL]), ("cf_a", [CP, CL, 2]),
              ("cf_d", [CH, CL, 2]), ("cf_c", [CH, CL, 2]), ("cf_g", [CH, CL, 2]), ("cf_e", [CH, CL]),
              ("cf_f", [P, CL, 2])]])
        att_rows, annex0, wo_rows, wv_rows = region([
            [("att_rows", [P, 2, 2, D])],
            [("annex0", [P, 3, D])],
            [("wo_rows", [P, 2, D]), ("wv_rows", [P, 2, D])]])
        att2_rows, gb2_rows, annex1 = region([
            [("att2_rows", [P, 2, D]), ("gb2_rows", [P, 2, D])],
            [("annex1", [P, 3, D])]])
        x_sb = place("x_sb", [P, D])
        x1 = place("x1", [P, D])
        xc = place("xc", [P, D])
        xn = place("xn", [P, D])
        xT = place("xT", [P, KT, P])
        att_e = place("att_e", [P, GROUP, P])
        att_p = place("att_p", [P, GROUP, P])
        att_T = place("att_T", [P, GROUP, P])
        elu_y, elu_e, h2_sb = region([
            [("elu_y", [P, 2, 3, P]), ("elu_e", [P, 2, 3, P])],
            [("h2_sb", [P, D])]])
        counts = place("counts", [P, P])
        mask_bias = place("mask_bias", [P, P])
        free_i = place("free_i", [P, P], i32)
        part_i = place("part_i", [P, 1], i32)
        free_f = place("free_f", [P, P])
        part_f = place("part_f", [P, 1])
        ident = place("ident", [P, P])
        ident_b = place("ident_b", [P, P], bf16)
        later = place("later", [P, P])
        slot_no = place("slot_no", [P, 2, CAP])
        fold = place("fold", [P, CAP])
        ones = place("ones", [P, P])
        edges_i = place("edges_i", [P, 2, EDGES // P], i32)
        edges_f = place("edges_f", [P, 2, EDGES // P])
        gb1_rows = place("gb1_rows", [HEADS * KT, P])
        gb1_T = place("gb1_T", [P, HEADS * KT])
        b1_rows = place("b1_rows", [96, 2, P])
        b1_T = place("b1_T", [P, EXPERTS + 1, QU * KT])
        b1_over = place("b1_over", [P, EXPERTS, QU * KT])
        b2_sb = place("b2_sb", [EXPERTS, D])
        gate_w = place("gate_w", [P, KT, EXPERTS + 1])
        gate_b = place("gate_b", [P, EXPERTS + 1])
        bv_c = place("bv_c", [P, 1])
        bk_c = place("bk_c", [P, 1])
        minus_bk = place("minus_bk", [P, 1])
        half_pow = place("half_pow", [P, 1])
        alpha = place("alpha", [P, 2, HEADS])
        alpha2 = place("alpha2", [P, 2, 1])
        small = place("small", [P, 64])
        e8 = place("e8", [P, EXPERTS])
        logit = place("logit", [P, EXPERTS + 1])
        prob = place("prob", [P, EXPERTS])
        hot_wide = place("hot_wide", [P, P])
        hot = hot_wide[:, 0:EXPERTS]
        best8 = place("best8", [P, EXPERTS])
        rank = place("rank", [P, EXPERTS + 2])
        over = place("over", [P, EXPERTS])
        route_f = place("route_f", [P, 2])
        route = place("route", [P, 2], i32)
        score_row = place("score_row", [1, 2, P])
        top16 = place("top16", [1, 16])
        keep = place("keep", [P, 1])
        feats = place("feats", [P, 2])
        shifted_i = place("shifted_i", [P, 4], i32)
        shifted = place("shifted", [P, 4])
        wide_i = place("wide_i", [P, 2, P], i32)
        wide = place("wide", [P, 2, P])
        to_forward = place("to_forward", [P, CP])
        to_back = place("to_back", [P, CP])
        step_mask = place("step_mask", [P, CL])
        own_step = place("own_step", [P, CL])
        v_steps = place("v_steps", [P, CL])
        own_chunk = place("own_chunk", [CP, CH])
        direction = place("direction", [CP, 2])
        to_chunks = place("to_chunks", [2, CP])
        turn_back = place("turn_back", [CP, CH])
        to_nodes = place("to_nodes", [CH, P])
        assert top[0] <= nc.sbuf_usable_end, (top[0], nc.sbuf_usable_end)

        ps = ctx.enter_context(nc.psum_tensor("ps", [P, 8, 512], f32))

        def col(i, n=1):
            return small[:, i:i + n]

        SUM, MEAN, VAR, RSTD, MX, SS, RS = 0, 1, 2, 3, 4, 12, 20
        TOPP, VSUM, VSLOT, SCORE, VCOL, SMAX, IDX = 28, 29, 30, 31, 32, 33, 34

        raw_in = [sem(f"raw_in{i}") for i in range(SLOTS)]
        annex_in = [sem(f"annex_in{i}") for i in range(2)]
        used = sem("used")
        x_in, edges_in, small_in = sem("x_in"), sem("edges_in"), sem("small_in")
        early_in = sem("early_in")
        row_in = sem("row_in")
        spread = sem("spread")
        iota_done, pool_ones = sem("iota_done"), sem("pool_ones")
        dve_step = sem("dve_step")
        consts = sem("consts")
        var_ready, rstd_ready = sem("var_ready"), sem("rstd_ready")
        xc_ready, xT_done = sem("xc_ready"), sem("xT_done")
        xT_first, xT_second = sem("xT_first"), sem("xT_second")
        xn_ready = sem("xn_ready")
        hot_ready, hot_used = sem("hot_ready"), sem("hot_used")
        bias_done, bias_ready = sem("bias_done"), sem("bias_ready")
        h_ready = sem("h_ready")
        alpha_used = sem("alpha_used")
        att_scores, att_shift, att_exp = sem("att_scores"), sem("att_shift"), sem("att_exp")
        att_prob, att_turned, att_ready = sem("att_prob"), sem("att_turned"), sem("att_ready")
        agg_done, elu_in, elu_exp, elu_ready = sem("agg_done"), sem("elu_in"), sem("elu_exp"), sem("elu_ready")
        h2_ready, out2_done = sem("h2_ready"), sem("out2_done")
        logit_done, gate_in, gate_exp = sem("logit_done"), sem("gate_in"), sem("gate_exp")
        onehot_ready, rank_done, hot_T_ready = sem("onehot_ready"), sem("rank_done"), sem("hot_T_ready")
        b2_ready = sem("b2_ready")
        route_ready = sem("route_ready")
        score_ready, score_turned, thr_ready, thr_done = (sem("score_ready"), sem("score_turned"),
                                                          sem("thr_ready"), sem("thr_done"))
        hi_ready, lo_ready, lo_pool = sem("hi_ready"), sem("lo_ready"), sem("lo_pool")
        upper_ready = sem("upper_ready")
        turned, biased_ready, gelu_done, hidden_ready = (sem("turned"), sem("biased_ready"),
                                                         sem("gelu_done"), sem("hidden_ready"))
        y_ready, scattered, ffn_added = sem("y_ready"), sem("scattered"), sem("ffn_added")
        place_ready, place_turned, place_T_ready = (sem("place_ready"), sem("place_turned"),
                                                    sem("place_T_ready"))
        gather_done, gathered_ready = sem("gather_done"), sem("gathered_ready")
        minus_ready, rows_scaled = sem("minus_ready"), sem("rows_scaled")
        last_dot, last_placed, ffn_scaled, x1_done = sem("last_dot"), sem("last_placed"), sem("ffn_scaled"), sem("x1_done")
        v_ready, v_turned = sem("v_ready"), sem("v_turned")
        cf_init, cf_ready, cf_moved = sem("cf_init"), sem("cf_ready"), sem("cf_moved")
        final_ready, out_done = sem("final_ready"), sem("out_done")

        def used_in(r, pos):
            return GRAINS * (2 * HEADS + 2 * QU * r + pos)

        annex = [annex0, annex1]

        def is_first(r):
            return isinstance(r, int) and r == 0

        def in_annex(i, first):
            return first and SLOTS + 2 <= i < SLOTS + 4

        def ring_slot(i, first):
            return i % SLOTS if first and i < SLOTS + 2 else (i - 2) % SLOTS

        def half_unit(i, first):
            return annex[i - SLOTS - 2][:, :, :] if in_annex(i, first) else raw[:, ring_slot(i, first), :, :]

        def landing(i, first):
            return annex_in[i - SLOTS - 2] if in_annex(i, first) else raw_in[ring_slot(i, first)]

        def landed(r, i, first):
            if in_annex(i, first):
                return 16
            late = 0 if first and i < SLOTS + 2 else 2
            return 16 * (GNN_HALVES // SLOTS + 2 * r + (i - late) // SLOTS + 1)

        def blocks(t):
            return t.rearrange("p (b c) -> p b c", b=2)

        block = ctx.enter_context(nc.Block())

        @block.sync
        def _(sp):
            def gnn_half(n):
                unit, half = n // 2, n % 2
                if unit < HEADS:
                    rows_ = gw1[half * 3 * P:(half + 1) * 3 * P, unit * D:(unit + 1) * D]
                else:
                    at = (unit - HEADS) * D + half * 3 * P
                    rows_ = gw2[at:at + 3 * P, :]
                return rows_.rearrange("(k p) c -> p k c", p=P)

            sp.dma_start(x_sb[:, :], x).then_inc(x_in, 16)
            for n in range(GNN_HALVES):
                if n >= SLOTS:
                    sp.wait_ge(used, 2 * (n - SLOTS + 1))
                sp.dma_start(raw[:, n % SLOTS, :, :], gnn_half(n)).then_inc(raw_in[n % SLOTS], 16)
                if n == 0:
                    for j, vectors in enumerate((gas1, gad1)):
                        sp.dma_start(early_rows[0:1, :, j, :], vectors[0:EARLY, :].unsqueeze(0)).then_inc(early_in, 16)

            def load_round(r, e):
                first = is_first(r)
                for i in range(ROUND_HALVES):
                    kind, q = UNITS[i // 2]
                    half = i % 2
                    if kind == "up":
                        view = w1[e, half * 3 * P:(half + 1) * 3 * P, q * D:(q + 1) * D]
                    else:
                        view = w2[e, q * D + half * 3 * P:q * D + (half + 1) * 3 * P, :]
                    if in_annex(i, first):
                        sp.wait_ge(alpha_used, HEADS + (0 if half == 0 else 2))
                    elif first and i < SLOTS:
                        sp.wait_ge(used, 2 * (GNN_HALVES + i - SLOTS + 1))
                    else:
                        unit = 2 * QU * r + (i - (SLOTS + 2 if beside_annex(r, i) else SLOTS)) // 2
                        if half == 0:
                            sp.wait_ge(lo_ready, 3 * unit + 2)
                        elif isinstance(r, int):
                            sp.wait_ge(lo_ready, 3 * unit + 3)
                            sp.wait_ge(lo_pool, unit + 1)
                        else:
                            sp.wait_ge(used, used_in(0, unit + 1))
                    sp.dma_start(half_unit(i, first),
                                 view.rearrange("(k p) c -> p k c", p=P)).then_inc(landing(i, first), 16)

            def beside_annex(r, i):
                return isinstance(r, int) and SLOTS + 4 <= ROUND_HALVES * r + i < 2 * SLOTS + 4

            load_round(0, 0)
            load_round(1, 1)
            with sp.Fori(2, ROUNDS) as r:
                load_round(r, r)
            sp.wait_ge(route_ready, 1)
            rounds = sp.value_load(route[0:1, 0:1], min_val=ROUNDS, max_val=ROUNDS + 1)
            expert = sp.value_load(route[0:1, 1:2], min_val=0, max_val=EXPERTS - 1)
            with sp.If(rounds > ROUNDS):
                load_round(ROUNDS, expert)
            sp.end_ifs()
            sp.wait_ge(final_ready, 1)
            sp.dma_start(out, xc[:, :]).then_inc(out_done, 16)
            sp.wait_ge(out_done, 16)

        @block.gpsimd
        def _(pool):
            pairs = [(gas1[h:h + 1, :], gad1[h:h + 1, :]) for h in range(HEADS)]
            pairs += [(gas2, gad2), (gb2, gb2), (wo[0:1, :], wo[1:2, :]), (wv, bo)]
            targets = [att2_rows, gb2_rows, wo_rows, wv_rows]

            def split_last(r, pos):
                pool.wait_ge(hi_ready, GRAINS * (2 * QU * r + pos) + POOL_GRAIN + 1)
                G.tensor_tensor(wlo[:, POOL_GRAIN, :, :], half_unit(2 * pos + 1, is_first(r))[:, :, 0:HB],
                                whi[:, POOL_GRAIN, :, :].bitcast(f32), ALU.subtract).then_inc(lo_pool, 1)

            G.iota(free_i[:, :], pattern=[[1, P]], base=0, channel_multiplier=0).then_inc(iota_done, 1)
            G.iota(part_i[:, :], pattern=[[0, 1]], base=0, channel_multiplier=1).then_inc(iota_done, 1)
            G.memset(half_pow[:, :], -0.5).then_inc(pool_ones, 1)
            places = [early_rows[0:1, i, :, :] for i in range(EARLY)]
            places += [rows[0:1, :, :], att2_rows[0:1, :, :], gb2_rows[0:1, :, :], rows[0:1, :, :],
                       early_rows[0:1, EARLY - 1, :, :]] + [rows[0:1, :, :]] * (len(pairs) - HEADS)

            def fetch(i, landed):
                for j in range(2):
                    pool.dma_start(places[i][:, j, :], pairs[i][j]).then_inc(landed, 16)

            for i in range(EARLY, ATONCE):
                fetch(i, row_in)
            pool.wait_ge(var_ready, 1)
            pool.wait_ge(pool_ones, 1)
            G.tensor_tensor(col(RSTD), col(VAR), half_pow[:, :], ALU.pow).then_inc(rstd_ready, 1)
            pool.wait_ge(early_in, 32)

            def spread_pair(i):
                if i >= EARLY:
                    pool.wait_ge(row_in, 32 * (max(i, HEADS - 1 if i >= ATONCE else ATONCE - 1) - EARLY + 1))
                if 2 <= i < HEADS:
                    pool.wait_ge(alpha_used, i - 1)
                target = att_rows[:, i % 2, :, :] if i < HEADS else targets[i - HEADS][:, :, :]
                n = 1 if i == HEADS + 1 else 2
                G.partition_broadcast(target[:, 0:n, :].rearrange("p a c -> p (a c)"),
                                      places[i][:, 0:n, :].rearrange("p a c -> p (a c)")).then_inc(spread, 1)
                following = {EARLY: (ATONCE, ATONCE + 1), ATONCE: (HEADS,)}.get(i, (i + 1,) if i >= HEADS else ())
                for later_pair in following:
                    if later_pair < len(pairs):
                        pool.wait_ge(spread, i + 1)
                        fetch(later_pair, row_in)

            for i in range(HEADS + 2):
                spread_pair(i)
            split_last(0, 0)
            pool.wait_ge(var_ready, 2)
            G.tensor_tensor(col(RSTD), col(VAR), half_pow[:, :], ALU.pow).then_inc(rstd_ready, 1)

            def round_(r, first=0, end=2 * QU):
                for pos in range(first, end):
                    split_last(r, pos)

            round_(0, first=1, end=2 * QU - 1)
            pool.wait_ge(lo_ready, 3 * (2 * QU - 2))
            spread_pair(HEADS + 2)
            round_(0, first=2 * QU - 1)
            spread_pair(HEADS + 3)

            pool.wait_ge(spread, len(pairs))
            G.memset(cf_w[:, 0:2, :], 0.0).then_inc(cf_init, 1)
            G.memset(cf_s[:, 0, :], 0.0).then_inc(cf_init, 1)
            G.memset(cf_d[:, :, 1], -1.0)
            pool.wait_ge(cf_init, 2)
            for at in range(2):
                for row, sign in ((0, 1.0), (1, 1.0), (2, -1.0), (3, -1.0)):
                    first = 4 * row + 2 * at + row % 2
                    G.memset(cf_w[:, at, first::16], sign)
            G.memset(cf_s[:, 0, 0:1], 1.0 / FAR)
            G.memset(cf_s[:, 0, 2:3], 1.0).then_inc(cf_init, 1)

            pool.wait_ge(route_ready, 1)
            rounds = pool.value_load(route[0:1, 0:1], min_val=ROUNDS, max_val=ROUNDS + 1)
            with pool.Fori(1, rounds) as r:
                round_(r)
            pool.wait_ge(rows_scaled, 1)
            G.tensor_tensor(x1[:, :], x1[:, :], wv_rows[:, 1, :], ALU.add).then_inc(x1_done, 1)
            for part, addend in enumerate((y_sb, ffn)):
                pool.wait_ge(ffn_scaled, part + 1)
                pool.wait_ge(x1_done, part + 1)
                G.tensor_tensor(x1[:, :], x1[:, :], addend[:, :], ALU.add).then_inc(x1_done, 1)

        @block.scalar
        def _(act):
            act.dma_start(edges_i[:, 0, :], src.rearrange("(p j) -> p j", p=P)).then_inc(edges_in, 16)
            act.dma_start(edges_i[:, 1, :], dst.rearrange("(p j) -> p j", p=P)).then_inc(edges_in, 16)
            for target, view in (
                    (gb1_rows[:, :], gb1.rearrange("(j p) -> j p", p=P)),
                    (b1_rows[:, 0, :], b1[0:4, :].rearrange("e (j p) -> (e j) p", p=P)),
                    (b1_rows[:, 1, :], b1[4:8, :].rearrange("e (j p) -> (e j) p", p=P)),
                    (b2_sb[:, :], b2),
                    (gate_w[:, :, 0:EXPERTS], wg.rearrange("(k p) e -> p k e", p=P)),
                    (gate_w[:, :, EXPERTS:EXPERTS + 1], wm.rearrange("(k p) e -> p k e", p=P)),
                    (gate_b[:, 0:EXPERTS], bg.to_broadcast([P, EXPERTS])),
                    (gate_b[:, EXPERTS:EXPERTS + 1], bm.to_broadcast([P, 1])),
                    (bv_c[:, :], bv.to_broadcast([P, 1])),
                    (bk_c[:, :], bks.to_broadcast([P, 1]))):
                act.dma_start(target, view).then_inc(small_in, 16)

            def split_high(r, pos, j):
                i, b = 2 * pos + j // 2, j % 2
                first = is_first(r)
                if b == 0:
                    act.wait_ge(landing(i, first), landed(r, i, first))
                S.copy(whi[:, j, :, :], half_unit(i, first)[:, :, b * HB:(b + 1) * HB]).then_inc(hi_ready, 1)

            def take_head(h):
                act.wait_ge(used, GRAINS * (h + 1))
                b = 2 * (h % 2)
                S.activation(blocks(h_sb[:, h, :]), ps[:, b:b + 2, 0:HB], ACT.Identity,
                             scale=col(RSTD)).then_inc(h_ready, 1)

            def exponents(a, n):
                act.wait_ge(att_shift, a + 1)
                S.activation(att_p[:, 0:n, :], att_e[:, 0:n, :], ACT.Exp).then_inc(att_exp, 1)

            def elu_exponent(k):
                act.wait_ge(elu_in, k + 1)
                S.activation(elu_e[:, k % 2, :, :], elu_e[:, k % 2, :, :], ACT.Exp).then_inc(elu_exp, 1)

            act.wait_ge(rstd_ready, 1)
            for h in range(4):
                take_head(h)
            act.wait_ge(bias_done, 1)
            S.copy(gb1_T[:, :], ps[:, 4, 0:HEADS * KT])
            S.copy(b1_T[:, 0:EXPERTS, :].rearrange("p (g e) j -> p g (e j)", g=2),
                   ps[:, 4, 192:384].rearrange("p (g j) -> p g j", g=2)).then_inc(bias_ready, 1)
            take_head(4)
            exponents(0, GROUP)
            take_head(5)
            take_head(6)
            for k in range(4):
                elu_exponent(k)
            take_head(7)
            for k in range(4, 8):
                elu_exponent(k)
            exponents(1, GROUP)
            for k in range(8, 16):
                elu_exponent(k)

            act.wait_ge(alpha_used, HEADS)
            act.wait_ge(agg_done, 2 * HEADS)
            for j in range(GRAINS):
                split_high(0, 0, j)

            act.wait_ge(used, GRAINS * 2 * HEADS)
            S.copy(blocks(h2_sb[:, :]), ps[:, 0:2, 0:HB]).then_inc(h2_ready, 1)
            act.wait_ge(att_shift, 3)
            S.activation(att_p[:, 0, :], att_e[:, 0, :], ACT.Exp, bias=col(MX)).then_inc(att_exp, 1)
            act.wait_ge(xT_done, 4)
            S.copy(xT[:, 3:KT, :].rearrange("p k t -> p (k t)"), ps[:, 6, 0:HB]).then_inc(xT_second, 1)
            act.wait_ge(gate_in, 1)
            S.activation(prob[:, :], prob[:, :], ACT.Exp)
            S.activation(col(SCORE), logit[:, EXPERTS:EXPERTS + 1], ACT.Exp, scale=-1.0).then_inc(gate_exp, 1)
            S.preload_act_table(ACT.Gelu_apprx_tanh)
            act.wait_ge(rank_done, 1)
            act.wait_ge(place_ready, 1)
            S.copy(place_T[:, :], ps[:, 7, 128:256]).then_inc(hot_T_ready, 1)

            def round_(r):
                first = is_first(r)

                def split_highs(pos, grains):
                    for j in grains:
                        act.wait_ge(used, used_in(r, pos - 1) + j + 1)
                        split_high(r, pos, j)

                def take_upper(q):
                    act.wait_ge(used, used_in(r, UNITS.index(("up", q)) + 1))
                    b = 2 * (q % 2)
                    S.copy(blocks(upper[:, q % 2, :]), ps[:, b:b + 2, 0:HB]).then_inc(upper_ready, 1)

                def gelu(q):
                    act.wait_ge(biased_ready, QU * r + q + 1)
                    S.activation(active[:, :, :], biased[:, :, :], ACT.Gelu_apprx_tanh).then_inc(gelu_done, 1)

                for pos, (kind, q) in enumerate(UNITS):
                    if first and pos == 0:
                        continue
                    split_highs(pos, range(1))
                    if pos >= 2 and UNITS[pos - 2][0] == "up":
                        gelu(UNITS[pos - 2][1])
                    split_highs(pos, range(1, 3))
                    if pos == 0:
                        take_y(r)
                    elif UNITS[pos - 1][0] == "up":
                        take_upper(UNITS[pos - 1][1])
                    split_highs(pos, range(3, GRAINS))
                    if first and pos == 1:
                        act.wait_ge(b2_ready, 1)
                        S.copy(blocks(ffn[:, :]), ps[:, 6:8, 0:HB]).then_inc(ffn_added, 1)
                    if pos == 2:
                        act.wait_ge(place_turned, r + 1)
                        S.copy(place_T[:, :], ps[:, 5, HB:512]).then_inc(place_T_ready, 1)

            def take_y(n):
                act.wait_ge(used, used_in(n, 0))
                S.copy(blocks(y_sb[:, :]), ps[:, 6:8, 0:HB]).then_inc(y_ready, 1)

            round_(0)
            act.wait_ge(route_ready, 1)
            rounds = act.value_load(route[0:1, 0:1], min_val=ROUNDS, max_val=ROUNDS + 1)
            with act.Fori(1, rounds) as r:
                round_(r)
            act.wait_ge(spread, HEADS + 4)
            act.wait_ge(minus_ready, 1)
            S.activation(wo_rows[:, 0, :], wo_rows[:, 0, :], ACT.Identity, scale=bk_c[:, :])
            S.activation(wo_rows[:, 1, :], wo_rows[:, 1, :], ACT.Identity, scale=minus_bk[:, :])
            S.activation(wv_rows[:, 1, :], wv_rows[:, 1, :], ACT.Identity, scale=bk_c[:, :]).then_inc(rows_scaled, 1)
            act.wait_ge(last_dot, 1)
            take_y(rounds)
            act.wait_ge(scattered, rounds)
            S.activation(blocks(y_sb[:, :]), ps[:, 4:6, 0:HB], ACT.Identity, scale=col(TOPP)).then_inc(ffn_scaled, 1)
            act.wait_ge(ffn_added, rounds)
            S.activation(ffn[:, :], ffn[:, :], ACT.Identity, scale=col(TOPP)).then_inc(ffn_scaled, 1)

        @block.vector
        def _(dve):
            steps = [0]

            def step(ins):
                steps[0] += 1
                ins.then_inc(dve_step, 1)
                dve.wait_ge(dve_step, steps[0])

            dve.wait_ge(iota_done, 2)
            V.tensor_copy(free_f[:, :], free_i[:, :])
            V.memset(ones[:, :], 1.0)
            V.memset(rank[:, EXPERTS + 1:EXPERTS + 2], 0.0)
            V.memset(hot_wide[:, EXPERTS:P], 0.0)
            step(V.tensor_copy(part_f[:, :], part_i[:, :]))
            V.tensor_scalar(later[:, :], free_f[:, :], part_f[:, :], None, ALU.is_gt)
            V.tensor_scalar(ident_b[:, :], free_f[:, :], part_f[:, :], None, ALU.is_equal)
            V.tensor_scalar(e8[:, :], free_f[:, 0:EXPERTS], -float(EXPERTS), None, ALU.add)
            for copy in range(2):
                V.tensor_scalar(slot_no[:, copy, :], free_f[:, 0:CAP], 1.0, None, ALU.add)
            step(V.tensor_scalar(ident[:, :], free_f[:, :], part_f[:, :], None, ALU.is_equal))
            V.tensor_tensor(fold[:, :], ident[:, 0:CAP], ident[:, CAP:2 * CAP], ALU.add).then_inc(consts, 1)

            def normalise(source, i):
                step(V.tensor_scalar(col(MEAN), col(SUM), 1.0 / D, None, ALU.mult))
                V.tensor_scalar(xc[:, :], source[:, :], col(MEAN), None, ALU.subtract).then_inc(xc_ready, 1)
                dve.wait_ge(xc_ready, i)
                step(V.tensor_tensor_reduce(out=xn[:, :], in0=xc[:, :], in1=xc[:, :], scale=1.0, scalar=0.0,
                                            op0=ALU.mult, op1=ALU.add, accum_out=col(SS)))
                V.tensor_scalar(col(VAR), col(SS), 1.0 / D, EPS, ALU.mult, ALU.add).then_inc(var_ready, 1)

            def take_xT(i):
                dve.wait_ge(xT_done, 2 * i - 1)
                V.tensor_copy(xT[:, 0:3, :].rearrange("p k t -> p (k t)"), ps[:, 5, 0:HB]).then_inc(xT_first, 1)
                if i == 1:
                    dve.wait_ge(xT_done, 2)
                    V.tensor_copy(xT[:, 3:KT, :].rearrange("p k t -> p (k t)"), ps[:, 6, 0:HB]).then_inc(xT_first, 1)

            dve.wait_ge(x_in, 16)
            step(V.reduce_sum(col(SUM), x_sb[:, :], AX))
            normalise(x_sb, 1)
            take_xT(1)

            dve.wait_ge(edges_in, 32)
            step(V.tensor_copy(edges_f[:, :, :], edges_i[:, :, :]))

            def hot_edges(c):
                if c:
                    dve.wait_ge(hot_used, c)
                for j, target in ((0, src_hot), (1, dst_hot)):
                    last = V.tensor_tensor(target[:, :, :], free_f[:, :].unsqueeze(1).to_broadcast([P, 8, P]),
                                           edges_f[:, j, 8 * c:8 * c + 8].unsqueeze(2).to_broadcast([P, 8, P]),
                                           ALU.is_equal)
                last.then_inc(hot_ready, 1)

            def take_counts():
                dve.wait_ge(hot_used, 4)
                V.tensor_copy(counts[:, :], ps[:, 7, 0:P])
                step(V.tensor_scalar(mask_bias[:, :], ps[:, 7, 0:P], 0.0, NEG, ALU.is_equal, ALU.mult))

            def head_alpha(h):
                dve.wait_ge(h_ready, h + 1)
                dve.wait_ge(spread, h + 1)
                for j in range(2):
                    dot = V.tensor_tensor_reduce(out=xc[:, :], in0=h_sb[:, h, :], in1=att_rows[:, h % 2, j, :],
                                                 scale=1.0, scalar=0.0, op0=ALU.mult, op1=ALU.add,
                                                 accum_out=alpha[:, j, h:h + 1])
                    if j == 0:
                        step(dot)
                dot.then_inc(alpha_used, 1)
                dve.wait_ge(alpha_used, h + 1)

            def attention(a, n, dst_alpha, turned_at):
                R = ps[:, 4, 0:n * P].rearrange("p (h s) -> p h s", h=n)
                shape = [P, n, P]
                e, p = att_e[:, 0:n, :], att_p[:, 0:n, :]
                dve.wait_ge(att_scores, a + 1)
                step(V.tensor_tensor(p, R, dst_alpha.unsqueeze(2).to_broadcast(shape), ALU.add))
                step(V.scalar_tensor_tensor(out=e, in0=p, scalar=0.2, in1=p, op0=ALU.mult, op1=ALU.max))
                step(V.tensor_tensor(e, e, mask_bias[:, :].unsqueeze(1).to_broadcast(shape), ALU.add))
                step(V.reduce_max(col(MX, n), e, AX))
                V.tensor_tensor(e, e, col(MX, n).unsqueeze(2).to_broadcast(shape), ALU.subtract).then_inc(att_shift, 1)
                dve.wait_ge(att_exp, a + 1)
                step(V.tensor_tensor(p, p, counts[:, :].unsqueeze(1).to_broadcast(shape), ALU.mult))
                step(V.reduce_sum(col(SS, n), p, AX))
                step(V.reciprocal(col(RS, n), col(SS, n)))
                V.tensor_tensor(p, p, col(RS, n).unsqueeze(2).to_broadcast(shape), ALU.mult).then_inc(att_prob, 1)
                dve.wait_ge(att_turned, a + 1)
                V.tensor_copy(att_T[:, 0:n, :].rearrange("p h s -> p (h s)"), turned_at).then_inc(att_ready, 1)

            def split_low(r, pos, j):
                i, b = 2 * pos + j // 2, j % 2
                dve.wait_ge(hi_ready, GRAINS * (2 * QU * r + pos) + j + 1)
                V.tensor_tensor(wlo[:, j, :, :], half_unit(i, is_first(r))[:, :, b * HB:(b + 1) * HB],
                                whi[:, j, :, :].bitcast(f32), ALU.subtract).then_inc(lo_ready, 1)

            def elu(k):
                shape = [P, 3, P]
                y, e = elu_y[:, k % 2, :, :], elu_e[:, k % 2, :, :]
                dve.wait_ge(agg_done, k + 1)
                if k >= 2:
                    dve.wait_ge(elu_ready, k - 1)
                step(V.tensor_tensor(y, ps[:, 5 + k % 2, 0:HB].rearrange("p (j t) -> p j t", j=3),
                                     gb1_T[:, 3 * k:3 * k + 3].unsqueeze(2).to_broadcast(shape), ALU.add))
                V.tensor_scalar(e, y, 0.0, None, ALU.min).then_inc(elu_in, 1)
                step(V.tensor_scalar(y, y, 0.0, None, ALU.max))
                if k % 8:
                    elu_out(k - 1)

            def elu_out(k):
                dve.wait_ge(elu_exp, k + 1)
                V.scalar_tensor_tensor(out=eluT[:, 3 * k:3 * k + 3, :], in0=elu_e[:, k % 2, :, :], scalar=-1.0,
                                       in1=elu_y[:, k % 2, :, :], op0=ALU.add, op1=ALU.add).then_inc(elu_ready, 1)

            hot_edges(0)
            V.tensor_scalar(shifted_i[:, 0:1], part_i[:, :], 3, None, ALU.logical_shift_right)
            V.tensor_scalar(shifted_i[:, 1:2], part_i[:, :], CL - 1, None, ALU.bitwise_and)
            V.tensor_scalar(shifted_i[:, 2:3], part_i[:, :], CH - 1, None, ALU.bitwise_and)
            V.tensor_scalar(wide_i[:, 0, :], free_i[:, :], 3, None, ALU.logical_shift_right)
            V.tensor_scalar(wide_i[:, 1, :], free_i[:, :], 5, None, ALU.logical_shift_right)
            V.memset(to_forward[:, :], 0.0)
            step(V.memset(to_back[:, :], 0.0))
            V.tensor_copy(wide[:, :, :], wide_i[:, :, :])
            step(V.tensor_copy(shifted[:, 0:3], shifted_i[:, 0:3]))
            step(V.tensor_scalar(shifted[:, 3:4], shifted[:, 0:1], -1.0, float(CH - 1), ALU.mult, ALU.add))
            V.tensor_scalar(to_forward[:, 0:CH], free_f[:, 0:CH], shifted[:, 0:1], None, ALU.is_equal)
            V.tensor_scalar(to_back[:, BACK:CP], free_f[:, 0:CH], shifted[:, 3:4], None, ALU.is_equal)
            V.tensor_scalar(step_mask[:, :], free_f[:, 0:CL], shifted[:, 1:2], None, ALU.is_equal)
            V.tensor_scalar(own_chunk[:, :], free_f[0:CP, 0:CH], shifted[0:CP, 2:3], CHUNK_SCALE,
                            ALU.is_equal, ALU.mult)
            V.tensor_scalar(direction[:, 0:1], part_f[0:CP, :], float(CH), None, ALU.is_lt)
            V.tensor_scalar(direction[:, 1:2], part_f[0:CP, :], float(BACK), None, ALU.is_ge)
            V.tensor_scalar(to_chunks[:, :], wide[0:2, 1, 0:CP], part_f[0:2, :], None, ALU.is_equal)
            V.tensor_scalar(turn_back[:, :], free_f[0:CP, 0:CH], part_f[0:CP, :], None, ALU.add)
            step(V.tensor_scalar(to_nodes[:, :], wide[0:CH, 0, :], part_f[0:CH, :], None, ALU.is_equal))
            V.tensor_scalar(turn_back[:, :], turn_back[:, :], float(CP - 1), None, ALU.is_equal)

            hot_edges(1)
            for h in range(2):
                head_alpha(h)
                hot_edges(h + 2)
            head_alpha(2)
            head_alpha(3)
            take_counts()
            attention(0, GROUP, alpha[:, 1, 0:GROUP], ps[:, 4, 0:512])
            head_alpha(4)
            head_alpha(5)
            head_alpha(6)
            dve.wait_ge(bias_ready, 1)
            for k in range(4):
                elu(k)
            head_alpha(7)
            for k in range(4, 8):
                elu(k)
            elu_out(7)
            dve.wait_ge(spread, HEADS + 2)
            V.tensor_tensor(x1[:, :], x_sb[:, :], gb2_rows[:, 0, :], ALU.add)
            attention(1, GROUP, alpha[:, 1, GROUP:2 * GROUP], ps[:, 4, 0:512])
            for k in range(8, 16):
                elu(k)
            elu_out(15)

            for j in VECTOR_GRAINS:
                split_low(0, 0, j)

            dve.wait_ge(h2_ready, 1)
            dve.wait_ge(spread, HEADS + 1)
            for j in range(2):
                dot = V.tensor_tensor_reduce(out=xc[:, :], in0=h2_sb[:, :],
                                             in1=att2_rows[:, j, :], scale=1.0, scalar=0.0,
                                             op0=ALU.mult, op1=ALU.add, accum_out=alpha2[:, j, :])
                if j == 0:
                    dot.then_inc(alpha_used, 1)
                    dve.wait_ge(alpha_used, HEADS + 1)
            dot.then_inc(alpha_used, 1)
            dve.wait_ge(alpha_used, HEADS + 2)
            e, p = att_e[:, 0, :], att_p[:, 0, :]
            dve.wait_ge(att_scores, 3)
            step(V.tensor_scalar(p, ps[:, 4, 0:P], alpha2[:, 1, :], None, ALU.add))
            step(V.scalar_tensor_tensor(out=e, in0=p, scalar=0.2, in1=p, op0=ALU.mult, op1=ALU.max))
            step(V.tensor_tensor(e, e, mask_bias[:, :], ALU.add))
            step(V.reduce_max(col(MX), e, AX))
            V.tensor_scalar(col(MX), col(MX), -1.0, None, ALU.mult).then_inc(att_shift, 1)
            dve.wait_ge(att_exp, 3)
            V.tensor_tensor_reduce(out=p, in0=p, in1=counts[:, :], scale=1.0, scalar=0.0, op0=ALU.mult,
                                   op1=ALU.add, accum_out=col(SS)).then_inc(att_prob, 1)
            dve.wait_ge(att_prob, 3)
            V.reciprocal(col(RS), col(SS))
            dve.wait_ge(att_turned, 3)
            V.tensor_copy(att_T[:, 0, :], ps[:, 4, P:2 * P]).then_inc(att_ready, 1)
            dve.wait_ge(out2_done, 1)
            dve.wait_ge(att_ready, 3)
            step(V.scalar_tensor_tensor(out=blocks(x1[:, :]), in0=ps[:, 2:4, 0:HB], scalar=col(RS),
                                        in1=blocks(x1[:, :]), op0=ALU.mult, op1=ALU.add, accum_out=col(SUM)))
            normalise(x1, 2)
            take_xT(2)
            dve.wait_ge(rstd_ready, 2)
            V.tensor_scalar(xn[:, :], xc[:, :], col(RSTD), None, ALU.mult).then_inc(xn_ready, 1)

            dve.wait_ge(logit_done, 1)
            step(V.scalar_tensor_tensor(out=logit[:, :], in0=ps[:, 7, 0:EXPERTS + 1], scalar=col(RSTD),
                                        in1=gate_b[:, :], op0=ALU.mult, op1=ALU.add))
            step(V.reduce_max(col(SMAX), logit[:, 0:EXPERTS], AX))
            step(V.scalar_tensor_tensor(out=best8[:, :], in0=logit[:, 0:EXPERTS], scalar=col(SMAX), in1=e8[:, :],
                                        op0=ALU.is_equal, op1=ALU.mult))
            step(V.tensor_reduce(col(IDX), best8[:, :], AX, ALU.min))
            V.tensor_scalar(hot, e8[:, :], col(IDX), None, ALU.is_equal).then_inc(onehot_ready, 1)
            V.tensor_scalar(prob[:, :], logit[:, 0:EXPERTS], col(SMAX), None, ALU.subtract).then_inc(gate_in, 1)

            dve.wait_ge(rank_done, 1)
            step(V.scalar_tensor_tensor(out=rank[:, 0:EXPERTS], in0=ps[:, 7, 16:24], scalar=1.0, in1=hot,
                                        op0=ALU.add, op1=ALU.mult))
            V.tensor_scalar(over[:, :], ps[:, 7, 24:32], float(CAP), None, ALU.is_gt)
            V.tensor_scalar(place_now[:, :], slot_no[:, :, :].rearrange("p a j -> p (a j)"), rank[:, 0:1],
                            None, ALU.is_equal).then_inc(place_ready, 1)
            dve.wait_ge(place_ready, 1)
            V.reduce_sum(route_f[:, 0:1], over[:, :], AX)
            step(V.tensor_tensor_reduce(out=best8[:, :], in0=over[:, :], in1=free_f[:, 0:EXPERTS], scale=1.0,
                                        scalar=0.0, op0=ALU.mult, op1=ALU.add, accum_out=route_f[:, 1:2]))
            step(V.tensor_scalar(route_f[:, 0:1], route_f[:, 0:1], float(ROUNDS), None, ALU.add))
            V.tensor_copy(route[:, :], route_f[:, :]).then_inc(route_ready, 1)
            dve.wait_ge(gate_exp, 1)
            V.reduce_sum(col(SS), prob[:, :], AX)
            step(V.tensor_scalar(col(SCORE), col(SCORE), 1.0, None, ALU.add))
            V.reciprocal(col(SCORE), col(SCORE)).then_inc(score_ready, 1)
            V.reciprocal(col(TOPP), col(SS))

            def take_gathered(r_done, bank):
                dve.wait_ge(gather_done, r_done)
                view = ps[:, bank, 0:HB].rearrange("p (k j) -> p k j", k=KT)
                V.tensor_copy(gathered[:, :, 0:CAP], view).then_inc(gathered_ready, 1)
                dve.wait_ge(gathered_ready, 2 * r_done - 1)
                V.tensor_tensor(gathered[:, :, CAP:P], view, gathered[:, :, 0:CAP].bitcast(f32),
                                ALU.subtract).then_inc(gathered_ready, 1)

            take_gathered(1, 5)

            dve.wait_ge(score_turned, 1)
            step(V.tensor_copy(score_row[:, 0, :], ps[0:1, 4, 0:P]))
            step(V.max(top16[:, 0:8], score_row[:, 0, :]))
            step(V.match_replace(out=score_row[:, 1, :], in_to_replace=top16[:, 0:8],
                                 in_values=score_row[:, 0, :], imm_value=-1.0))
            V.max(top16[:, 8:16], score_row[:, 1, :]).then_inc(thr_ready, 1)

            dve.wait_ge(small_in, 16 * SMALL)
            V.tensor_scalar(minus_bk[:, :], bk_c[:, :], -1.0, None, ALU.mult).then_inc(minus_ready, 1)
            step(V.tensor_tensor_reduce(out=best8[:, :], in0=over[:, :], in1=rank[:, 0:EXPERTS], scale=1.0,
                                        scalar=0.0, op0=ALU.mult, op1=ALU.add, accum_out=rank[:, 8:9]))
            step(V.tensor_scalar(rank[:, 8:9], rank[:, 8:9], -float(CAP), None, ALU.add))
            step(V.tensor_tensor(b1_over[:, :, :], b1_T[:, 0:EXPERTS, :],
                                 over[:, :].unsqueeze(2).to_broadcast([P, EXPERTS, QU * KT]), ALU.mult))
            step(V.reduce_sum(b1_T[:, EXPERTS, :], b1_over[:, :, :].rearrange("p e j -> p j e"), AX))

            def take_threshold():
                dve.wait_ge(thr_done, 1)
                step(V.tensor_scalar(keep[:, :], col(SCORE), ps[:, 5, HB:HB + 1], None, ALU.is_ge))
                V.tensor_scalar(own_step[:, :], step_mask[:, :], keep[:, :], None, ALU.mult)

            def add_ffn(n):
                dve.wait_ge(scattered, n)
                dve.wait_ge(ffn_added, n)
                V.tensor_tensor(blocks(ffn[:, :]), ps[:, 4:6, 0:HB], blocks(ffn[:, :]),
                                ALU.add).then_inc(ffn_added, 1)

            def round_(r):
                first = is_first(r)

                def add_bias(q):
                    dve.wait_ge(turned, QU * r + q + 1)
                    V.tensor_tensor(biased[:, :, :], ps[:, 4, 0:HB].rearrange("p (k j) -> p k j", k=KT),
                                    b1_T[:, bass.ds(r, 1), q * KT:(q + 1) * KT].rearrange("p o k -> p (o k)")
                                    .unsqueeze(2).to_broadcast([P, KT, CAP]),
                                    ALU.add).then_inc(biased_ready, 1)

                def split_hidden(q):
                    dve.wait_ge(gelu_done, QU * r + q + 1)
                    V.tensor_copy(hidden[:, q % 2, :, 0:CAP], active[:, :, :]).then_inc(hidden_ready, 1)
                    dve.wait_ge(hidden_ready, 2 * (QU * r + q) + 1)
                    V.tensor_tensor(hidden[:, q % 2, :, CAP:P], active[:, :, :],
                                    hidden[:, q % 2, :, 0:CAP].bitcast(f32), ALU.subtract).then_inc(hidden_ready, 1)

                g0, g1, g3 = VECTOR_GRAINS
                for pos in range(2 * QU):
                    if first and pos == 0:
                        continue
                    split_low(r, pos, g0)
                    if pos >= 2 and UNITS[pos - 2][0] == "up":
                        split_hidden(UNITS[pos - 2][1])
                    split_low(r, pos, g1)
                    split_low(r, pos, g3)
                    if pos == 0:
                        add_ffn(r)
                    if pos >= 1 and UNITS[pos - 1][0] == "up":
                        add_bias(UNITS[pos - 1][1])
                    if pos == 3:
                        dve.wait_ge(place_turned, r + 1)
                        V.tensor_scalar(place_now[:, :], slot_no[:, :, :].rearrange("p a j -> p (a j)"),
                                        rank[:, bass.ds(r + 1, 1)], None, ALU.is_equal).then_inc(place_ready, 1)
                    if pos == 2 * QU - 1:
                        take_gathered(r + 2, 5)
                    if first and pos == 2 * QU - 1:
                        take_threshold()

            round_(0)
            dve.wait_ge(route_ready, 1)
            rounds = dve.value_load(route[0:1, 0:1], min_val=ROUNDS, max_val=ROUNDS + 1)
            with dve.Fori(1, rounds) as r:
                round_(r)

            dve.wait_ge(spread, HEADS + 4)
            dve.wait_ge(ffn_added, rounds)
            step(V.tensor_tensor_reduce(out=xc[:, :], in0=ffn[:, :], in1=wv_rows[:, 0, :], scale=1.0, scalar=0.0,
                                        op0=ALU.mult, op1=ALU.add, accum_out=col(VSUM)))
            dve.wait_ge(used, used_in(rounds, 0))
            V.tensor_tensor_reduce(out=blocks(xc[:, :]), in0=ps[:, 6:8, 0:HB], in1=blocks(wv_rows[:, 0, :]), scale=1.0,
                                   scalar=0.0, op0=ALU.mult, op1=ALU.add, accum_out=col(VSLOT)).then_inc(last_dot, 1)
            dve.wait_ge(last_placed, 1)
            step(V.scalar_tensor_tensor(out=col(VCOL), in0=ps[:, 3, 0:1], scalar=col(VSUM), in1=col(TOPP), op0=ALU.add,
                                        op1=ALU.mult))
            step(V.tensor_scalar(col(VCOL), col(VCOL), bv_c[:, :], VMAX, ALU.add, ALU.min))
            V.scalar_tensor_tensor(out=v_steps[:, :], in0=col(VCOL).to_broadcast([P, CL]), scalar=-VMAX,
                                   in1=step_mask[:, :], op0=ALU.max, op1=ALU.mult).then_inc(v_ready, 1)

            dve.wait_ge(cf_init, 3)
            dve.wait_ge(v_turned, 1)
            step(V.tensor_copy(cf_v[:, :], ps[0:CP, 2, 0:CL]))
            V.tensor_copy(cf_d[:, :, 0], cf_v[0:CH, :])
            for i in range(CL):
                n = 4 * (CL + 1 - i)
                step(V.tensor_tensor(cf_t[:, 0:n], cf_w[:, i + 1, 4:4 + n], cf_w[:, i, 0:n], ALU.subtract))
                step(V.scalar_tensor_tensor(out=cf_w[:, i + 2, 0:n], in0=cf_w[:, i + 1, 0:n],
                                            scalar=cf_v[:, i:i + 1], in1=cf_t[:, 0:n], op0=ALU.mult, op1=ALU.add))
            V.tensor_tensor(cf_m[:, :, :].rearrange("p c (a b) -> p c a b", a=2),
                            cf_w[:, CL:CL + 2, 0:8].unsqueeze(1).to_broadcast([CP, CH, 2, 8]),
                            own_chunk[:, :].unsqueeze(2).unsqueeze(3).to_broadcast([CP, CH, 2, 8]),
                            ALU.mult).then_inc(cf_ready, 1)
            dve.wait_ge(cf_moved, 1)
            step(V.tensor_copy(cf_mm[:, :, :], ps[0:2, 7, 0:16 * CH].rearrange("p (c m) -> p c m", c=CH)))
            for c in range(CH - 1):
                step(V.tensor_tensor(cf_x[:, :, :], cf_mm[:, c, :].rearrange("p (a b) -> p a b", a=4),
                                     cf_s[:, c, :].unsqueeze(1).to_broadcast([2, 4, 4]), ALU.mult))
                step(V.reduce_sum(cf_s[:, c + 1, :], cf_x[:, :, :], AX))
            step(V.tensor_reduce(cf_n[:, :], cf_s[:, :, :], AX, ALU.max, apply_absolute_value=True))
            step(V.reciprocal(cf_n[:, :], cf_n[:, :]))
            V.tensor_tensor(cf_s[:, :, :], cf_s[:, :, :], cf_n[:, :].unsqueeze(2).to_broadcast([2, CH, 4]),
                            ALU.mult).then_inc(cf_ready, 1)
            dve.wait_ge(cf_moved, 2)
            step(V.tensor_tensor(cf_p[:, :, :], ps[0:CP, 7, 0:4 * CH].rearrange("p (c m) -> p c m", c=CH),
                                 own_chunk[:, :].unsqueeze(2).to_broadcast([CP, CH, 4]), ALU.mult))
            step(V.reduce_sum(cf_b[:, :], cf_p[:, :, :].rearrange("p c m -> p m c"), AX))
            step(V.tensor_tensor(cf_y[:, :, :, :], cf_w[:, 1:CL + 2, 0:8].rearrange("p s (a b) -> p s a b", a=2),
                                 cf_b[:, :].unsqueeze(1).unsqueeze(1).to_broadcast([CP, CL + 1, 2, 4]), ALU.mult))
            step(V.reduce_sum(cf_th[:, :, :], cf_y[:, :, :, :], AX))
            tx, ty = cf_th[:, 1:CL + 1, :], cf_th[:, 0:CL, :]
            V.tensor_tensor(cf_q[:, 0, :, :], ty, ty, ALU.mult)
            V.tensor_tensor(cf_q[:, 1, :, :], tx, ty, ALU.mult)
            step(V.tensor_tensor(cf_q[:, 2, :, :], tx[:, :, ::-1], ty, ALU.mult))
            V.reduce_sum(cf_r[:, :], cf_q[:, 0, :, :], AX)
            V.reduce_sum(cf_a[:, :, 0], cf_q[:, 1, :, :], AX)
            step(V.tensor_tensor(cf_a[:, :, 1], cf_q[:, 2, :, 0], cf_q[:, 2, :, 1], ALU.subtract))
            step(V.reciprocal(cf_r[:, :], cf_r[:, :]))
            V.tensor_tensor(cf_a[:, :, :], cf_a[:, :, :], cf_r[:, :].unsqueeze(2).to_broadcast([CP, CL, 2]),
                            ALU.mult).then_inc(cf_ready, 1)
            dve.wait_ge(cf_moved, 3)
            step(V.tensor_tensor(cf_c[:, :, :], ps[0:CH, 7, 0:2 * CL].rearrange("p (j c) -> p j c", j=CL),
                                 cf_d[:, :, :], ALU.subtract))
            step(V.tensor_tensor(cf_g[:, :, :], cf_c[:, :, :], cf_c[:, :, :], ALU.mult))
            step(V.reduce_sum(cf_e[:, :], cf_g[:, :, :], AX))
            step(V.reciprocal(cf_e[:, :], cf_e[:, :]))
            V.tensor_tensor(cf_g[:, :, :], cf_c[:, :, :], cf_e[:, :].unsqueeze(2).to_broadcast([CH, CL, 2]),
                            ALU.mult).then_inc(cf_ready, 1)
            dve.wait_ge(cf_moved, 4)
            step(V.tensor_tensor(cf_f[:, :, :], ps[:, 7, 0:2 * CL].rearrange("p (j c) -> p j c", j=CL),
                                 own_step[:, :].unsqueeze(2).to_broadcast([P, CL, 2]), ALU.mult))
            step(V.reduce_sum(feats[:, :], cf_f[:, :, :].rearrange("p j c -> p c j"), AX))
            step(V.tensor_scalar(feats[:, :], feats[:, :], FCLAMP, -FCLAMP, ALU.min, ALU.max))
            dve.wait_ge(x1_done, 3)
            step(V.scalar_tensor_tensor(out=x1[:, :], in0=wo_rows[:, 0, :], scalar=feats[:, 0:1], in1=x1[:, :],
                                        op0=ALU.mult, op1=ALU.add))
            V.scalar_tensor_tensor(out=xc[:, :], in0=wo_rows[:, 1, :], scalar=feats[:, 1:2], in1=x1[:, :],
                                   op0=ALU.mult, op1=ALU.add).then_inc(final_ready, 1)

        @block.tensor
        def _(pe):
            def turn_x(i):
                pe.wait_ge(xc_ready, i)
                for half in range(2):
                    for k in range(3):
                        c = (3 * half + k) * P
                        last = T.transpose(ps[:, 5 + half, k * P:(k + 1) * P], xc[:, c:c + P], ident[:, :])
                    last.then_inc(xT_done, 1)

            def stay_warm(n, bank=7):
                for _ in range(n):
                    T.matmul(ps[:, bank, 0:P], ident[:, :], ident[:, :], start=True, stop=True)

            pe.wait_ge(consts, 1)
            stay_warm(WARM[0])
            turn_x(1)
            stay_warm(WARM[1])
            def raw_ready(n):
                pe.wait_ge(raw_in[n % SLOTS], 16 * (n // SLOTS + 1))

            def head_up(h, halves=(0, 1)):
                if h >= 2 and 0 in halves:
                    pe.wait_ge(h_ready, h - 1)
                for half in halves:
                    n = 2 * h + half
                    raw_ready(n)
                    if n == 1:
                        pe.wait_ge(xT_first, 2)
                    for k in range(3):
                        for b in range(2):
                            last = T.matmul(ps[:, 2 * (h % 2) + b, 0:HB], xT[:, 3 * half + k, :],
                                            raw[:, n % SLOTS, k, b * HB:(b + 1) * HB],
                                            start=(n % 2 == 0 and k == 0), stop=(n % 2 == 1 and k == 2))
                    last.then_inc(used, 2)

            def scores(a, n, source):
                if a:
                    pe.wait_ge(att_ready, a)
                for h in range(n):
                    last = T.matmul(ps[:, 4, h * P:(h + 1) * P], source(h).to_broadcast([P, P]), ident[:, :],
                                    start=True, stop=True)
                last.then_inc(att_scores, 1)

            def turn_weights(a, n, first):
                pe.wait_ge(att_prob, a + 1)
                for h in range(n):
                    last = T.transpose(ps[:, 4, first + h * P:first + (h + 1) * P], att_p[:, h, :], ident[:, :])
                last.then_inc(att_turned, 1)

            def aggregate(k):
                h = k // 2
                pe.wait_ge(att_ready, h // GROUP + 1)
                if k >= 2:
                    pe.wait_ge(elu_in, k - 1)
                for j in range(3):
                    c = (3 * (k % 2) + j) * P
                    last = T.matmul(ps[:, 5 + k % 2, j * P:(j + 1) * P], h_sb[:, h, c:c + P],
                                    att_T[:, h % GROUP, :], start=True, stop=True)
                last.then_inc(agg_done, 1)

            def head_down(h, halves=(0, 1)):
                for half in halves:
                    pe.wait_ge(elu_ready, 2 * h + half + 1)
                    n = 2 * (HEADS + h) + half
                    raw_ready(n)
                    for k in range(3):
                        for b in range(2):
                            last = T.matmul(ps[:, b, 0:HB], eluT[:, KT * h + 3 * half + k, :],
                                            raw[:, n % SLOTS, k, b * HB:(b + 1) * HB],
                                            start=(h == 0 and half == 0 and k == 0),
                                            stop=(h == HEADS - 1 and half == 1 and k == 2))
                    last.then_inc(used, 2)

            def turn_biases():
                pe.wait_ge(small_in, 16 * SMALL)
                T.transpose(ps[:, 4, 0:HEADS * KT], gb1_rows[:, :], ident[0:HEADS * KT, 0:HEADS * KT])
                for g in range(2):
                    last = T.transpose(ps[:, 4, 192 + 96 * g:288 + 96 * g], b1_rows[:, g, :], ident[0:96, 0:96])
                last.then_inc(bias_done, 1)

            def count_edges(c):
                pe.wait_ge(hot_ready, c + 1)
                for j in range(8):
                    last = T.matmul(ps[:, 7, 0:P], dst_hot[:, j, :], src_hot[:, j, :],
                                    start=(c == 0 and j == 0), stop=False)
                if c == 3:
                    last = T.matmul(ps[:, 7, 0:P], ident_b[:, :], ident_b[:, :], start=False, stop=True)
                last.then_inc(hot_used, 1)

            pe.wait_ge(xT_first, 1)
            for h in range(4):
                head_up(h)
                count_edges(h)
            head_up(4, [0])
            turn_biases()
            head_up(4, [1])
            head_up(5, [0])
            pe.wait_ge(bias_ready, 1)
            pe.wait_ge(alpha_used, GROUP)
            scores(0, GROUP, lambda h: alpha[:, 0, h:h + 1])
            head_up(5, [1])
            head_up(6, [0])
            turn_weights(0, GROUP, 0)
            head_up(6, [1])
            aggregate(0)
            aggregate(1)
            head_up(7, [0])
            aggregate(2)
            aggregate(3)
            head_up(7, [1])
            aggregate(4)
            aggregate(5)
            pe.wait_ge(h_ready, HEADS - 1)
            head_down(0, [0])
            aggregate(6)
            aggregate(7)
            head_down(0, [1])
            pe.wait_ge(alpha_used, HEADS)
            scores(1, GROUP, lambda h: alpha[:, 0, GROUP + h:GROUP + h + 1])
            head_down(1)
            head_down(2, [0])
            turn_weights(1, GROUP, 0)
            head_down(2, [1])
            aggregate(8)
            aggregate(9)
            head_down(3, [0])
            aggregate(10)
            aggregate(11)
            head_down(3, [1])
            aggregate(12)
            aggregate(13)
            head_down(4, [0])
            aggregate(14)
            aggregate(15)
            head_down(4, [1])
            for h in range(5, HEADS):
                head_down(h)

            stay_warm(WARM[2])
            pe.wait_ge(alpha_used, HEADS + 1)
            scores(2, 1, lambda h: alpha2[:, 0, :])
            stay_warm(WARM[3])
            turn_weights(2, 1, P)
            stay_warm(WARM[4])
            pe.wait_ge(att_ready, 3)
            pe.wait_ge(h2_ready, 1)
            for b in range(2):
                last = T.matmul(ps[:, 2 + b, 0:HB], att_T[:, 0, :], h2_sb[:, b * HB:(b + 1) * HB],
                                start=True, stop=True)
            last.then_inc(out2_done, 1)
            stay_warm(WARM[5], 0)
            turn_x(2)
            stay_warm(WARM[6], 0)
            pe.wait_ge(xT_first, 3)
            for k in range(KT):
                if k == 3:
                    pe.wait_ge(xT_second, 1)
                last = T.matmul(ps[:, 7, 0:EXPERTS + 1], xT[:, k, :], gate_w[:, k, :], start=(k == 0),
                                stop=(k == KT - 1))
            last.then_inc(logit_done, 1)
            stay_warm(WARM[7], 0)

            pe.wait_ge(onehot_ready, 1)
            T.matmul(ps[:, 7, 16:24], later[:, :], hot, start=True, stop=True)
            T.matmul(ps[:, 7, 24:32], ones[:, :], hot, start=True, stop=True)
            T.transpose(ps[:, 7, 128:256], hot_wide[:, :], ident[:, :]).then_inc(rank_done, 1)
            stay_warm(WARM[8], 0)

            def gather(bank):
                for k in range(KT):
                    last = T.matmul(ps[:, bank, k * CAP:(k + 1) * CAP], xn[:, k * P:(k + 1) * P],
                                    place_now[:, 0:CAP], start=True, stop=True)
                last.then_inc(gather_done, 1)

            pe.wait_ge(xn_ready, 1)
            pe.wait_ge(place_ready, 1)
            gather(5)
            pe.wait_ge(score_ready, 1)
            T.matmul(ps[0:1, 4, 0:P], col(SCORE), ident[:, :], start=True, stop=True).then_inc(score_turned, 1)
            stay_warm(WARM[9], 0)

            def first_ffn():
                pe.wait_ge(hot_T_ready, 1)
                for b in range(2):
                    last = T.matmul(ps[:, 6 + b, 0:HB], place_T[0:EXPERTS, :], b2_sb[:, b * HB:(b + 1) * HB],
                                    start=True, stop=True)
                last.then_inc(b2_ready, 1)

            def round_(r):
                first = is_first(r)

                unit0 = 2 * QU * r

                def stream(pos, stationary, bank, first, last_, grains=range(GRAINS)):
                    for j in grains:
                        half, b = j // 2, j % 2
                        if j == POOL_GRAIN:
                            pe.wait_ge(lo_pool, unit0 + pos + 1)
                        else:
                            pe.wait_ge(lo_ready, 3 * (unit0 + pos) + VECTOR_GRAINS.index(j) + 1)
                        for k in range(3):
                            for part in (whi, wlo):
                                last = T.matmul(ps[:, bank + b, 0:HB], stationary[:, 3 * half + k, :],
                                                part[:, j, k, :],
                                                start=(first and half == 0 and k == 0 and part is whi),
                                                stop=(last_ and half == 1 and k == 2 and part is wlo))
                        last.then_inc(used, 1)

                def turn_upper(q):
                    pe.wait_ge(upper_ready, QU * r + q + 1)
                    for k in range(KT):
                        last = T.matmul(ps[:, 4, k * CAP:(k + 1) * CAP], upper[:, q % 2, k * P:(k + 1) * P],
                                        fold[:, :], start=True, stop=True)
                    last.then_inc(turned, 1)

                def up(q, grains):
                    stream(UNITS.index(("up", q)), gathered, 2 * (q % 2), True, True, grains)

                def down(q, grains):
                    if 0 in grains:
                        pe.wait_ge(hidden_ready, 2 * (QU * r + q + 1))
                    stream(UNITS.index(("down", q)), hidden[:, q % 2, :, :], 6, q == 0, q == QU - 1, grains)

                pe.wait_ge(gathered_ready, 2 * r + 2)
                if first:
                    up(0, range(GRAINS))
                    first_ffn()
                else:
                    up(0, range(2))
                    scatter(r)
                    up(0, range(2, GRAINS))
                up(1, range(1))
                if first:
                    pe.wait_ge(thr_ready, 1)
                else:
                    pe.wait_ge(ffn_added, r + 1)
                T.transpose(ps[:, 5, HB:512], place_now[:, :], ident[:, :]).then_inc(place_turned, 1)
                turn_upper(0)
                up(1, range(1, GRAINS))
                if first:
                    pe.wait_ge(ffn_added, 1)
                down(0, range(1))
                turn_upper(1)
                down(0, range(1, GRAINS))
                up(2, range(GRAINS))
                down(1, range(1))
                turn_upper(2)
                down(1, range(1, GRAINS))
                up(3, range(GRAINS))
                if first:
                    pe.wait_ge(place_T_ready, 1)
                    T.matmul(ps[:, 5, HB:HB + 1], ones[0:1, :], top16[0:1, KEEP - 1:KEEP], start=True,
                             stop=True).then_inc(thr_done, 1)
                pe.wait_ge(place_ready, r + 2)
                pe.wait_ge(place_T_ready, r + 1)
                gather(5)
                down(2, range(1))
                turn_upper(3)
                down(2, range(1, GRAINS))
                down(3, range(GRAINS))

            def scatter(n):
                pe.wait_ge(y_ready, n)
                for b in range(2):
                    last = T.matmul(ps[:, 4 + b, 0:HB], place_T[:, :], y_sb[:, b * HB:(b + 1) * HB],
                                    start=True, stop=True)
                last.then_inc(scattered, 1)

            round_(0)
            pe.wait_ge(route_ready, 1)
            rounds = pe.value_load(route[0:1, 0:1], min_val=ROUNDS, max_val=ROUNDS + 1)
            with pe.Fori(1, rounds) as r:
                round_(r)
            pe.wait_ge(last_dot, 1)
            T.matmul(ps[:, 3, 0:1], place_T[:, :], col(VSLOT), start=True, stop=True).then_inc(last_placed, 1)
            pe.wait_ge(v_ready, 1)
            T.matmul(ps[0:CP, 2, 0:CL], to_forward[:, :], v_steps[:, :], start=True, stop=False)
            T.matmul(ps[0:CP, 2, 0:CL], to_back[:, :], v_steps[:, ::-1], start=False, stop=True).then_inc(v_turned, 1)
            pe.wait_ge(gathered_ready, 2 * rounds + 2)
            scatter(rounds)
            pe.wait_ge(cf_ready, 1)
            T.matmul(ps[0:2, 7, 0:16 * CH], direction[:, :], cf_m[:, :, :].rearrange("p c m -> p (c m)"),
                     start=True, stop=True).then_inc(cf_moved, 1)
            pe.wait_ge(cf_ready, 2)
            T.matmul(ps[0:CP, 7, 0:4 * CH], to_chunks[:, :], cf_s[:, :, :].rearrange("p c m -> p (c m)"),
                     start=True, stop=True).then_inc(cf_moved, 1)
            pe.wait_ge(cf_ready, 3)
            T.matmul(ps[0:CH, 7, 0:2 * CL], ident[0:CP, 0:CH], cf_a[:, :, :].rearrange("p j c -> p (j c)"),
                     start=True, stop=False)
            T.matmul(ps[0:CH, 7, 0:2 * CL].rearrange("p (j c) -> p j c", j=CL), turn_back[:, :],
                     cf_a[:, ::-1, :], start=False, stop=True).then_inc(cf_moved, 1)
            pe.wait_ge(cf_ready, 4)
            T.matmul(ps[:, 7, 0:2 * CL], to_nodes[:, :], cf_g[:, :, :].rearrange("p j c -> p (j c)"),
                     start=True, stop=True).then_inc(cf_moved, 1)


_SHAPES = {
    "x": (N, D), "src": (EDGES,), "dst": (EDGES,), "L0_gnn_W1": (D, HEADS * D), "L0_gnn_a_src1": (HEADS, D),
    "L0_gnn_a_dst1": (HEADS, D), "L0_gnn_b1": (HEADS * D,), "L0_gnn_W2": (HEADS * D, D),
    "L0_gnn_a_src2": (1, D), "L0_gnn_a_dst2": (1, D), "L0_gnn_b2": (1, D), "L0_ffn_Wg": (D, EXPERTS),
    "L0_ffn_bg": (1, EXPERTS), "L0_ffn_W1": (EXPERTS, D, HID), "L0_ffn_b1": (EXPERTS, HID),
    "L0_ffn_W2": (EXPERTS, HID, D), "L0_ffn_b2": (EXPERTS, D), "L0_ffn_Wv": (1, D), "L0_ffn_bv": (1, 1),
    "L0_ffn_Wm": (D, 1), "L0_ffn_bm": (1, 1), "L0_ffn_Wo": (2, D), "L0_ffn_bo": (1, D),
    "L0_ffn_bk_scale": (1, 1),
}


def kernel(**inputs):
    import numpy as _np
    import concourse.bacc as _bacc
    from concourse import mybir as _mybir
    from concourse.bass_utils import run_bass_kernel_spmd as _run

    nc = _bacc.Bacc("TRN2", target_bir_lowering=False, num_devices=1)
    arrays, args = {}, []
    for name, shape in _SHAPES.items():
        a = _np.ascontiguousarray(inputs[name]).reshape(shape)
        arrays[f"in_{name}"] = a
        args.append(nc.dram_tensor(f"in_{name}", shape, _mybir.dt.from_np(a.dtype), kind="ExternalInput").ap())
    out = nc.dram_tensor("out", (N, D), _mybir.dt.float32, kind="ExternalOutput").ap()
    gnn_moe_kernel(nc, *args, out)
    r = _run(nc, [arrays], core_ids=[0])
    return r.results[0]["out"]
```
